# Optimizing a Trainium2 kernel written in Bass

```python
import numpy as np
import jax
import jax.numpy as jnp

def _softmax(x, axis=-1):
    return jax.nn.softmax(x, axis=axis)

def _gelu(x):
    return jax.nn.gelu(x, approximate=True)

def _silu(x):
    return jax.nn.silu(x)

def _sigmoid(x):
    return jax.nn.sigmoid(x)

def _layernorm(x, axis=-1, eps=1e-05):
    m = jnp.mean(x, axis=axis, keepdims=True)
    v = jnp.var(x, axis=axis, keepdims=True)
    return (x - m) / jnp.sqrt(v + eps)

def _scatter_add(tgt, idx, src, axis=0):
    return tgt.at[idx].add(src)

def _segment_sum(src, seg, n):
    return jax.ops.segment_sum(src, seg, n)
kernel_name = 'mk_gps_d2_gnn_r8_21a7ee'

def setup_inputs(seed: int=0):
    np.random.seed(seed)
    _w = jnp.asarray

    def _rec_inputs():
        import jax
        import jax.numpy as jnp
        _gk = jax.random.key(seed)
        x = -8.776e-05 + 1 * jax.random.normal(jax.random.fold_in(_gk, 1), (1250, 512), jnp.float32)
        src = jax.random.randint(jax.random.fold_in(_gk, 2), (20000,), 0, 1250, jnp.int32)
        dst = jnp.minimum((1250 * jax.random.uniform(jax.random.fold_in(_gk, 3), (20000,)) ** 2.0).astype(jnp.int32), 9999)
        _o = jnp.argsort(dst, stable=True)
        src = src[_o]
        dst = dst[_o]
        edge_attr_8 = jax.random.uniform(jax.random.fold_in(_gk, 11), (20000, 8), jnp.float32, 0.0, 0.999999)
        return (x, src, dst, edge_attr_8)
    x, src, dst, edge_attr_8 = _rec_inputs()

    def _L0_gnn_setup():
        import jax, jax.numpy as jnp
        import numpy as np
        N, E, D, H = (1250, 20000, 512, 8)
        HD = D // H
        SCALE = HD ** (-0.5)

        def _layernorm(x, g, b):
            mu = jnp.mean(x, axis=-1, keepdims=True)
            var = jnp.mean(jnp.square(x - mu), axis=-1, keepdims=True)
            return (x - mu) * jax.lax.rsqrt(var + 1e-05) * g + b
        key = jax.random.key(seed)
        ks = jax.random.split(key, 12)
        s = D ** (-0.5)
        return {'x': jax.random.normal(ks[0], (N, D), jnp.float32), 'edge_index': jax.random.randint(ks[1], (2, E), 0, N, jnp.int64), 'edge_weights': jax.random.uniform(ks[2], (E, H), jnp.float32), 'ln_g': jnp.ones((D,), jnp.float32), 'ln_b': jnp.zeros((D,), jnp.float32), 'Wq': jax.random.normal(ks[3], (D, D), jnp.float32) * s, 'bq': jnp.zeros((D,), jnp.float32), 'Wk': jax.random.normal(ks[4], (D, D), jnp.float32) * s, 'bk': jnp.zeros((D,), jnp.float32), 'Wv': jax.random.normal(ks[5], (D, D), jnp.float32) * s, 'bv': jnp.zeros((D,), jnp.float32), 'W1': jax.random.normal(ks[6], (D, D), jnp.float32) * s, 'b1': jnp.zeros((D,), jnp.float32), 'W2': jax.random.normal(ks[7], (D, D), jnp.float32) * s, 'b2': jnp.zeros((D,), jnp.float32)}
    _L0_gnn_all = _L0_gnn_setup()
    _L0_gnn_in = {k: v for k, v in _L0_gnn_all.items() if k in ('ln_g', 'ln_b', 'Wq', 'bq', 'Wk', 'bk', 'Wv', 'bv', 'W1', 'b1', 'W2', 'b2')}
    del _L0_gnn_all

    def _L0_mix_setup():
        import jax, jax.numpy as jnp
        import numpy as np
        HEADS = 8
        DIM_HEAD = 64
        key = jax.random.key(seed)
        k1, k2, k3 = jax.random.split(key, 3)
        B, L, D = (8, 512, 512)
        hidden = HEADS * DIM_HEAD
        x = jax.random.normal(k1, (B, L, D), dtype=jnp.float32)
        Wqkv = jax.random.normal(k2, (3 * hidden, D), dtype=jnp.float32) * (1.0 / np.sqrt(D))
        Wout = jax.random.normal(k3, (D, hidden), dtype=jnp.float32) * (1.0 / np.sqrt(hidden))
        bout = jnp.zeros((D,), dtype=jnp.float32)
        return {'x': x, 'Wqkv': Wqkv, 'Wout': Wout, 'bout': bout}
    _L0_mix_all = _L0_mix_setup()
    _L0_mix_in = {k: v for k, v in _L0_mix_all.items() if k in ('Wqkv', 'Wout', 'bout')}
    del _L0_mix_all

    def _L0_ffn_setup():
        import jax, jax.numpy as jnp
        import numpy as np
        NUM_EXPERTS = 8
        TOP_K = 2
        HIDDEN = 512
        INTERMEDIATE = 256
        BATCH, SEQ = (8, 256)
        key = jax.random.key(seed)
        ks = jax.random.split(key, 7)
        s_in = 1.0 / np.sqrt(HIDDEN)
        s_mid = 1.0 / np.sqrt(INTERMEDIATE)
        return {'x': jax.random.normal(ks[0], (BATCH, SEQ, HIDDEN), jnp.float32), 'Wg': jax.random.normal(ks[1], (HIDDEN, NUM_EXPERTS), jnp.float32) * s_in, 'bg': jnp.zeros((NUM_EXPERTS,), jnp.float32), 'W1': jax.random.normal(ks[2], (NUM_EXPERTS, HIDDEN, INTERMEDIATE), jnp.float32) * s_in, 'b1': jnp.zeros((NUM_EXPERTS, INTERMEDIATE), jnp.float32), 'W2': jax.random.normal(ks[3], (NUM_EXPERTS, INTERMEDIATE, HIDDEN), jnp.float32) * s_mid, 'b2': jnp.zeros((NUM_EXPERTS, HIDDEN), jnp.float32)}
    _L0_ffn_all = _L0_ffn_setup()
    _L0_ffn_in = {k: v for k, v in _L0_ffn_all.items() if k in ('Wg', 'bg', 'W1', 'b1', 'W2', 'b2')}
    del _L0_ffn_all

    def _L1_gnn_setup():
        import jax, jax.numpy as jnp
        import numpy as np
        N, E, D = (6250, 50000, 512)

        def _sage_conv(x, src, dst, Wl, bl, Wr, n_nodes):
            agg = jax.ops.segment_sum(x[src], dst, num_segments=n_nodes)
            deg = jax.ops.segment_sum(jnp.ones((src.shape[0],), x.dtype), dst, num_segments=n_nodes)
            agg = agg / jnp.maximum(deg, 1.0)[:, None]
            return agg @ Wl.T + bl + x @ Wr.T

        def _layer_norm(h, w, b, eps=1e-05):
            mu = jnp.mean(h, axis=-1, keepdims=True)
            var = jnp.mean(jnp.square(h - mu), axis=-1, keepdims=True)
            return (h - mu) * jax.lax.rsqrt(var + eps) * w + b
        key = jax.random.key(seed)
        ks = jax.random.split(key, 8)
        s = 1.0 / np.sqrt(D)
        x = jax.random.normal(ks[0], (N, D), dtype=jnp.float32)
        edge_index = jax.random.randint(ks[1], (2, E), 0, N, dtype=jnp.int64)
        return {'x': x, 'edge_index': edge_index, 'W1l': jax.random.uniform(ks[2], (D, D), jnp.float32, -s, s), 'b1l': jnp.zeros((D,), jnp.float32), 'W1r': jax.random.uniform(ks[3], (D, D), jnp.float32, -s, s), 'W2l': jax.random.uniform(ks[4], (D, D), jnp.float32, -s, s), 'b2l': jnp.zeros((D,), jnp.float32), 'W2r': jax.random.uniform(ks[5], (D, D), jnp.float32, -s, s), 'ln1_w': jnp.ones((D,), jnp.float32), 'ln1_b': jnp.zeros((D,), jnp.float32), 'ln2_w': jnp.ones((D,), jnp.float32), 'ln2_b': jnp.zeros((D,), jnp.float32)}
    _L1_gnn_all = _L1_gnn_setup()
    _L1_gnn_in = {k: v for k, v in _L1_gnn_all.items() if k in ('W1l', 'b1l', 'W1r', 'W2l', 'b2l', 'W2r', 'ln1_w', 'ln1_b', 'ln2_w', 'ln2_b')}
    del _L1_gnn_all

    def _L1_mix_setup():
        import jax, jax.numpy as jnp
        import numpy as np
        HEADS = 8
        DIM_HEAD = 64
        EPS = 0.0001

        def softmax_kernel(data, proj, is_query):
            data_normalizer = data.shape[-1] ** (-0.25)
            ratio = proj.shape[0] ** (-0.5)
            data_dash = jnp.einsum('bhnd,md->bhnm', data_normalizer * data, proj)
            diag = (data * data).sum(-1) * 0.5 * data_normalizer ** 2
            diag = diag[..., None]
            if is_query:
                stab = jnp.max(data_dash, axis=-1, keepdims=True)
            else:
                stab = jnp.max(data_dash)
            return ratio * (jnp.exp(data_dash - diag - stab) + EPS)

        def linear_attention(q, k, v):
            k_cumsum = k.sum(axis=-2)
            d_inv = 1.0 / jnp.einsum('bhnm,bhm->bhn', q, k_cumsum)
            context = jnp.einsum('bhnm,bhne->bhme', k, v)
            return jnp.einsum('bhme,bhnm,bhn->bhne', context, q, d_inv)
        key = jax.random.key(seed)
        ks = jax.random.split(key, 6)
        b, n, dim = (8, 512, 512)
        m, dh = (266, DIM_HEAD)
        x = jax.random.normal(ks[0], (b, n, dim), dtype=jnp.float32)
        s = dim ** (-0.5)
        Wq = jax.random.normal(ks[1], (dim, dim), dtype=jnp.float32) * s
        Wk = jax.random.normal(ks[2], (dim, dim), dtype=jnp.float32) * s
        Wv = jax.random.normal(ks[3], (dim, dim), dtype=jnp.float32) * s
        Wo = jax.random.normal(ks[4], (dim, dim), dtype=jnp.float32) * s
        bo = jnp.zeros((dim,), dtype=jnp.float32)
        proj = jax.random.normal(ks[5], (m, dh), dtype=jnp.float32)
        return {'x': x, 'Wq': Wq, 'Wk': Wk, 'Wv': Wv, 'Wo': Wo, 'bo': bo, 'proj': proj}
    _L1_mix_all = _L1_mix_setup()
    _L1_mix_in = {k: v for k, v in _L1_mix_all.items() if k in ('Wq', 'Wk', 'Wv', 'Wo', 'bo', 'proj')}
    del _L1_mix_all

    def _L1_ffn_setup():
        import jax, jax.numpy as jnp
        import numpy as np
        B, S, D, E, O = (1024, 256, 512, 16, 512)
        key = jax.random.key(seed)
        k_x, k_wg, k_bg, k_we, k_be = jax.random.split(key, 5)
        scale_g = 1.0 / np.sqrt(D)
        scale_e = 1.0 / np.sqrt(D)
        return {'x': jax.random.normal(k_x, (B, S, D), dtype=jnp.float32), 'Wg': jax.random.uniform(k_wg, (D, E), jnp.float32, -scale_g, scale_g), 'bg': jax.random.uniform(k_bg, (E,), jnp.float32, -scale_g, scale_g), 'We': jax.random.uniform(k_we, (E, D, O), jnp.float32, -scale_e, scale_e), 'be': jax.random.uniform(k_be, (E, O), jnp.float32, -scale_e, scale_e)}
    _L1_ffn_all = _L1_ffn_setup()
    _L1_ffn_in = {k: v for k, v in _L1_ffn_all.items() if k in ('Wg', 'bg', 'We', 'be')}
    del _L1_ffn_all
    return {'x': x, 'src': src, 'dst': dst, 'edge_attr_8': edge_attr_8, 'L0_gnn_ln_g': _L0_gnn_in['ln_g'], 'L0_gnn_ln_b': _L0_gnn_in['ln_b'], 'L0_gnn_Wq': _L0_gnn_in['Wq'], 'L0_gnn_bq': _L0_gnn_in['bq'], 'L0_gnn_Wk': _L0_gnn_in['Wk'], 'L0_gnn_bk': _L0_gnn_in['bk'], 'L0_gnn_Wv': _L0_gnn_in['Wv'], 'L0_gnn_bv': _L0_gnn_in['bv'], 'L0_gnn_W1': _L0_gnn_in['W1'], 'L0_gnn_b1': _L0_gnn_in['b1'], 'L0_gnn_W2': _L0_gnn_in['W2'], 'L0_gnn_b2': _L0_gnn_in['b2'], 'L0_mix_Wqkv': _L0_mix_in['Wqkv'], 'L0_mix_Wout': _L0_mix_in['Wout'], 'L0_mix_bout': _L0_mix_in['bout'], 'L0_ffn_Wg': _L0_ffn_in['Wg'], 'L0_ffn_bg': _L0_ffn_in['bg'], 'L0_ffn_W1': _L0_ffn_in['W1'], 'L0_ffn_b1': _L0_ffn_in['b1'], 'L0_ffn_W2': _L0_ffn_in['W2'], 'L0_ffn_b2': _L0_ffn_in['b2'], 'L1_gnn_W1l': _L1_gnn_in['W1l'], 'L1_gnn_b1l': _L1_gnn_in['b1l'], 'L1_gnn_W1r': _L1_gnn_in['W1r'], 'L1_gnn_W2l': _L1_gnn_in['W2l'], 'L1_gnn_b2l': _L1_gnn_in['b2l'], 'L1_gnn_W2r': _L1_gnn_in['W2r'], 'L1_gnn_ln1_w': _L1_gnn_in['ln1_w'], 'L1_gnn_ln1_b': _L1_gnn_in['ln1_b'], 'L1_gnn_ln2_w': _L1_gnn_in['ln2_w'], 'L1_gnn_ln2_b': _L1_gnn_in['ln2_b'], 'L1_mix_Wq': _L1_mix_in['Wq'], 'L1_mix_Wk': _L1_mix_in['Wk'], 'L1_mix_Wv': _L1_mix_in['Wv'], 'L1_mix_Wo': _L1_mix_in['Wo'], 'L1_mix_bo': _L1_mix_in['bo'], 'L1_mix_proj': _L1_mix_in['proj'], 'L1_ffn_Wg': _L1_ffn_in['Wg'], 'L1_ffn_bg': _L1_ffn_in['bg'], 'L1_ffn_We': _L1_ffn_in['We'], 'L1_ffn_be': _L1_ffn_in['be']}

def reference(x, src, dst, edge_attr_8, L0_gnn_ln_g, L0_gnn_ln_b, L0_gnn_Wq, L0_gnn_bq, L0_gnn_Wk, L0_gnn_bk, L0_gnn_Wv, L0_gnn_bv, L0_gnn_W1, L0_gnn_b1, L0_gnn_W2, L0_gnn_b2, L0_mix_Wqkv, L0_mix_Wout, L0_mix_bout, L0_ffn_Wg, L0_ffn_bg, L0_ffn_W1, L0_ffn_b1, L0_ffn_W2, L0_ffn_b2, L1_gnn_W1l, L1_gnn_b1l, L1_gnn_W1r, L1_gnn_W2l, L1_gnn_b2l, L1_gnn_W2r, L1_gnn_ln1_w, L1_gnn_ln1_b, L1_gnn_ln2_w, L1_gnn_ln2_b, L1_mix_Wq, L1_mix_Wk, L1_mix_Wv, L1_mix_Wo, L1_mix_bo, L1_mix_proj, L1_ffn_Wg, L1_ffn_bg, L1_ffn_We, L1_ffn_be):
    import jax
    import jax.numpy as jnp

    def _L0_gnn_ref(x, edge_index, edge_weights, ln_g, ln_b, Wq, bq, Wk, bk, Wv, bv, W1, b1, W2, b2):
        import jax, jax.numpy as jnp
        import numpy as np
        N, E, D, H = (1250, 20000, 512, 8)
        HD = D // H
        SCALE = HD ** (-0.5)

        def _layernorm(x, g, b):
            mu = jnp.mean(x, axis=-1, keepdims=True)
            var = jnp.mean(jnp.square(x - mu), axis=-1, keepdims=True)
            return (x - mu) * jax.lax.rsqrt(var + 1e-05) * g + b
        origin, destination = (edge_index[0], edge_index[1])
        x_norm = _layernorm(x, ln_g, ln_b)
        q = (x_norm @ Wq + bq).reshape(N, H, HD)
        k = (x_norm @ Wk + bk).reshape(N, H, HD)
        v = (x_norm @ Wv + bv).reshape(N, H, HD)
        scores = jnp.einsum('ehd,ehd->eh', q[origin], k[destination]) * SCALE
        ws = scores * edge_weights
        seg_max = jax.ops.segment_max(ws, origin, num_segments=N)
        seg_max = jnp.where(jnp.isfinite(seg_max), seg_max, 0.0)
        e = jnp.exp(ws - seg_max[origin])
        denom = jax.ops.segment_sum(e, origin, num_segments=N)
        att = e / (denom[origin] + 1e-16)
        weighted_values = att[:, :, None] * v[destination]
        values = jax.ops.segment_sum(weighted_values, origin, num_segments=N)
        values = values.reshape(N, D)
        values = (values @ W1 + b1) @ W2 + b2
        return x + values

    def _L0_mix_ref(x, Wqkv, Wout, bout):
        import jax, jax.numpy as jnp
        import numpy as np
        HEADS = 8
        DIM_HEAD = 64
        B, L, D = x.shape
        H, C = (HEADS, DIM_HEAD)
        qkv = jnp.einsum('bld,od->bol', x, Wqkv)
        qkv = qkv.reshape(B, 3, H, C, L)
        q, k, v = (qkv[:, 0], qkv[:, 1], qkv[:, 2])
        k = jax.nn.softmax(k, axis=-1)
        q = jax.nn.softmax(q, axis=-2)
        context = jnp.einsum('bhdn,bhen->bhde', k, v)
        out = jnp.einsum('bhde,bhdn->bhen', context, q)
        out = out.reshape(B, H * C, L)
        y = jnp.einsum('bcl,dc->bld', out, Wout) + bout
        return y

    def _L0_ffn_ref(x, Wg, bg, W1, b1, W2, b2):
        import jax, jax.numpy as jnp
        import numpy as np
        NUM_EXPERTS = 8
        TOP_K = 2
        HIDDEN = 512
        INTERMEDIATE = 256
        BATCH, SEQ = (8, 256)
        B, S, H = x.shape
        xf = x.reshape(B * S, H)
        logits = xf @ Wg + bg
        probs = jax.nn.softmax(logits, axis=-1)
        _, top_idx = jax.lax.top_k(probs, TOP_K)
        mask = jnp.any(top_idx[:, :, None] == jnp.arange(NUM_EXPERTS)[None, None, :], axis=1)
        comb = probs * mask.astype(probs.dtype)
        out = jnp.zeros_like(xf)
        for e in range(NUM_EXPERTS):
            h = jax.nn.gelu(xf @ W1[e] + b1[e])
            y = h @ W2[e] + b2[e]
            out = out + comb[:, e:e + 1] * y
        return out.reshape(B, S, H)

    def _L1_gnn_ref(x, edge_index, W1l, b1l, W1r, W2l, b2l, W2r, ln1_w, ln1_b, ln2_w, ln2_b):
        import jax, jax.numpy as jnp
        import numpy as np
        N, E, D = (6250, 50000, 512)

        def _sage_conv(x, src, dst, Wl, bl, Wr, n_nodes):
            agg = jax.ops.segment_sum(x[src], dst, num_segments=n_nodes)
            deg = jax.ops.segment_sum(jnp.ones((src.shape[0],), x.dtype), dst, num_segments=n_nodes)
            agg = agg / jnp.maximum(deg, 1.0)[:, None]
            return agg @ Wl.T + bl + x @ Wr.T

        def _layer_norm(h, w, b, eps=1e-05):
            mu = jnp.mean(h, axis=-1, keepdims=True)
            var = jnp.mean(jnp.square(h - mu), axis=-1, keepdims=True)
            return (h - mu) * jax.lax.rsqrt(var + eps) * w + b
        src, dst = (edge_index[0], edge_index[1])
        n_nodes = x.shape[0]
        h = _sage_conv(x, src, dst, W1l, b1l, W1r, n_nodes)
        h = jax.nn.relu(_layer_norm(h, ln1_w, ln1_b)) + x
        h2 = _sage_conv(h, src, dst, W2l, b2l, W2r, n_nodes)
        h2 = _layer_norm(h2, ln2_w, ln2_b)
        return h2 + h

    def _L1_mix_ref(x, Wq, Wk, Wv, Wo, bo, proj):
        import jax, jax.numpy as jnp
        import numpy as np
        HEADS = 8
        DIM_HEAD = 64
        EPS = 0.0001

        def softmax_kernel(data, proj, is_query):
            data_normalizer = data.shape[-1] ** (-0.25)
            ratio = proj.shape[0] ** (-0.5)
            data_dash = jnp.einsum('bhnd,md->bhnm', data_normalizer * data, proj)
            diag = (data * data).sum(-1) * 0.5 * data_normalizer ** 2
            diag = diag[..., None]
            if is_query:
                stab = jnp.max(data_dash, axis=-1, keepdims=True)
            else:
                stab = jnp.max(data_dash)
            return ratio * (jnp.exp(data_dash - diag - stab) + EPS)

        def linear_attention(q, k, v):
            k_cumsum = k.sum(axis=-2)
            d_inv = 1.0 / jnp.einsum('bhnm,bhm->bhn', q, k_cumsum)
            context = jnp.einsum('bhnm,bhne->bhme', k, v)
            return jnp.einsum('bhme,bhnm,bhn->bhne', context, q, d_inv)
        b, n, dim = x.shape
        h, dh = (HEADS, DIM_HEAD)
        q = (x @ Wq).reshape(b, n, h, dh).transpose(0, 2, 1, 3)
        k = (x @ Wk).reshape(b, n, h, dh).transpose(0, 2, 1, 3)
        v = (x @ Wv).reshape(b, n, h, dh).transpose(0, 2, 1, 3)
        qp = softmax_kernel(q, proj, is_query=True)
        kp = softmax_kernel(k, proj, is_query=False)
        out = linear_attention(qp, kp, v)
        out = out.transpose(0, 2, 1, 3).reshape(b, n, h * dh)
        return out @ Wo + bo

    def _L1_ffn_ref(x, Wg, bg, We, be):
        import jax, jax.numpy as jnp
        import numpy as np
        B, S, D, E, O = (1024, 256, 512, 16, 512)
        scores = jax.nn.softmax(jnp.mean(x, axis=1) @ Wg + bg, axis=-1)
        idx = jnp.argmax(scores, axis=-1)
        gate = jnp.take_along_axis(scores, idx[:, None], axis=-1)
        W_sel = We[idx]
        b_sel = be[idx]
        y = jnp.einsum('bsd,bdo->bso', x, W_sel) + b_sel[:, None, :]
        return gate[:, :, None] * y
    edge_index = jnp.stack([src, dst])
    xn = _layernorm(x, axis=-1)
    x = x + _L0_gnn_ref(xn, edge_index, edge_attr_8, L0_gnn_ln_g, L0_gnn_ln_b, L0_gnn_Wq, L0_gnn_bq, L0_gnn_Wk, L0_gnn_bk, L0_gnn_Wv, L0_gnn_bv, L0_gnn_W1, L0_gnn_b1, L0_gnn_W2, L0_gnn_b2) + _L0_mix_ref(xn[None], L0_mix_Wqkv, L0_mix_Wout, L0_mix_bout)[0]
    x = x + _L0_ffn_ref(_layernorm(x, axis=-1)[None], L0_ffn_Wg, L0_ffn_bg, L0_ffn_W1, L0_ffn_b1, L0_ffn_W2, L0_ffn_b2)[0]
    xn = _layernorm(x, axis=-1)
    x = x + _L1_gnn_ref(xn, edge_index, L1_gnn_W1l, L1_gnn_b1l, L1_gnn_W1r, L1_gnn_W2l, L1_gnn_b2l, L1_gnn_W2r, L1_gnn_ln1_w, L1_gnn_ln1_b, L1_gnn_ln2_w, L1_gnn_ln2_b) + _L1_mix_ref(xn[None], L1_mix_Wq, L1_mix_Wk, L1_mix_Wv, L1_mix_Wo, L1_mix_bo, L1_mix_proj)[0]
    x = x + _L1_ffn_ref(_layernorm(x, axis=-1)[None], L1_ffn_Wg, L1_ffn_bg, L1_ffn_We, L1_ffn_be)[0]
    return x

_drawn_inputs = setup_inputs


def setup_inputs(seed=0):
    import zlib

    import numpy as np

    out = dict(_drawn_inputs(seed))
    spreads = {'L0_gnn_ln_g': (1.0, 0.2),
     'L0_gnn_ln_b': (0.0, 0.1),
     'L0_gnn_bq': (0.0, 0.649),
     'L0_gnn_bk': (0.0, 0.8),
     'L0_gnn_bv': (0.0, 0.1),
     'L0_gnn_b1': (0.0, 0.1),
     'L0_gnn_b2': (0.0, 0.1),
     'L0_mix_bout': (0.0, 0.1),
     'L0_ffn_bg': (0.0, 0.328),
     'L0_ffn_b1': (0.0, 0.55),
     'L0_ffn_b2': (0.0, 0.363),
     'L1_gnn_b1l': (0.0, 0.1),
     'L1_gnn_b2l': (0.0, 0.1),
     'L1_gnn_ln1_w': (1.0, 0.2),
     'L1_gnn_ln1_b': (0.0, 0.278),
     'L1_gnn_ln2_w': (1.0, 0.2),
     'L1_gnn_ln2_b': (0.0, 0.1),
     'L1_mix_bo': (0.0, 0.1)}
    factors = {'L1_mix_Wq': 8.0,
     'L1_mix_Wk': 8.0,
     'L1_mix_proj': 8.0,
     'L1_ffn_Wg': 28.8,
     'L1_ffn_bg': 57.115,
     'L1_ffn_We': 4.315,
     'L1_ffn_be': 29.908}
    for name, (base, spread) in spreads.items():
        noise = np.random.default_rng([zlib.crc32(name.encode()), seed]).standard_normal(out[name].shape)
        drawn = base * np.exp(spread * noise) if base else spread * noise
        out[name] = jnp.asarray(drawn.astype(out[name].dtype))
    for name, factor in factors.items():
        out[name] = (out[name] * factor).astype(out[name].dtype)
    return out
```

```python
from collections import namedtuple
from contextlib import ExitStack

import concourse.bass as bass
from concourse import mybir
import numpy as np

P = 128
N = 1250
D = 512
E = 20000
H = 8
HD = D // H
NT = 10
NP = NT * P
LAST = N - (NT - 1) * P
KC = D // P
GRP = [(0, 4), (4, 4), (8, 2)]
CH = [(0, 512), (512, 512), (1024, 256)]
EP = 125
ET = E // EP
ST = 176
RW = 12
HI, LO = 40, 32
M = 266
MC = [(0, 128), (128, 128), (256, 10)]
EXP0, HID0 = 8, 256
EXP1 = 16
SCALE = float(HD) ** -0.5
BIG = 1.0e30
LN_EPS = 1e-5

F32 = mybir.dt.float32
BF16 = mybir.dt.bfloat16
F16 = mybir.dt.float16
I32 = mybir.dt.int32
U32 = mybir.dt.uint32
ALU = mybir.AluOpType
ACT = mybir.ActivationFunctionType
AX = mybir.AxisListType


def constants():
    i = np.arange(P)
    c = np.zeros((P, 1056), np.float32)
    c[:, 0:128] = np.eye(P)
    c[:, 128:256] = i[None, :]
    c[:, 256:256 + HI] = np.arange(HI)
    c[:, 256 + HI:256 + HI + LO] = np.arange(LO)
    h = np.arange(HI)
    c[:HI, 384:424] = (h[:, None] // 4 == h[None, :] // 4) & (h[:, None] < h[None, :])
    c[:HI, 424:464] = h[:, None] // 4 == h[None, :] // 4
    c[:HI, 464:504] = (h[:, None] % 4 == 0) & (h[:, None] // 4 < h[None, :] // 4)
    b = np.arange(11)
    c[:HI, 504:515] = (h[:, None] % 4 == 0) & (h[:, None] // 4 < b[None, :])
    c[:, 520:648] = i[None, :] < i[:, None]
    c[:, 648:650] = (i[:, None] // HD) == np.arange(2)[None, :]
    c[:, 656:784] = (i[:, None] // HD) == (i[None, :] // HD)
    c[:, 784:792] = np.arange(8)
    c[:8, 792 + 128:792 + 136] = np.eye(8)
    return c, np.broadcast_to(np.arange(NP, dtype=np.float16), (P, NP)).copy()


class Build:

    def __init__(self, nc, a, out):
        self.nc, self.a, self.out, self.stage = nc, a, out, 0

    def tools(self, ctx, sems):
        nc = self.nc
        self.stage = n = self.stage + 1
        sb = lambda name, shape, dt=F32: ctx.enter_context(nc.sbuf_tensor(f"s{n}_{name}", shape, dt))
        ps = lambda name, shape, dt=F32: ctx.enter_context(nc.psum_tensor(f"s{n}_{name}", shape, dt))
        self.held = held = []
        ctx.callback(self.clear, held)
        s = namedtuple("Semaphores", sems)(*[self.semaphore(f"{n}_{self.stage}") for n in sems.split()])
        return sb, ps, s

    def clear(self, held):
        if held:
            self.nc.clear_and_free_semaphores(held)
            self.nc.all_engine_barrier()

    def semaphore(self, name):
        self.held.append(self.nc.alloc_semaphore(name))
        return self.held[-1]


def chain(eng, sem):
    n = [0]

    def link(ins):
        n[0] += 1
        ins.then_inc(sem, 1)
        eng.wait_ge(sem, n[0])
    return link


class Filler:

    def __init__(self, pe, banks, full, free):
        self.pe, self.banks, self.full, self.free, self.n = pe, banks, full, free, 0

    def take(self):
        n, k = self.n, len(self.banks)
        self.n += 1
        if n >= k:
            self.pe.wait_ge(self.free, n - k + 1)
        return self.banks[n % k]

    def done(self, ins):
        ins.then_inc(self.full, 1)


class Emptier:

    def __init__(self, eng, banks, full, free):
        self.eng, self.banks, self.full, self.free, self.n = eng, banks, full, free, 0

    def take(self):
        self.n += 1
        self.eng.wait_ge(self.full, self.n)
        return self.banks[(self.n - 1) % len(self.banks)]

    def done(self, ins):
        ins.then_inc(self.free, 1)

    def all_done(self):
        self.eng.wait_ge(self.free, self.n)


def product(nc, dst, lhs, rhs, first=True, last=True):
    for i, (x, y) in enumerate(zip(lhs, rhs)):
        ins = nc.tensor.matmul(dst, x, y, start=first and i == 0, stop=last and i == len(lhs) - 1)
    return ins


def tile(x, t):
    return [x[:, c, t * P:(t + 1) * P] for c in range(x.shape[1])]


def chunks(w, c0=0, cw=D):
    return [w[:, c, c0:c0 + cw] for c in range(w.shape[1])]


def transposes(nc, fill, rows, ident, t0, nt, c):
    dst = fill.take()
    for t in range(nt):
        last = nc.tensor.transpose(dst[:, t * P:(t + 1) * P], rows[:, t0 + t, c * P:(c + 1) * P], ident)
    fill.done(last)


class Norm:

    def __init__(self, nc, sb, name):
        self.nc = nc
        self.st, self.mv, self.ln = sb(name + "_st", [P, NT, 6]), sb(name + "_mv", [P, NT, 2]), sb(name + "_ln", [P, 3, NT])

    def stats(self, link, rows, stats_sem):
        v = self.nc.vector
        for t in range(NT):
            last = v.bn_stats(self.st[:, t, :], rows[:, t, :])
        link(last)
        for t in range(NT):
            last = v.bn_aggr(self.mv[:, t, :], self.st[:, t, :])
        link(last)
        v.tensor_scalar_add(self.ln[:, 0, :], self.mv[:, :, 1], LN_EPS).then_inc(stats_sem, 1)

    def root(self, act, stats_sem, n, sd_sem):
        act.wait_ge(stats_sem, n)
        self.nc.scalar.activation(self.ln[:, 0, :], self.ln[:, 0, :], ACT.Sqrt).then_inc(sd_sem, 1)

    def scales(self, dve, link, sd_sem, n, ready_sem):
        v, ln = self.nc.vector, self.ln
        dve.wait_ge(sd_sem, n)
        link(v.reciprocal(ln[:, 1, :], ln[:, 0, :]))
        v.scalar_tensor_tensor(out=ln[:, 2, :], in0=self.mv[:, :, 0], scalar=-1.0, in1=ln[:, 1, :],
                               op0=ALU.mult, op1=ALU.mult).then_inc(ready_sem, 1)

    def apply(self, out, rows, t):
        return self.nc.scalar.activation(out[:, t, :], rows[:, t, :], ACT.Identity, scale=self.ln[:, 1, t:t + 1],
                                         bias=self.ln[:, 2, t:t + 1])


def row_chunks(w):
    return w.rearrange("(c p) n -> p c n", p=P)


def bcast(v, parts=P):
    return v.rearrange("(a n) -> a n", a=1).broadcast_to([parts, v.shape[0]])


def prepare(b, top):
    nc, a = b.nc, b.a
    psb, _, _ = b.tools(top, "")
    b.cst = psb("cst", [P, 1056])
    b.iota_h = psb("iota_h", [P, NP], F16)
    b.starts = psb("starts", [1, 16], I32)
    b.cols = psb("cols", [P, 28])
    b.R0 = psb("R0", [P, NT, D])
    b.xnT = psb("xnT", [P, KC, NP])
    b.q_dram = nc.dram_tensor("q_dram", (NP, D), F32).ap()
    b.k_dram = nc.dram_tensor("k_dram", (NP, D), F32).ap()
    b.v_dram = nc.dram_tensor("v_dram", (NP, D), F32).ap()
    b.rec_dram = nc.dram_tensor("rec_dram", (P * ST, RW), F32).ap()
    cst = b.cst
    ident = cst[:, 0:128]

    with ExitStack() as ctx:
        sb, ps, s = b.tools(ctx, "cst_in x_in ids_in ew_in gb_in zeroed stats sd rs xn added xn2 tp tp_free onehot "
                                "chain_v chain_p counted offs_ps based pairs mm mm_free ids rec_ready pad_ready "
                                "pad_out scattered kv_sb identb_in")
        w_in = [b.semaphore(f"w_in{i}") for i in range(3)]
        kv_out = [b.semaphore(f"kv_out{i}") for i in range(4)]
        oh_reg = sb("xn_rows", [P, ET * (HI + LO) // 2])
        xn = oh_reg[:, 0:NT * D].rearrange("p (t d) -> p t d", t=NT)
        oh = oh_reg[:, :].bitcast(BF16).rearrange("p (t j) -> p t j", t=ET)
        xn2_reg = sb("xn2_rows", [P, NT * D])
        xn2 = xn2_reg[:, :].rearrange("p (t d) -> p t d", t=NT)
        cum = xn2_reg[:HI, 0:LO * ET].rearrange("p (l t) -> p l t", l=LO)
        xnormT = sb("xnormT", [P, KC, NP])
        ohT = sb("ohT", [HI + LO, ET, EP], BF16)
        hist = sb("hist", [HI, LO, ET], BF16)
        base_hi = sb("base_hi", [HI, LO, ET], BF16)
        w = [sb(f"w{i}", [P, KC, D]) for i in range(2)]
        rec = sb("rec", [EP, ET, RW])
        bias = sb("bias", [P, 2, D])
        st = sb("st", [P, NT, 6])
        mv = sb("mv", [P, NT, 2])
        ln = sb("ln", [P, 3, NT])
        identb = sb("identb", [P, P], BF16)
        ids_i = sb("ids_i", [EP, 2, ET], I32)
        hilo = sb("hilo", [EP, 2, ET], I32)
        lof = sb("lof", [EP, ET])
        tmp_i = sb("tmp_i", [EP, ET], I32)
        off = sb("off", [HI, 4])
        off_i = sb("off_i", [HI, 2], I32)
        rank = sb("rank", [EP, ET])
        basev = sb("basev", [EP, ET])
        rowid = sb("rowid", [EP, ET], I32)
        pos = sb("pos", [EP, 3, 16], I32)
        pad = sb("pad", [P, ST // 4, RW])
        kvs = oh_reg[:, 0:4 * D].rearrange("p (j d) -> p j d", j=4)
        bank = [ps(f"bank{i}", [P, D]) for i in range(8)]
        FULL = (NT - 1) * P
        PROJ = [("L0_gnn_Wk", "L0_gnn_bk", b.k_dram), ("L0_gnn_Wv", "L0_gnn_bv", b.v_dram),
                ("L0_gnn_Wq", "L0_gnn_bq", b.q_dram)]
        MAGIC = 1.5 * 2.0 ** 23 * 256

        block = ctx.enter_context(nc.Block())

        def store(sp, i, j):
            n = i * NT + j
            sp.wait_ge(s.kv_sb, n + 1)
            sp.dma_start(PROJ[i][2][j * P:(j + 1) * P, :], kvs[:, n % 4, :]).then_inc(kv_out[n % 4], 16)

        @block.sync
        def _(sp):
            sp.dma_start(cst[:, :], a["c_cst"]).then_inc(s.cst_in, 16)
            sp.dma_start(b.iota_h[:, :], a["c_iota"]).then_inc(s.cst_in, 16)
            sp.dma_start(b.R0[:, 0:NT - 1, :], a["x"][0:FULL].rearrange("(t p) d -> p t d", p=P)).then_inc(s.x_in, 16)
            sp.wait_ge(s.zeroed, 1)
            sp.dma_start(b.R0[0:LAST, NT - 1, :], a["x"][FULL:N]).then_inc(s.x_in, 16)
            sp.dma_start(ids_i[:, 0, :], a["src"].rearrange("(p t) -> p t", p=EP)).then_inc(s.ids_in, 16)
            sp.dma_start(ids_i[:, 1, :], a["dst"].rearrange("(p t) -> p t", p=EP)).then_inc(s.ids_in, 16)
            sp.dma_start(b.cols[:, :], a["c_cols"]).then_inc(s.gb_in, 16)
            for i, (wn, bn, _) in enumerate(PROJ):
                if i == 2:
                    sp.wait_ge(s.kv_sb, NT)
                sp.dma_start(w[i % 2][:, :, :], row_chunks(a[wn])).then_inc(w_in[i], 16)
                sp.dma_start(bias[:, i % 2, :], bcast(a[bn])).then_inc(w_in[i], 16)
                if i == 0:
                    sp.dma_start(rec[:, :, 4:RW], a["edge_attr_8"].rearrange("(p t) h -> p t h", p=EP)).then_inc(s.ew_in, 16)
                if i == 1:
                    sp.wait_ge(s.pad_ready, 1)
                    for j in range(4):
                        sp.dma_start(b.rec_dram.rearrange("(p t) w -> p t w", p=P)[:, j * ST // 4:(j + 1) * ST // 4, :],
                                     pad[:, :, :]).then_inc(s.pad_out, 16)
                    for j in range(NT):
                        store(sp, 0, j)
            for i in (1, 2):
                for j in range(NT):
                    store(sp, i, j)
            for i in range(4):
                sp.wait_ge(kv_out[i], 16 * len(range(i, 3 * NT, 4)))

        @block.gpsimd
        def _(pool):
            link = chain(pool, s.chain_p)
            link(nc.gpsimd.memset(pad[:, :, :], 0.0))
            for j in (0, 3):
                last = nc.gpsimd.memset(pad[:, :, j:j + 1], -1.0)
            last.then_inc(s.pad_ready, 1)
            for t in range(NT):
                pool.wait_ge(s.xn, t + 1)
                nc.gpsimd.tensor_tensor(b.R0[:, t, :], b.R0[:, t, :], xn[:, t, :], ALU.add).then_inc(s.added, 1)
            pool.wait_ge(s.rec_ready, 1)
            pool.wait_ge(s.ew_in, 16)
            pool.wait_ge(s.pad_out, 64)
            for t in range(ET):
                if t % 16 == 0:
                    pool.wait_ge(s.ids, t // 16 + 1)
                nc.gpsimd.indirect_dma_start(
                    out=b.rec_dram, out_offset=bass.IndirectOffsetOnAxis(ap=rowid[:, t:t + 1], axis=0),
                    in_=rec[:, t, :], in_offset=None).then_inc(s.scattered, 16)
            pool.wait_ge(s.scattered, 16 * ET)

        @block.scalar
        def _(act):
            def sqrt_var(n):
                act.wait_ge(s.stats, n)
                nc.scalar.activation(ln[:, 0, :], ln[:, 0, :], ACT.Sqrt).then_inc(s.sd, 1)

            sqrt_var(1)
            act.wait_ge(s.rs, 1)
            for t in range(NT):
                nc.scalar.activation(xn[:, t, :], b.R0[:, t, :], ACT.Identity, scale=ln[:, 1, t:t + 1],
                                     bias=ln[:, 2, t:t + 1]).then_inc(s.xn, 1)
            sqrt_var(2)
            n = 0
            act.wait_ge(s.gb_in, 16)
            for which in range(2):
                for t0, nt in GRP:
                    for c in range(KC):
                        act.wait_ge(s.tp, n + 1)
                        cols = slice(t0 * P, (t0 + nt) * P)
                        if which == 0:
                            ins = nc.scalar.activation(b.xnT[:, c, cols], bank[n % 4][:, 0:nt * P], ACT.Copy)
                        else:
                            ins = nc.scalar.activation(xnormT[:, c, cols], bank[n % 4][:, 0:nt * P], ACT.Identity,
                                                       scale=b.cols[:, c:c + 1], bias=b.cols[:, KC + c:KC + c + 1])
                        ins.then_inc(s.tp_free, 1)
                        n += 1
            for g in range(ET // 8):
                act.wait_ge(s.tp, n + 1)
                nc.scalar.activation(ohT[:, 8 * g:8 * g + 8, :],
                                     bank[n % 4][:, :].bitcast(BF16)[:HI + LO, :].rearrange("p (t e) -> p t e", t=8)[:, :, 0:EP],
                                     ACT.Copy).then_inc(s.tp_free, 1)
                n += 1
            for g in range(ET // 16):
                act.wait_ge(s.tp, n + 1)
                nc.scalar.activation(hist[:, :, 16 * g:16 * g + 16],
                                     bank[n % 4][:HI, :].rearrange("p (t l) -> p l t", t=16),
                                     ACT.Copy).then_inc(s.tp_free, 1)
                n += 1

        @block.vector
        def _(dve):
            link = chain(dve, s.chain_v)
            nc.vector.memset(b.R0[96:P, NT - 1, :], 0.0).then_inc(s.zeroed, 1)
            dve.wait_ge(s.cst_in, 32)
            nc.vector.tensor_copy(identb[:, :], ident).then_inc(s.identb_in, 1)

            def stats(rows, wait):
                for t in range(NT):
                    wait(t)
                    last = nc.vector.bn_stats(st[:, t, :], rows[:, t, :])
                link(last)
                for t in range(NT):
                    last = nc.vector.bn_aggr(mv[:, t, :], st[:, t, :])
                link(last)
                nc.vector.tensor_scalar_add(ln[:, 0, :], mv[:, :, 1], LN_EPS).then_inc(s.stats, 1)

            def scales(n):
                dve.wait_ge(s.sd, n)
                link(nc.vector.reciprocal(ln[:, 1, :], ln[:, 0, :]))
                link(nc.vector.scalar_tensor_tensor(out=ln[:, 2, :], in0=mv[:, :, 0], scalar=-1.0, in1=ln[:, 1, :],
                                                    op0=ALU.mult, op1=ALU.mult))

            stats(b.R0, lambda t: dve.wait_ge(s.x_in, 32) if t == 0 else None)
            scales(1)
            nc.vector.engine_nop().then_inc(s.rs, 1)
            stats(xn, lambda t: dve.wait_ge(s.xn, t + 1))
            scales(2)
            for t in range(NT):
                nc.vector.tensor_scalar(xn2[:, t, :], xn[:, t, :], ln[:, 1, t:t + 1], ln[:, 2, t:t + 1],
                                        ALU.mult, ALU.add).then_inc(s.xn2, 1)
            dve.wait_ge(s.ids_in, 32)
            nc.vector.tensor_scalar(hilo[:, 0, :], ids_i[:, 0, :], 5, None, ALU.logical_shift_right)
            nc.vector.tensor_scalar(tmp_i[:, :], ids_i[:, 0, :], P - 1, None, ALU.bitwise_and)
            link(nc.vector.tensor_scalar(hilo[:, 1, :], ids_i[:, 0, :], LO - 1, None, ALU.bitwise_and))
            nc.vector.tensor_copy(lof[:, :], hilo[:, 1, :])
            nc.vector.tensor_copy(rec[:, :, 0], tmp_i[:, :])
            nc.vector.tensor_copy(rec[:, :, 1], ids_i[:, 1, :])
            nc.vector.tensor_copy(rec[:, :, 2].bitcast(I32), ids_i[:, 1, :])
            nc.vector.tensor_copy(rec[:, :, 3], ids_i[:, 0, :]).then_inc(s.rec_ready, 1)
            dve.wait_ge(s.tp_free, 24)
            dve.wait_ge(s.added, NT)
            nc.vector.tensor_tensor(oh[:EP, :, 0:HI], hilo[:, 0, :].unsqueeze(2).broadcast_to([EP, ET, HI]),
                                    cst[:EP, 256:256 + HI].unsqueeze(1).broadcast_to([EP, ET, HI]), ALU.is_equal)
            nc.vector.tensor_tensor(oh[:EP, :, HI:], hilo[:, 1, :].unsqueeze(2).broadcast_to([EP, ET, LO]),
                                    cst[:EP, 256 + HI:256 + HI + LO].unsqueeze(1).broadcast_to([EP, ET, LO]),
                                    ALU.is_equal).then_inc(s.onehot, 1)
            dve.wait_ge(s.tp_free, 24 + ET // 8 + ET // 16)
            link(nc.vector.tensor_tensor_scan(cum.rearrange("p l t -> p (l t)"), hist[:, :, :].rearrange("p l t -> p (l t)"),
                                              hist[:, :, :].rearrange("p l t -> p (l t)"), 0.0, ALU.add, ALU.max))
            link(nc.vector.tensor_copy(off[:, 0:1], cum[:, LO - 1, ET - 1:ET]))
            nc.vector.engine_nop().then_inc(s.counted, 1)
            dve.wait_ge(s.offs_ps, 1)
            link(nc.vector.tensor_copy(off[:, 1:3], bank[4][:HI, 0:2]))
            link(nc.vector.tensor_scalar(off_i[:, 0:1], off[:, 2:3], 255.0, None, ALU.add))
            link(nc.vector.tensor_scalar(off_i[:, 1:2], off_i[:, 0:1], 8, None, ALU.logical_shift_right))
            nc.vector.tensor_scalar(off[:, 3:4], off_i[:, 1:2], 1.0, None, ALU.max).then_inc(s.pairs, 1)
            dve.wait_ge(s.offs_ps, 2)
            link(nc.vector.tensor_copy(b.starts[0:1, 0:11], bank[4][0:1, 16:27]))
            link(nc.vector.tensor_scalar(b.starts[0:1, 12:13], b.starts[0:1, 10:11], 1.0, None, ALU.add))
            link(nc.vector.tensor_scalar(b.starts[0:1, 11:12], b.starts[0:1, 12:13], 1, None, ALU.logical_shift_right))
            link(nc.vector.tensor_scalar(b.starts[0:1, 10:11], b.starts[0:1, 11:12], 2.0, None, ALU.mult))
            link(nc.vector.scalar_tensor_tensor(out=off[:, 2:3], in0=bank[4][:HI, 8:9], scalar=256.0, in1=off[:, 1:2],
                                                op0=ALU.mult, op1=ALU.add))
            link(nc.vector.scalar_tensor_tensor(out=cum, in0=cum, scalar=off[:, 2:3], in1=hist[:, :, :],
                                                op0=ALU.add, op1=ALU.subtract))
            link(nc.vector.tensor_scalar(base_hi[:, :, :], cum, MAGIC, -MAGIC, ALU.add, ALU.add))
            nc.vector.tensor_tensor(hist[:, :, :], cum, base_hi[:, :, :], ALU.subtract).then_inc(s.based, 1)

            n = 0
            for g in range(ET // 16):
                for q in range(4):
                    dve.wait_ge(s.mm, n + 1)
                    for i in range(4):
                        t = 16 * g + 4 * q + i
                        last = nc.vector.scalar_tensor_tensor(
                            out=bank[4 + n % 4][:EP, i * EP:(i + 1) * EP], in0=bank[4 + n % 4][:EP, i * EP:(i + 1) * EP], scalar=1.5,
                            in1=cst[:EP, 520:520 + EP], op0=ALU.is_ge, op1=ALU.mult, accum_out=rank[:, t:t + 1])
                    last.then_inc(s.mm_free, 1)
                    n += 1
                dve.wait_ge(s.mm, n + 1)
                for i in range(16):
                    t = 16 * g + i
                    last = nc.vector.scalar_tensor_tensor(
                        out=bank[4 + n % 4][:EP, i * LO:(i + 1) * LO], in0=cst[:EP, 256 + HI:256 + HI + LO], scalar=lof[:, t:t + 1],
                        in1=bank[4 + n % 4][:EP, i * LO:(i + 1) * LO], op0=ALU.is_equal, op1=ALU.mult,
                        accum_out=basev[:, t:t + 1])
                last.then_inc(s.mm_free, 1)
                n += 1
                dve.wait_ge(s.mm_free, n)
                sl = slice(16 * g, 16 * g + 16)
                link(nc.vector.tensor_tensor(pos[:, 0, :], basev[:, sl], rank[:, sl], ALU.add))
                nc.vector.tensor_scalar(pos[:, 1, :], pos[:, 0, :], 7, None, ALU.logical_shift_right)
                link(nc.vector.tensor_scalar(pos[:, 2, :], pos[:, 0, :], P - 1, None, ALU.bitwise_and))
                nc.vector.scalar_tensor_tensor(out=rowid[:, sl], in0=pos[:, 2, :], scalar=float(ST), in1=pos[:, 1, :],
                                               op0=ALU.mult, op1=ALU.add).then_inc(s.ids, 1)
                for j in range(3 * g, 3 * g + 3):
                    dve.wait_ge(s.mm, n + 1)
                    if j % NT == 0:
                        dve.wait_ge(w_in[j // NT], 32)
                    if j >= 4:
                        dve.wait_ge(kv_out[j % 4], 16 * (j // 4))
                    nc.vector.tensor_tensor(kvs[:, j % 4, :], bank[4 + n % 4][:, :], bias[:, (j // NT) % 2, :],
                                            ALU.add).then_inc(s.kv_sb, 1)
                    n += 1
                    dve.wait_ge(s.kv_sb, j + 1)
                    nc.vector.engine_nop().then_inc(s.mm_free, 1)

        @block.tensor
        def _(pe):
            pe.wait_ge(s.cst_in, 32)
            n = 0
            for which in range(2):
                for t0, nt in GRP:
                    pe.wait_ge((s.xn, s.xn2)[which], t0 + nt)
                    for c in range(KC):
                        if n >= 4:
                            pe.wait_ge(s.tp_free, n - 3)
                        for t in range(nt):
                            last = nc.tensor.transpose(bank[n % 4][:, t * P:(t + 1) * P],
                                                       (xn, xn2)[which][:, t0 + t, c * P:(c + 1) * P], ident)
                        last.then_inc(s.tp, 1)
                        n += 1
            pe.wait_ge(s.onehot, 1)
            pe.wait_ge(s.identb_in, 1)
            for g in range(ET // 8):
                pe.wait_ge(s.tp_free, n - 3)
                for i in range(8):
                    last = nc.tensor.transpose(bank[n % 4][:, :].bitcast(BF16)[:HI + LO, i * P:i * P + EP],
                                               oh[:EP, 8 * g + i, :], identb[:EP, :EP])
                last.then_inc(s.tp, 1)
                n += 1
            for g in range(ET // 16):
                pe.wait_ge(s.tp_free, n - 3)
                for i in range(16):
                    last = nc.tensor.matmul(bank[n % 4][:HI, i * LO:(i + 1) * LO], oh[:EP, 16 * g + i, 0:HI],
                                            oh[:EP, 16 * g + i, HI:], start=True, stop=True)
                last.then_inc(s.tp, 1)
                n += 1
            pe.wait_ge(s.counted, 1)
            nc.tensor.matmul(bank[4][:HI, 0:1], cst[:HI, 384:424], off[:, 0:1], start=True, stop=True)
            nc.tensor.matmul(bank[4][:HI, 1:2], cst[:HI, 424:464], off[:, 0:1], start=True, stop=True).then_inc(s.offs_ps, 1)
            pe.wait_ge(s.pairs, 1)
            nc.tensor.matmul(bank[4][:HI, 8:9], cst[:HI, 464:504], off[:, 3:4], start=True, stop=True)
            nc.tensor.matmul(bank[4][0:1, 16:27], off[:, 3:4], cst[:HI, 504:515], start=True, stop=True).then_inc(s.offs_ps, 1)
            pe.wait_ge(s.based, 1)

            n = 0

            def free(n):
                if n >= 4:
                    pe.wait_ge(s.mm_free, n - 3)

            for g in range(ET // 16):
                for q in range(4):
                    free(n)
                    for i in range(4):
                        t = 16 * g + 4 * q + i
                        last = nc.tensor.matmul(bank[4 + n % 4][:EP, i * EP:(i + 1) * EP], ohT[:, t, :], ohT[:, t, :],
                                                start=True, stop=True)
                    last.then_inc(s.mm, 1)
                    n += 1
                free(n)
                for i in range(16):
                    t = 16 * g + i
                    out = bank[4 + n % 4][:EP, i * LO:(i + 1) * LO]
                    nc.tensor.matmul(out, ohT[:HI, t, :], base_hi[:, :, t], start=True, stop=False)
                    last = nc.tensor.matmul(out, ohT[:HI, t, :], hist[:, :, t], start=False, stop=True)
                last.then_inc(s.mm, 1)
                n += 1
                for j in range(3 * g, 3 * g + 3):
                    free(n)
                    if j % NT == 0:
                        pe.wait_ge(w_in[j // NT], 32)
                    t = j % NT
                    for c in range(KC):
                        last = nc.tensor.matmul(bank[4 + n % 4][:, :], xnormT[:, c, t * P:(t + 1) * P],
                                                w[(j // NT) % 2][:, c, :], start=(c == 0), stop=(c == KC - 1))
                    last.then_inc(s.mm, 1)
                    n += 1



def linear_attention(b, top):
    nc, a, cst = b.nc, b.a, b.cst
    ident = cst[:, 0:128]
    with ExitStack() as ctx:
        sb, ps, s = b.tools(ctx, "fa fa_free fd fd_free kmax kexp qsub qexp qn v_in krow qT_in ctx_in cv ca")
        w_in = [b.semaphore(f"mw_in{i}") for i in range(3)]
        w = [sb(f"w{i}", [P, KC, D]) for i in range(3)]
        kT = sb("kT", [P, KC, NP])
        q = sb("q", [P, NT, D])
        v = sb("v", [P, NT, D])
        krow = sb("krow", [P, NT, D])
        qT = sb("qT", [P, KC, NP])
        nmax = sb("nmax", [P, KC])
        ksum = sb("ksum", [P, KC])
        rsum = sb("rsum", [P, KC])
        hm = sb("hm", [P, NT, 3, H])
        cx = sb("cx", [P, KC, P])
        bank = [ps(f"bank{i}", [P, D]) for i in range(8)]
        block = ctx.enter_context(nc.Block())

        @block.sync
        def _(sp):
            for i in (1, 0, 2):
                sp.dma_start(w[i][:, :, :], row_chunks(a["L0_mix_WqkvT"])[:, :, i * D:(i + 1) * D]).then_inc(w_in[i], 16)

        @block.tensor
        def _(pe):
            na, nd = [0], [0]

            def fill_a():
                n = na[0]
                na[0] += 1
                if n >= 4:
                    pe.wait_ge(s.fa_free, n - 3)
                return bank[n % 4]

            def fill_d():
                n = nd[0]
                nd[0] += 1
                if n >= 4:
                    pe.wait_ge(s.fd_free, n - 3)
                return bank[4 + n % 4]

            def rows(dst, wi, t, sem):
                for c in range(KC):
                    last = nc.tensor.matmul(dst[:, :], b.xnT[:, c, t * P:(t + 1) * P], w[wi][:, c, :], start=(c == 0), stop=(c == KC - 1))
                last.then_inc(sem, 1)

            pe.wait_ge(w_in[1], 16)
            for m in range(KC):
                for c0, cw in CH:
                    dst = fill_a()
                    for c in range(KC):
                        last = nc.tensor.matmul(dst[:, 0:cw], w[1][:, c, m * P:(m + 1) * P], b.xnT[:, c, c0:c0 + cw],
                                                start=(c == 0), stop=(c == KC - 1))
                    last.then_inc(s.fa, 1)
            pe.wait_ge(w_in[0], 16)
            pe.wait_ge(w_in[2], 16)
            for t in range(NT):
                rows(fill_d(), 0, t, s.fd)
                rows(fill_a(), 2, t, s.fa)
            for m in range(KC):
                pe.wait_ge(s.kexp, m + 1)
                for t0, nt in GRP:
                    dst = fill_a()
                    for t in range(nt):
                        last = nc.tensor.transpose(dst[:, t * P:(t + 1) * P], kT[:, m, (t0 + t) * P:(t0 + t + 1) * P], ident)
                    last.then_inc(s.fa, 1)
            for t0, nt in GRP:
                pe.wait_ge(s.qn, t0 + nt)
                for m in range(KC):
                    dst = fill_a()
                    for t in range(nt):
                        last = nc.tensor.transpose(dst[:, t * P:(t + 1) * P], q[:, t0 + t, m * P:(m + 1) * P], ident)
                    last.then_inc(s.fa, 1)
            pe.wait_ge(s.v_in, NT)
            pe.wait_ge(s.krow, 3 * KC)
            for m in range(KC):
                dst = fill_d()
                for t in range(NT):
                    last = nc.tensor.matmul(dst[:, 0:P], krow[:, t, m * P:(m + 1) * P], v[:, t, m * P:(m + 1) * P],
                                            start=(t == 0), stop=(t == NT - 1))
                last.then_inc(s.fd, 1)
            pe.wait_ge(s.qT_in, 3 * KC)
            for m in range(KC):
                pe.wait_ge(s.ctx_in, m + 1)
                for c0, cw in CH:
                    dst = fill_a()
                    nc.tensor.matmul(dst[:, 0:cw], cx[:, m, :], qT[:, m, c0:c0 + cw], start=True, stop=True).then_inc(s.fa, 1)

        @block.scalar
        def _(act):
            n = [0]

            def empty(out, shape, sem):
                act.wait_ge(s.fa, n[0] + 1)
                src = bank[n[0] % 4][:, 0:shape]
                if len(out.shape) == 3:
                    src = src.rearrange("p (t d) -> p t d", d=out.shape[2])
                n[0] += 1
                nc.scalar.activation(out, src, ACT.Copy).then_inc(s.fa_free, 1)

            link = chain(act, s.ca)
            for m in range(KC):
                for c0, cw in CH:
                    empty(kT[:, m, c0:c0 + cw], cw, None)
            for m in range(KC):
                act.wait_ge(s.kmax, m + 1)
                nc.scalar.activation(kT[:, m, 0:N], kT[:, m, 0:N], ACT.Exp, bias=nmax[:, m:m + 1],
                                     accum_out=ksum[:, m:m + 1]).then_inc(s.kexp, 1)
            for t in range(NT):
                act.wait_ge(s.qsub, t + 1)
                nc.scalar.activation(q[:, t, :], q[:, t, :], ACT.Exp).then_inc(s.qexp, 1)
                empty(v[:, t, :], D, None)
            act.wait_ge(s.fa_free, n[0])
            act.sem_inc(s.v_in, NT)
            for m in range(KC):
                for t0, nt in GRP:
                    empty(krow[:, t0:t0 + nt, m * P:(m + 1) * P], nt * P, None)
            act.wait_ge(s.fa_free, n[0])
            act.sem_inc(s.krow, 3 * KC)
            for t0, nt in GRP:
                for m in range(KC):
                    empty(qT[:, m, t0 * P:(t0 + nt) * P], nt * P, None)
            act.wait_ge(s.fa_free, n[0])
            act.sem_inc(s.qT_in, 3 * KC)
            for m in range(KC):
                for c0, cw in CH:
                    empty(b.xnT[:, m, c0:c0 + cw], cw, None)
            act.wait_ge(s.fa_free, n[0])

        @block.vector
        def _(dve):
            link = chain(dve, s.cv)
            for m in range(KC):
                dve.wait_ge(s.fa_free, 3 * (m + 1))
                nc.vector.memset(kT[:, m, N:NP], 0.0)
                nc.vector.tensor_reduce(nmax[:, m:m + 1], kT[:, m, 0:N], AX.X, ALU.max, negate=True).then_inc(s.kmax, 1)
            heads = lambda x: x.rearrange("p (h d) -> p h d", h=H)
            each = lambda x: x.unsqueeze(2).broadcast_to([P, H, HD])

            def normalise(t):
                dve.wait_ge(s.qexp, t + 1)
                link(nc.vector.tensor_reduce(hm[:, t, 1, :], heads(q[:, t, :]), AX.X, ALU.add))
                link(nc.vector.reciprocal(hm[:, t, 2, :], hm[:, t, 1, :]))
                nc.vector.tensor_tensor(heads(q[:, t, :]), heads(q[:, t, :]), each(hm[:, t, 2, :]), ALU.mult).then_inc(s.qn, 1)

            for t in range(NT):
                dve.wait_ge(s.fd, t + 1)
                link(nc.vector.tensor_reduce(hm[:, t, 0, :], heads(bank[4 + t % 4][:, :]), AX.X, ALU.max))
                nc.vector.tensor_tensor(heads(q[:, t, :]), heads(bank[4 + t % 4][:, :]), each(hm[:, t, 0, :]),
                                        ALU.subtract).then_inc(s.qsub, 1)
                dve.wait_ge(s.qsub, t + 1)
                dve.sem_inc(s.fd_free, 1)
                if t:
                    normalise(t - 1)
            normalise(NT - 1)
            dve.wait_ge(s.kexp, KC)
            link(nc.vector.reciprocal(rsum[:, :], ksum[:, :]))
            for m in range(KC):
                dve.wait_ge(s.fd, NT + m + 1)
                nc.vector.scalar_tensor_tensor(out=cx[:, m, :], in0=bank[4 + (NT + m) % 4][:, 0:P], scalar=rsum[:, m:m + 1],
                                               in1=cst[:, 656:784], op0=ALU.mult, op1=ALU.mult).then_inc(s.ctx_in, 1)


def bounds(b, eng, cols):
    return [eng.value_load(b.starts[0:1, j:j + 1], min_val=0 if j == 0 else 1, max_val=ST // (4 if j == 11 else 2))
            for j in cols]


def edge_scores(b, top):
    nc = b.nc
    psb, _, _ = b.tools(top, "")
    b.AT = psb("AT", [P, NT, NP])
    b.vals = psb("vals", [P, NT, D])
    b.den = psb("den", [P, NT, H])
    b.mid = top.enter_context(ExitStack())
    psb, _, _ = b.tools(b.mid, "")
    b.recs = psb("recs", [P, ST + 4, RW])
    b.W = psb("W", [P, ST, H])
    with ExitStack() as ctx:
        sb, ps, s = b.tools(ctx, "loaded zeroed oh0 oh1 tp0 tp1 ohT0 ohT1 qe0 qe1 prod0 prod1 red chain_p issued")
        arrived = [b.semaphore(f"k_in{i}") for i in range(4)]
        q_rows = sb("q_rows", [P, NT, D])
        ohf = [sb(f"ohf{i}", [P, P]) for i in range(2)]
        ohT = [sb(f"ohT_{i}", [P, P]) for i in range(2)]
        prod = [sb(f"prod{i}", [P, D]) for i in range(2)]
        kbuf = [sb(f"kbuf{i}", [P, D]) for i in range(4)]
        idx = [sb(f"idx{i}", [P, 1], I32) for i in range(4)]
        psT = [ps(f"psT{i}", [P, P]) for i in range(2)]
        psQ = [ps(f"psQ{i}", [P, D]) for i in range(2)]
        oh_s, tp, ohT_s, qe, prod_s = (s.oh0, s.oh1), (s.tp0, s.tp1), (s.ohT0, s.ohT1), (s.qe0, s.qe1), (s.prod0, s.prod1)
        recs, W = b.recs, b.W
        block = ctx.enter_context(nc.Block())

        @block.sync
        def _(sp):
            sp.dma_start(recs[:, 0:ST, :], b.rec_dram.rearrange("(p t) w -> p t w", p=P)).then_inc(s.loaded, 16)
            sp.dma_start(q_rows[:, :, :], b.q_dram.rearrange("(t p) d -> p t d", p=P)).then_inc(s.loaded, 16)


        @block.gpsimd
        def _(pool):
            pool.wait_ge(s.loaded, 32)
            pool.wait_ge(s.zeroed, 2)
            twos, = bounds(b, pool, (11,))
            with pool.Fori(0, twos) as v:
                for k in range(4):
                    pool.wait_ge(prod_s[k % 2], v * 2 + (k // 2 + 1))
                    nc.gpsimd.tensor_copy(idx[k][:, :], recs[:, bass.ds(v * 4 + k, 1), 2].bitcast(I32)).then_inc(s.chain_p, 1)
                    pool.wait_ge(s.chain_p, v * 4 + (k + 1))
                    pool.sem_inc(s.issued, 1)
                    nc.gpsimd.indirect_dma_start(out=kbuf[k][:, :], out_offset=None, in_=b.k_dram,
                                                 in_offset=bass.IndirectOffsetOnAxis(ap=idx[k][:, :], axis=0)
                                                 ).then_inc(arrived[k], 16)

        @block.scalar
        def _(act):
            twos, = bounds(b, act, (11,))
            with act.Fori(0, twos) as v:
                for k in range(4):
                    i = k % 2
                    act.wait_ge(tp[i], v * 2 + (k // 2 + 1))
                    act.wait_ge(qe[i], v * 2 + (k // 2 + 1))
                    nc.scalar.activation(ohT[i][:, :], psT[i][:, :], ACT.Copy).then_inc(ohT_s[i], 1)

        @block.vector
        def _(dve):
            nc.vector.memset(W[:, :, :], 0.0).then_inc(s.zeroed, 1)
            nc.vector.memset(recs[:, ST:ST + 4, :], 0.0).then_inc(s.zeroed, 1)
            dve.wait_ge(s.zeroed, 2)
            dve.wait_ge(s.loaded, 32)
            dve.sem_inc(s.prod0, 2)
            dve.sem_inc(s.prod1, 2)

            def one_hot(i, t):
                nc.vector.tensor_scalar(ohf[i][:, :], b.cst[:, 128:256], recs[:, t, 0], None,
                                        ALU.is_equal).then_inc(oh_s[i], 1)

            for i in range(2):
                one_hot(i, slice(i, i + 1))
            twos, = bounds(b, dve, (11,))
            with dve.Fori(0, twos) as v:
                for h in range(2):
                    for i in range(2):
                        dve.wait_ge(tp[i], v * 2 + (h + 1))
                        one_hot(i, bass.ds(v * 4 + (2 * h + 2 + i), 1))
                    for i in range(2):
                        dve.wait_ge(qe[i], v * 2 + (h + 2))
                        dve.wait_ge(arrived[2 * h + i], v * 16 + 16)
                        nc.vector.tensor_tensor(prod[i][:, :], psQ[i][:, :], kbuf[2 * h + i][:, :],
                                                ALU.mult).then_inc(prod_s[i], 1)
                    for i in range(2):
                        dve.wait_ge(prod_s[i], v * 2 + (h + 3))
                        nc.vector.tensor_reduce(W[:, bass.ds(v * 4 + (2 * h + i), 1), :],
                                                prod[i][:, :].rearrange("p (h d) -> p h d", h=H), AX.X,
                                                ALU.add).then_inc(s.red, 1)
                    dve.wait_ge(s.red, v * 4 + (2 * h + 2))

        @block.tensor
        def _(pe):
            pe.wait_ge(s.loaded, 32)
            pe.sem_inc(s.qe0, 1)
            pe.sem_inc(s.qe1, 1)
            at = bounds(b, pe, range(11))
            for j in range(NT):
                with pe.Fori(at[j], at[j + 1]) as u:
                    for i in range(2):
                        pe.wait_ge(oh_s[i], u + 1)
                        nc.tensor.transpose(psT[i][:, :], ohf[i][:, :], b.cst[:, 0:128]).then_inc(tp[i], 1)
                    for i in range(2):
                        pe.wait_ge(ohT_s[i], u + 1)
                        pe.wait_ge(prod_s[i], u + 2)
                        nc.tensor.matmul(psQ[i][:, :], ohT[i][:, :], q_rows[:, j, :], start=True,
                                         stop=True).then_inc(qe[i], 1)


def edge_softmax(b, top):
    nc, cst = b.nc, b.cst
    G = ST // 16
    with ExitStack() as ctx:
        sb, ps, s = b.tools(ctx, "c srep_s tpw tps evac sel selc back evc tb fin")
        srep = sb("srep", [P, ST, H])
        Wt = sb("Wt", [P, G * P])
        Ft = sb("Ft", [P, G, P])
        Fs = sb("Fs", [P, G * P + 4])
        B = sb("B", [P, G, P])
        T = sb("T", [P, G, P])
        X = sb("X", [P, 4, G])
        Y = sb("Y", [H, 4, G * 16 + 2])
        nf = sb("nf", [H, ST])
        cf = sb("cf", [H, ST + 2])
        mc = sb("mc", [H, ST])
        UV = sb("UV", [H, 2, ST + 2])
        LR = sb("LR", [H, 2, ST])
        LRb = sb("LRb", [P, 2, G])
        bank = [ps(f"sb{i}", [P, D]) for i in range(8)]
        W, recs = b.W, b.recs
        ident = cst[:, 0:128]
        flat = lambda x: x[:, :, :].rearrange("p g e -> p (g e)")
        block = ctx.enter_context(nc.Block())

        @block.vector
        def _(dve):
            link = chain(dve, s.c)
            v = nc.vector
            v.tensor_copy(srep[:, :, :], recs[:, 0:ST, 3].unsqueeze(2).broadcast_to([P, ST, H])).then_inc(s.srep_s, 1)
            v.scalar_tensor_tensor(out=W[:, :, :], in0=W[:, :, :], scalar=SCALE, in1=recs[:, 0:ST, 4:RW],
                                   op0=ALU.mult, op1=ALU.mult).then_inc(s.srep_s, 1)
            v.memset(Fs[:, :], -BIG)
            v.memset(Y[:, :, :], -1.0)
            v.memset(cf[:, :], -BIG)
            link(v.memset(UV[:, :, :], -BIG))
            dve.wait_ge(s.evac, 6)
            link(v.tensor_tensor(T[:, :, 1:P], Ft[:, :, 1:P], Ft[:, :, 0:P - 1], ALU.not_equal))
            link(v.tensor_scalar(Fs[:, 0:G * P].rearrange("p (g e) -> p g e", g=G)[:, :, 1:P], T[:, :, 1:P], -BIG, None, ALU.mult))
            link(v.tensor_tensor_scan(flat(T), Fs[:, 0:G * P], Wt[:, :], -BIG, ALU.add, ALU.max))
            link(v.tensor_tensor_scan(flat(B)[:, ::-1], Fs[:, 1:G * P + 1][:, ::-1], flat(T)[:, ::-1], -BIG, ALU.add, ALU.max))
            v.tensor_copy(X[:, 0, :], B[:, :, 0])
            v.tensor_copy(X[:, 1, :], B[:, :, P - 1])
            v.tensor_copy(X[:, 2, :], Ft[:, :, 0])
            v.tensor_copy(X[:, 3, :], Ft[:, :, P - 1]).then_inc(s.sel, 1)
            dve.wait_ge(s.selc, 1)
            link(v.tensor_copy(Y[:, 0:2, 0:ST].rearrange("h q (g t) -> h q g t", t=16),
                               bank[0][:H, 0:16 * 2 * G].rearrange("h (t q g) -> h q g t", t=16, q=2)))
            link(v.tensor_copy(Y[:, 2:4, 0:ST].rearrange("h q (g t) -> h q g t", t=16),
                               bank[1][:H, 0:16 * 2 * G].rearrange("h (t q g) -> h q g t", t=16, q=2)))
            link(v.tensor_tensor(nf[:, :], Y[:, 2, 0:ST], Y[:, 3, 0:ST], ALU.not_equal))
            link(v.tensor_tensor(mc[:, 1:ST], Y[:, 2, 1:ST], Y[:, 3, 0:ST - 1], ALU.not_equal))
            link(v.tensor_scalar(cf[:, 1:ST], mc[:, 1:ST], -BIG, None, ALU.mult))
            link(v.scalar_tensor_tensor(out=mc[:, :], in0=nf[:, :], scalar=-BIG, in1=cf[:, 0:ST], op0=ALU.mult, op1=ALU.add))
            link(v.tensor_tensor_scan(UV[:, 0, 1:ST + 1], mc[:, :], Y[:, 1, 0:ST], -BIG, ALU.add, ALU.max))
            link(v.scalar_tensor_tensor(out=mc[:, :], in0=nf[:, :], scalar=-BIG, in1=cf[:, 1:ST + 1], op0=ALU.mult, op1=ALU.add))
            link(v.tensor_tensor_scan(UV[:, 1, 0:ST][:, ::-1], mc[:, ::-1], Y[:, 0, 0:ST][:, ::-1], -BIG, ALU.add, ALU.max))
            v.tensor_tensor(LR[:, 0, :], UV[:, 0, 0:ST], cf[:, 0:ST], ALU.add)
            v.tensor_tensor(LR[:, 1, :], UV[:, 1, 1:ST + 1], cf[:, 1:ST + 1], ALU.add).then_inc(s.back, 1)
            dve.wait_ge(s.evc, 1)
            link(v.tensor_copy(LRb[:, :, :], bank[2][:, 0:2 * G].rearrange("p (q g) -> p q g", q=2)))
            for q, e in ((0, 0), (1, P - 1)):
                link(v.tensor_tensor(T[:, :, :], Ft[:, :, :], Ft[:, :, e:e + 1].broadcast_to([P, G, P]), ALU.not_equal))
                link(v.scalar_tensor_tensor(out=T[:, :, :], in0=T[:, :, :], scalar=-BIG,
                                            in1=LRb[:, q, :].unsqueeze(2).broadcast_to([P, G, P]), op0=ALU.mult, op1=ALU.add))
                link(v.tensor_tensor(B[:, :, :], B[:, :, :], T[:, :, :], ALU.max))
            v.engine_nop().then_inc(s.tb, 1)
            for n in range(3):
                g0, g1 = 4 * n, min(4 * n + 4, G)
                dve.wait_ge(s.fin, n + 1)
                last = v.tensor_tensor(W[:, 16 * g0:16 * g1, :], W[:, 16 * g0:16 * g1, :],
                                       bank[3 + n][:, 0:(g1 - g0) * P].rearrange("p (t h) -> p t h", h=H), ALU.subtract)
            link(last)
            v.engine_nop().then_inc(s.evac, 1)

        @block.tensor
        def _(pe):
            for which, src in ((0, srep), (1, W)):
                pe.wait_ge(s.srep_s, which + 1)
                for n in range(3):
                    for g in range(4 * n, min(4 * n + 4, G)):
                        last = nc.tensor.transpose(bank[3 * which + n][:, (g - 4 * n) * P:(g - 4 * n + 1) * P],
                                                   src[:, 16 * g:16 * g + 16, :].rearrange("p t h -> p (t h)"), ident)
                    last.then_inc(s.tps, 1)
            pe.wait_ge(s.sel, 1)
            for q in range(2):
                for t in range(16):
                    last = nc.tensor.matmul(bank[q][:H, t * 2 * G:(t + 1) * 2 * G], ident[:, 8 * t:8 * t + 8],
                                            X[:, 2 * q:2 * q + 2, :].rearrange("p q g -> p (q g)"), start=True, stop=True)
            last.then_inc(s.selc, 1)
            pe.wait_ge(s.back, 1)
            for q in range(2):
                for t in range(16):
                    last = nc.tensor.matmul(bank[2][:, q * G:(q + 1) * G], cst[:H, 792 + 128 - 8 * t:792 + 256 - 8 * t],
                                            LR[:, q, :].rearrange("h (g t) -> h t g", t=16)[:, t, :],
                                            start=(t == 0), stop=(t == 15))
            last.then_inc(s.evc, 1)
            pe.wait_ge(s.tb, 1)
            for n in range(3):
                for g in range(4 * n, min(4 * n + 4, G)):
                    last = nc.tensor.transpose(bank[3 + n][:, (g - 4 * n) * P:(g - 4 * n + 1) * P], B[:, g, :], ident)
                last.then_inc(s.fin, 1)

        @block.scalar
        def _(act):
            for which, dst in ((0, flat(Ft)), (1, Wt)):
                for n in range(3):
                    w = (min(4 * n + 4, G) - 4 * n) * P
                    act.wait_ge(s.tps, 3 * which + n + 1)
                    nc.scalar.activation(dst[:, 4 * n * P:4 * n * P + w], bank[3 * which + n][:, 0:w], ACT.Copy).then_inc(s.evac, 1)
            act.wait_ge(s.evac, 7)
            nc.scalar.activation(W[:, :, :], W[:, :, :], ACT.Exp).then_inc(s.tpw, 1)
            act.wait_ge(s.tpw, 1)


def edge_sums(b, top):
    nc = b.nc
    with ExitStack() as ctx:
        sb, ps, s = b.tools(ctx, "zeroed made0 made1 oh0 oh1 used0 used1 summed kept chain_p issued")
        arrived = [b.semaphore(f"v_in{i}") for i in range(4)]
        made, used, oh_s = (s.made0, s.made1), (s.used0, s.used1), (s.oh0, s.oh1)
        ohf = [sb(f"ohf{i}", [P, P]) for i in range(2)]
        ohb = [sb(f"ohb{i}", [P, P], BF16) for i in range(2)]
        ohd = [sb(f"ohd{i}", [P, NP], BF16) for i in range(2)]
        ew = [sb(f"ew{i}", [P, H]) for i in range(2)]
        vw = [sb(f"vw{i}", [P, D]) for i in range(2)]
        vbuf = [sb(f"vbuf{i}", [P, D]) for i in range(4)]
        idx = [sb(f"vidx{i}", [P, 1], I32) for i in range(4)]
        zeros = sb("zeros", [1, D], BF16)
        pV = ps("pV", [P, D])
        pD = ps("pD", [P, H])
        pA = [ps(f"pA{i}", [P, D]) for i in range(3)]
        recs, W = b.recs, b.W
        block = ctx.enter_context(nc.Block())


        @block.gpsimd
        def _(pool):
            twos, = bounds(b, pool, (11,))
            with pool.Fori(0, twos) as v:
                for k in range(4):
                    pool.wait_ge(used[k % 2], v * 2 + (k // 2 + 1))
                    nc.gpsimd.tensor_copy(idx[k][:, :], recs[:, bass.ds(v * 4 + k, 1), 2].bitcast(I32)).then_inc(s.chain_p, 1)
                    pool.wait_ge(s.chain_p, v * 4 + (k + 1))
                    pool.sem_inc(s.issued, 1)
                    nc.gpsimd.indirect_dma_start(out=vbuf[k][:, :], out_offset=None, in_=b.v_dram,
                                                 in_offset=bass.IndirectOffsetOnAxis(ap=idx[k][:, :], axis=0)
                                                 ).then_inc(arrived[k], 16)

        @block.vector
        def _(dve):
            nc.vector.memset(zeros[:, :], 0.0).then_inc(s.zeroed, 1)
            dve.sem_inc(s.used0, 2)
            dve.sem_inc(s.used1, 2)
            twos, = bounds(b, dve, (11,))
            with dve.Fori(0, twos) as v:
                for k in range(4):
                    i, h = k % 2, k // 2
                    t = bass.ds(v * 4 + k, 1)
                    dve.wait_ge(used[i], v * 2 + (h + 2))
                    nc.vector.tensor_scalar(ohf[i][:, :], b.cst[:, 128:256], recs[:, t, 0], None, ALU.is_equal)
                    nc.vector.tensor_scalar(ohb[i][:, :], b.iota_h[:, 0:P], recs[:, t, 0], None, ALU.is_equal)
                    nc.vector.tensor_scalar(ohd[i][:, :], b.iota_h[:, :], recs[:, t, 1], None, ALU.is_equal)
                    nc.vector.tensor_copy(ew[i][:, :].unsqueeze(1), W[:, t, :]).then_inc(oh_s[i], 1)
                    dve.wait_ge(arrived[k], v * 16 + 16)
                    nc.vector.tensor_tensor(vw[i][:, :].rearrange("p (h d) -> p h d", h=H),
                                            vbuf[k][:, :].rearrange("p (h d) -> p h d", h=H),
                                            W[:, t, :].rearrange("p t h -> p (t h)").unsqueeze(2).broadcast_to([P, H, HD]),
                                            ALU.mult).then_inc(made[i], 1)

        @block.tensor
        def _(pe):
            pe.wait_ge(s.zeroed, 1)
            at = bounds(b, pe, range(11))
            for j in range(NT):
                if j:
                    pe.wait_ge(s.kept, 5 * j)
                for dst, w in ((pV, D), (pD, H), (pA[0], 512), (pA[1], 512), (pA[2], 256)):
                    nc.tensor.matmul(dst[:, 0:w], zeros[:, 0:P], zeros[:, 0:w], start=True, stop=False, skip_group_check=True)
                with pe.Fori(at[j], at[j + 1]) as u:
                    for i in range(2):
                        pe.wait_ge(oh_s[i], u + 1)
                        nc.tensor.matmul(pD[:, :], ohf[i][:, :], ew[i][:, :], start=False, stop=False, skip_group_check=True)
                        for (c0, cw), dst in zip(CH, pA):
                            nc.tensor.matmul(dst[:, 0:cw], ohb[i][:, :], ohd[i][:, c0:c0 + cw], start=False, stop=False,
                                             skip_group_check=True)
                        pe.wait_ge(made[i], u + 1)
                        nc.tensor.matmul(pV[:, :], ohf[i][:, :], vw[i][:, :], start=False, stop=False,
                                         skip_group_check=True).then_inc(used[i], 1)
                for dst, w in ((pV, D), (pD, H), (pA[0], 512), (pA[1], 512), (pA[2], 256)):
                    last = nc.tensor.matmul(dst[:, 0:w], zeros[:, 0:P], zeros[:, 0:w], start=False, stop=True, skip_group_check=True)
                last.then_inc(s.summed, 1)

        @block.scalar
        def _(act):
            for j in range(NT):
                act.wait_ge(s.summed, j + 1)
                for out, src in [(b.vals[:, j, :], pV[:, :]), (b.den[:, j, :], pD[:, :])] \
                        + [(b.AT[:, j, c0:c0 + cw], p[:, 0:cw]) for (c0, cw), p in zip(CH, pA)]:
                    nc.scalar.activation(out, src, ACT.Copy).then_inc(s.kept, 1)
            act.wait_ge(s.kept, 5 * NT)
    b.mid.close()


def attention_out(b, top):
    nc, a = b.nc, b.a
    ident = b.cst[:, 0:128]
    with ExitStack() as ctx:
        sb, ps, s = b.tools(ctx, "fa fa_free fd fd_free w_in b_in normed biased stats sd scaled xf cv cp vt_in h_in")
        w1, w2, wo = sb("w1", [P, KC, D]), sb("w2", [P, KC, D]), sb("wo", [P, KC, D])
        vT, hT = sb("vT", [P, KC, NP]), sb("hT", [P, KC, NP])
        bias = sb("bias", [P, 2, D])
        rden = sb("rden", [P, NT, H])
        norm = Norm(nc, sb, "x1")
        bank = [ps(f"bank{i}", [P, D]) for i in range(8)]
        vals, R0, mixT = b.vals, b.R0, b.xnT
        block = ctx.enter_context(nc.Block())

        @block.sync
        def _(sp):
            sp.dma_start(w1[:, :, :], row_chunks(a["L0_gnn_W1"])).then_inc(s.w_in, 16)
            sp.dma_start(w2[:, :, :], row_chunks(a["L0_gnn_W2"])).then_inc(s.w_in, 16)
            sp.dma_start(wo[:, :, :], row_chunks(a["L0_mix_WoutT"])).then_inc(s.w_in, 16)
            sp.dma_start(bias[:, 0, :], bcast(a["L0_gnn_b2"])).then_inc(s.b_in, 16)
            sp.dma_start(bias[:, 1, :], bcast(a["L0_mix_bout"])).then_inc(s.b_in, 16)

        @block.gpsimd
        def _(pool):
            link = chain(pool, s.cp)
            pool.wait_ge(s.b_in, 32)
            link(nc.gpsimd.tensor_tensor(bias[:, 0, :], bias[:, 0, :], bias[:, 1, :], ALU.add))
            for t in range(NT):
                nc.gpsimd.tensor_tensor(R0[:, t, :], R0[:, t, :], bias[:, 0, :], ALU.add).then_inc(s.biased, 1)

        @block.vector
        def _(dve):
            link = chain(dve, s.cv)
            v = nc.vector
            link(v.tensor_scalar_add(rden[:, :, :], b.den[:, :, :], 1e-16))
            link(v.reciprocal(rden[:, :, :], rden[:, :, :]))
            for t in range(NT):
                v.tensor_tensor(vals[:, t, :].rearrange("p (h d) -> p h d", h=H), vals[:, t, :].rearrange("p (h d) -> p h d", h=H),
                                rden[:, t, :].unsqueeze(2).broadcast_to([P, H, HD]), ALU.mult).then_inc(s.normed, 1)
            full = Emptier(dve, bank[4:], s.fd, s.fd_free)
            for t in range(NT):
                dve.wait_ge(s.biased, t + 1)
                src = full.take()
                full.done(v.tensor_tensor(R0[:, t, :], R0[:, t, :], src[:, :], ALU.add))
            full.all_done()
            norm.stats(link, R0, s.stats)
            norm.scales(dve, link, s.sd, 1, s.scaled)

        @block.scalar
        def _(act):
            full = Emptier(act, bank[:4], s.fa, s.fa_free)
            for t0, nt in GRP:
                for c in range(KC):
                    src = full.take()
                    full.done(nc.scalar.activation(vT[:, c, t0 * P:(t0 + nt) * P], src[:, 0:nt * P], ACT.Copy))
            full.all_done()
            act.sem_inc(s.vt_in, 1)
            for m in range(KC):
                for c0, cw in CH:
                    src = full.take()
                    full.done(nc.scalar.activation(hT[:, m, c0:c0 + cw], src[:, 0:cw], ACT.Identity,
                                                   bias=b.cols[:, 8 + m:9 + m]))
            full.all_done()
            act.sem_inc(s.h_in, 1)
            norm.root(act, s.stats, 1, s.sd)
            act.wait_ge(s.scaled, 1)
            for t in range(NT):
                norm.apply(vals, R0, t).then_inc(s.xf, 1)
            for t0, nt in GRP:
                for c in range(KC):
                    src = full.take()
                    full.done(nc.scalar.activation(mixT[:, c, t0 * P:(t0 + nt) * P], src[:, 0:nt * P], ACT.Copy))
            full.all_done()

        @block.tensor
        def _(pe):
            fa = Filler(pe, bank[:4], s.fa, s.fa_free)
            fd = Filler(pe, bank[4:], s.fd, s.fd_free)
            for t0, nt in GRP:
                pe.wait_ge(s.normed, t0 + nt)
                for c in range(KC):
                    transposes(nc, fa, vals, ident, t0, nt, c)
            pe.wait_ge(s.w_in, 48)
            pe.wait_ge(s.vt_in, 1)
            for m in range(KC):
                for c0, cw in CH:
                    dst = fa.take()
                    fa.done(product(nc, dst[:, 0:cw], chunks(w1, m * P, P), chunks(vT, c0, cw)))
            pe.wait_ge(s.h_in, 1)
            for t in range(NT):
                dst = fd.take()
                fd.done(product(nc, dst[:, :], tile(hT, t) + tile(mixT, t), chunks(w2) + chunks(wo)))
            for t0, nt in GRP:
                pe.wait_ge(s.xf, t0 + nt)
                for c in range(KC):
                    transposes(nc, fa, vals, ident, t0, nt, c)


def experts0(b, top):
    nc, a, cst = b.nc, b.a, b.cst
    ident = cst[:, 0:128]
    with ExitStack() as ctx:
        sb, ps, s = b.tools(ctx, "fa fa_free fd fd_free g_in lg combT_in comb_in h_in0 h_in1 cv exp_s")
        w_in = [b.semaphore(f"ew_in{i}") for i in range(4)]
        NW = 4
        w1 = [sb(f"w1_{i}", [P, KC, HID0]) for i in range(NW)]
        w2 = [sb(f"w2_{i}", [P, 2, D]) for i in range(NW)]
        wg = sb("wg", [P, KC, EXP0])
        bg = sb("bg", [P, EXP0])
        b2 = sb("b2", [EXP0, D])
        hT = [sb(f"hT{i}", [P, 2, NP]) for i in range(2)]
        lg = sb("lg", [P, NT, EXP0])
        pr = sb("pr", [P, NT, EXP0])
        sm = sb("sm", [P, 3, NT])
        mx8 = sb("mx8", [P, NT, 8])
        ix8 = sb("ix8", [P, NT, 8], U32)
        ixf = sb("ixf", [P, NT, 8])
        m1, m2 = sb("m1", [P, NT, EXP0]), sb("m2", [P, NT, EXP0])
        comb = sb("comb", [P, NT, EXP0])
        combT = sb("combT", [EXP0, NP])
        bank = [ps(f"bank{i}", [P, D]) for i in range(8)]
        R0, xfT = b.R0, b.xnT
        block = ctx.enter_context(nc.Block())

        @block.sync
        def _(sp):
            sp.dma_start(wg[:, :, :], row_chunks(a["L0_ffn_Wg"])).then_inc(s.g_in, 16)
            sp.dma_start(bg[:, :], bcast(a["L0_ffn_bg"])).then_inc(s.g_in, 16)
            sp.dma_start(b2[:, :], a["L0_ffn_b2"]).then_inc(s.g_in, 16)
            for e in range(EXP0):
                if e >= NW:
                    sp.wait_ge(s.fd_free, 4 + NT * (e - NW + 1))
                sp.dma_start(w1[e % NW][:, :, :], row_chunks(a["L0_ffn_W1"][e])).then_inc(w_in[e % NW], 16)
                sp.dma_start(w2[e % NW][:, :, :], row_chunks(a["L0_ffn_W2"][e])).then_inc(w_in[e % NW], 16)

        @block.tensor
        def _(pe):
            fa = Filler(pe, bank[:3], s.fa, s.fa_free)
            fd = Filler(pe, bank[3:], s.fd, s.fd_free)

            def hidden(e):
                pe.wait_ge(w_in[e % NW], 32 * (e // NW + 1))
                for m in range(2):
                    for c0, cw in CH:
                        dst = fa.take()
                        fa.done(product(nc, dst[:, 0:cw], chunks(w1[e % NW], m * P, P), chunks(xfT, c0, cw)))

            pe.wait_ge(s.g_in, 48)
            dst = fd.take()
            for t in range(NT):
                last = product(nc, dst[:, t * EXP0:(t + 1) * EXP0], tile(xfT, t), chunks(wg, 0, EXP0))
            fd.done(last)
            hidden(0)
            hidden(1)
            pe.wait_ge(s.comb_in, 1)
            dst = [fd.take(), fd.take()]
            for t in range(8):
                last = nc.tensor.transpose(dst[t // 4][:EXP0, (t % 4) * P:(t % 4 + 1) * P], comb[:, t, :], ident)
                if t % 4 == 3:
                    fd.done(last)
            dst = fd.take()
            for t in range(8, NT):
                last = nc.tensor.transpose(dst[:EXP0, (t % 4) * P:(t % 4 + 1) * P], comb[:, t, :], ident)
            fd.done(last)
            pe.wait_ge(s.combT_in, 1)
            for e in range(EXP0):
                i = e % 2
                pe.wait_ge((s.h_in0, s.h_in1)[i], e // 2 + 1)
                for t in range(NT):
                    dst = fd.take()
                    last = product(nc, dst[:, :], tile(hT[i], t), chunks(w2[e % NW]))
                    fd.done(last)
                    if e == EXP0 - 1:
                        dst = fd.take()
                        fd.done(nc.tensor.matmul(dst[:, :], combT[:, t * P:(t + 1) * P], b2[:, :], start=True, stop=True))
                if e + 2 < EXP0:
                    hidden(e + 2)

        @block.scalar
        def _(act):
            full = Emptier(act, bank[:3], s.fa, s.fa_free)
            act.wait_ge(s.lg, 1)
            nc.scalar.activation(pr[:, :, :], lg[:, :, :], ACT.Exp).then_inc(s.exp_s, 1)
            for e in range(EXP0):
                if e >= 2:
                    act.wait_ge(s.fd, 4 + NT * (e - 1))
                for m in range(2):
                    for c0, cw in CH:
                        src = full.take()
                        full.done(nc.scalar.activation(hT[e % 2][:, m, c0:c0 + cw], src[:, 0:cw], ACT.Gelu_apprx_tanh,
                                                       bias=b.cols[:, 12 + 2 * e + m:13 + 2 * e + m]))
                full.all_done()
                act.sem_inc((s.h_in0, s.h_in1)[e % 2], 1)

        @block.vector
        def _(dve):
            v = nc.vector
            link = chain(dve, s.cv)
            full = Emptier(dve, bank[3:], s.fd, s.fd_free)
            each = lambda x: x.unsqueeze(2).broadcast_to([P, NT, EXP0])
            col = lambda x: x.broadcast_to([P, NT, EXP0])
            dve.wait_ge(s.g_in, 48)
            src = full.take()
            full.done(v.tensor_tensor(lg[:, :, :], src[:, 0:NT * EXP0].rearrange("p (t e) -> p t e", t=NT),
                                      bg[:, :].unsqueeze(1).broadcast_to([P, NT, EXP0]), ALU.add))
            full.all_done()
            link(v.tensor_reduce(sm[:, 0, :], lg[:, :, :], AX.X, ALU.max))
            v.tensor_tensor(lg[:, :, :], lg[:, :, :], each(sm[:, 0, :]), ALU.subtract).then_inc(s.lg, 1)
            dve.wait_ge(s.exp_s, 1)
            link(v.tensor_reduce(sm[:, 1, :], pr[:, :, :], AX.X, ALU.add))
            link(v.reciprocal(sm[:, 2, :], sm[:, 1, :]))
            link(v.tensor_tensor(pr[:, :, :], pr[:, :, :], each(sm[:, 2, :]), ALU.mult))
            for t in range(NT):
                last = v.max(mx8[:, t, :], pr[:, t, :])
            link(last)
            for t in range(NT):
                last = v.max_index(ix8[:, t, :], mx8[:, t, :], pr[:, t, :])
            link(last)
            link(v.tensor_copy(ixf[:, :, :], ix8[:, :, :]))
            iota = cst[:, 784:792].unsqueeze(1).broadcast_to([P, NT, EXP0])
            v.tensor_tensor(m1[:, :, :], iota, col(ixf[:, :, 0:1]), ALU.is_equal)
            link(v.tensor_tensor(m2[:, :, :], iota, col(ixf[:, :, 1:2]), ALU.is_equal))
            link(v.tensor_tensor(m1[:, :, :], m1[:, :, :], m2[:, :, :], ALU.add))
            v.tensor_tensor(comb[:, :, :], pr[:, :, :], m1[:, :, :], ALU.mult).then_inc(s.comb_in, 1)
            for i, w in enumerate((4, 4, 2)):
                src = full.take()
                full.done(v.tensor_copy(combT[:, 4 * i * P:(4 * i + w) * P], src[:EXP0, 0:w * P]))
            full.all_done()
            dve.sem_inc(s.combT_in, 1)
            for e in range(EXP0):
                for t in range(NT):
                    if e:
                        dve.wait_ge(s.fd_free, full.n - NT + 1)
                    src = full.take()
                    full.done(v.scalar_tensor_tensor(out=R0[:, t, :], in0=src[:, :], scalar=comb[:, t, e:e + 1],
                                                     in1=R0[:, t, :], op0=ALU.mult, op1=ALU.add))
                    if e == EXP0 - 1:
                        src = full.take()
                        dve.wait_ge(s.fd_free, full.n - 1)
                        full.done(v.tensor_tensor(R0[:, t, :], R0[:, t, :], src[:, :], ALU.add))

def sage(b, top):
    nc, a, cst = b.nc, b.a, b.cst
    ident = cst[:, 0:128]
    with ExitStack() as ctx:
        sb, ps, s = b.tools(ctx, "fa fa_free fd fd_free stats sd scaled xn hn hw hb h1 cv ones_in mid agg x3a")
        w_in = [b.semaphore(f"gw_in{i}") for i in range(2)]
        wl, wr = sb("wl", [P, KC, D]), sb("wr", [P, KC, D])
        vec = sb("vec", [P, 3, D])
        h = sb("h", [P, NT, D])
        aggT, h1T = sb("aggT", [P, KC, NP]), sb("h1T", [P, KC, NP])
        rdeg = sb("rdeg", [P, NT])
        ones = sb("ones", [P, 1])
        norm = Norm(nc, sb, "n")
        bank = [ps(f"bank{i}", [P, D]) for i in range(8)]
        R0, xn, xnT, AT = b.R0, b.vals, b.xnT, b.AT
        VEC = (("L1_gnn_b1l", "L1_gnn_ln1_w", "L1_gnn_ln1_b"), ("L1_gnn_b2l", "L1_gnn_ln2_w", "L1_gnn_ln2_b"))
        block = ctx.enter_context(nc.Block())

        @block.sync
        def _(sp):
            for i in range(2):
                if i:
                    sp.wait_ge(s.h1, NT)
                sp.dma_start(wl[:, :, :], row_chunks(a[f"L1_gnn_W{i + 1}lT"])).then_inc(w_in[i], 16)
                sp.dma_start(wr[:, :, :], row_chunks(a[f"L1_gnn_W{i + 1}rT"])).then_inc(w_in[i], 16)
                for j in range(3):
                    sp.dma_start(vec[:, j, :], bcast(a[VEC[i][j]])).then_inc(w_in[i], 16)

        @block.tensor
        def _(pe):
            fa = Filler(pe, bank[:4], s.fa, s.fa_free)
            fd = Filler(pe, bank[4:], s.fd, s.fd_free)
            for t0, nt in GRP:
                pe.wait_ge(s.xn, t0 + nt)
                for c in range(KC):
                    transposes(nc, fa, xn, ident, t0, nt, c)
            pe.wait_ge(s.ones_in, 1)
            dst = fd.take()
            for t in range(NT):
                last = product(nc, dst[:, t:t + 1], [AT[:, k, t * P:(t + 1) * P] for k in range(NT)], [ones[:, :]] * NT)
            fd.done(last)
            for layer, rows, selfT in ((0, xn, xnT), (1, h, h1T)):
                if layer:
                    for t0, nt in GRP:
                        pe.wait_ge(s.h1, t0 + nt)
                        for c in range(KC):
                            transposes(nc, fa, h, ident, t0, nt, c)
                for m in range(KC):
                    for c0, cw in CH:
                        dst = fa.take()
                        fa.done(product(nc, dst[:, 0:cw], [rows[:, k, m * P:(m + 1) * P] for k in range(NT)],
                                        [AT[:, k, c0:c0 + cw] for k in range(NT)]))
                pe.wait_ge(w_in[layer], 80)
                pe.wait_ge(s.agg, layer + 1)
                for t in range(NT):
                    dst = fd.take()
                    fd.done(product(nc, dst[:, :], tile(aggT, t), chunks(wl)))
                    dst = fd.take()
                    fd.done(product(nc, dst[:, :], tile(selfT, t), chunks(wr)))

        @block.scalar
        def _(act):
            full = Emptier(act, bank[:4], s.fa, s.fa_free)

            def empty_transposes(out):
                for t0, nt in GRP:
                    for c in range(KC):
                        src = full.take()
                        full.done(nc.scalar.activation(out[:, c, t0 * P:(t0 + nt) * P], src[:, 0:nt * P], ACT.Copy))

            norm.root(act, s.stats, 1, s.sd)
            act.wait_ge(s.scaled, 1)
            for t in range(NT):
                norm.apply(xn, R0, t).then_inc(s.xn, 1)
            empty_transposes(xnT)
            for layer in range(2):
                if layer:
                    empty_transposes(h1T)
                for m in range(KC):
                    for c0, cw in CH:
                        src = full.take()
                        full.done(nc.scalar.activation(aggT[:, m, c0:c0 + cw], src[:, 0:cw], ACT.Copy))
                full.all_done()
                act.sem_inc(s.agg, 1)
                norm.root(act, s.stats, layer + 2, s.sd)
                act.wait_ge(s.scaled, layer + 2)
                for t in range(NT):
                    rows = (h, xn)[layer]
                    norm.apply(rows, rows, t).then_inc(s.hn, 1)

        def finish(dve, layer, t):
            dve.wait_ge(s.hb, layer * NT + t + 1)
            if layer == 0:
                nc.vector.scalar_tensor_tensor(out=h[:, t, :], in0=h[:, t, :], scalar=0.0, in1=xn[:, t, :],
                                               op0=ALU.max, op1=ALU.add).then_inc(s.h1, 1)
            else:
                nc.vector.tensor_tensor(R0[:, t, :], R0[:, t, :], xn[:, t, :], ALU.add).then_inc(s.x3a, 1)

        @block.vector
        def _(dve):
            v = nc.vector
            link = chain(dve, s.cv)
            full = Emptier(dve, bank[4:], s.fd, s.fd_free)
            v.memset(ones[:, :], 1.0).then_inc(s.ones_in, 1)
            norm.stats(link, R0, s.stats)
            norm.scales(dve, link, s.sd, 1, s.scaled)
            src = full.take()
            full.done(v.tensor_scalar(rdeg[:, :], src[:, 0:NT], 1.0, None, ALU.max))
            full.all_done()
            link(v.reciprocal(rdeg[:, :], rdeg[:, :]))
            for layer in range(2):
                dve.wait_ge(w_in[layer], 80)
                out = h if layer == 0 else xn
                if layer:
                    dve.wait_ge(s.mid, NT)
                for t in range(NT):
                    src = full.take()
                    full.done(v.scalar_tensor_tensor(out=out[:, t, :], in0=src[:, :], scalar=rdeg[:, t:t + 1], in1=vec[:, 0, :],
                                                     op0=ALU.mult, op1=ALU.add))
                    src = full.take()
                    dve.wait_ge(s.fd_free, full.n - 1)
                    full.done(v.tensor_tensor(out[:, t, :], out[:, t, :], src[:, :], ALU.add))
                full.all_done()
                norm.stats(link, out, s.stats)
                norm.scales(dve, link, s.sd, layer + 2, s.scaled)
                for t in range(NT):
                    dve.wait_ge(s.hn, layer * NT + t + 1)
                    v.tensor_tensor(out[:, t, :], out[:, t, :], vec[:, 1, :], ALU.mult).then_inc(s.hw, 1)
                    if t:
                        finish(dve, layer, t - 1)
                finish(dve, layer, NT - 1)

        @block.gpsimd
        def _(pool):
            for layer in range(2):
                for t in range(NT):
                    out = h if layer == 0 else xn
                    pool.wait_ge(s.hw, layer * NT + t + 1)
                    nc.gpsimd.tensor_tensor(out[:, t, :], out[:, t, :], vec[:, 2, :], ALU.add).then_inc(s.hb, 1)
                if layer == 0:
                    for t in range(NT):
                        pool.wait_ge(s.h1, t + 1)
                        nc.gpsimd.tensor_tensor(R0[:, t, :], R0[:, t, :], h[:, t, :], ALU.add).then_inc(s.mid, 1)


def performer(b, top):
    nc, a, cst = b.nc, b.a, b.cst
    ident = cst[:, 0:128]
    EPS = 1e-4
    NORM = float(HD) ** -0.25
    VW = HD + 1
    with ExitStack() as ctx:
        sb, ps, s = b.tools(ctx, "fa fa_free fd fd_free tq tq_free dq dq_free oq oq_free p_in sq v_in diag_in ones_in "
                                "kbias ek ekp ekf ctx_in qbias eqp qpt orow cv gm o_in bo biased kmx")
        wgt = [sb(f"w{i}", [P, KC, D]) for i in range(2)]
        w_s = [b.semaphore(f"pw_in{i}") for i in range(2)]
        proj = sb("proj", [P, M])
        flat = b.AT[:, :, :].rearrange("p t n -> p (t n)")
        qT = flat[:, 0:KC * NP].rearrange("p (c n) -> p c n", c=KC)
        kT = flat[:, KC * NP:2 * KC * NP].rearrange("p (c n) -> p c n", c=KC)
        sqT = b.vals[:, :, :].rearrange("p t d -> p (t d)").rearrange("p (c n) -> p c n", c=KC)
        v1 = sb("v1", [P, NT, H, VW])
        diag = sb("diag", [P, 2, NT, H])
        kmax = sb("kmax", [P, NT, H])
        qmax = sb("qmax", [P, NT, H])
        kb = sb("kb", [P, NT, H])
        qb = sb("qb", [P, NT, H])
        g1 = sb("g1", [P, 4])
        gr = sb("gr", [1, 4])
        ones = sb("ones", [1, P])
        ef = [sb(f"ef{i}", [P, H, M]) for i in range(2)]
        qpT = [sb(f"qpT{i}", [P, 3, H, P]) for i in range(2)]
        cx = sb("cx", [P, 3, H, VW])
        zeros = sb("zeros", [1, D], BF16)
        rd = sb("rd", [P, NT, H])
        orow = b.xnT[:, :, :].rearrange("p c n -> p (c n)").rearrange("p (t d) -> p t d", t=NT)
        bo = sb("bo", [P, D])
        bank = [ps(f"bank{i}", [P, D]) for i in range(8)]
        R0, xnT = b.R0, b.xnT
        half = lambda x, h, t: x[(h % 2) * HD:(h % 2) * HD + HD, h // 2, t * P:(t + 1) * P]
        valid = lambda t: P if t < NT - 1 else LAST
        PER = 7
        block = ctx.enter_context(nc.Block())


        @block.sync
        def _(sp):
            W = ("L1_mix_Wq", "L1_mix_Wk", "L1_mix_Wv", "L1_mix_Wo")
            for i in range(2):
                sp.dma_start(proj[i * HD:(i + 1) * HD, :], a["L1_mix_projT"]).then_inc(s.p_in, 16)
            sp.dma_start(bo[:, :], bcast(a["L1_mix_bo"])).then_inc(s.bo, 16)
            for i in range(4):
                if i >= 2:
                    sp.wait_ge(s.fa, 12 * (i - 1))
                sp.dma_start(wgt[i % 2][:, :, :], row_chunks(a[W[i]])).then_inc(w_s[i % 2], 16)

        def dash(pe, dst, x, h, t):
            o = (h % 2) * HD
            return nc.tensor.matmul(dst[:, 0:M], half(x, h, t), proj[o:o + HD, :], start=True, stop=True)

        @block.tensor
        def _(pe):
            fa = Filler(pe, bank[:4], s.fa, s.fa_free)
            fd = Filler(pe, bank[4:], s.fd, s.fd_free)
            for i in range(2):
                pe.wait_ge(w_s[i], 16)
                for m in range(KC):
                    for c0, cw in CH:
                        dst = fa.take()
                        fa.done(product(nc, dst[:, 0:cw], chunks(wgt[i], m * P, P), chunks(xnT, c0, cw)))
            for i in range(2):
                pe.wait_ge(s.sq, i + 1)
                dst = fd.take()
                for t in range(NT):
                    for c in range(KC):
                        last = nc.tensor.matmul(dst[:, t * H + 2 * c:t * H + 2 * c + 2], sqT[:, c, t * P:(t + 1) * P],
                                                cst[:, 648:650], start=True, stop=True)
                fd.done(last)
                if i == 0:
                    pe.wait_ge(w_s[0], 32)
                    for t in range(NT):
                        dst = fa.take()
                        fa.done(product(nc, dst[:, :], tile(xnT, t), chunks(wgt[0])))
            pe.wait_ge(s.p_in, 32)
            for t in range(NT):
                for h in range(H):
                    dst = fd.take()
                    fd.done(dash(pe, dst, kT, h, t))
            pe.wait_ge(s.ones_in, 1)
            pe.wait_ge(s.gm, 1)
            dst = fd.take()
            fd.done(nc.tensor.transpose(dst[0:1, 0:P], g1[:, 0:1], ident))
            pe.wait_ge(s.gm, 2)
            dst = fd.take()
            fd.done(nc.tensor.matmul(dst[:, 0:1], ones[:, :], gr[:, 0:1], start=True, stop=True))
            pe.wait_ge(s.kbias, 1)
            pe.wait_ge(s.v_in, 1)
            pe.wait_ge(s.fd_free, fd.n)
            for x in bank[4:]:
                nc.tensor.matmul(x[:, :], zeros[:, 0:P], zeros[:, :], start=True, stop=False, skip_group_check=True)
            for t in range(NT + 1):
                if t < NT:
                    for h in range(H):
                        dst = fa.take()
                        fa.done(dash(pe, dst, kT, h, t))
                if t:
                    u = t - 1
                    pe.wait_ge(s.ekp, u + 1)
                    for h in range(H):
                        for ci, (c0, cw) in enumerate(MC):
                            n = 3 * h + ci
                            last = nc.tensor.matmul(bank[4 + n // PER][:cw, (n % PER) * VW:(n % PER + 1) * VW],
                                                    ef[u % 2][:valid(u), h, c0:c0 + cw], v1[:valid(u), u, h, :],
                                                    start=False, stop=(u == NT - 1), skip_group_check=True)
                    last.then_inc(s.ekf, 1)
            pe.wait_ge(s.ctx_in, 3 * H)
            pe.wait_ge(s.fa_free, fa.n)
            tq = Filler(pe, bank[0:3], s.tq, s.tq_free)
            dq = Filler(pe, bank[4:7], s.dq, s.dq_free)
            oq = Filler(pe, [bank[3], bank[7]], s.oq, s.oq_free)
            for t in range(NT + 2):
                if t < NT:
                    for h in range(H):
                        dst = dq.take()
                        dq.done(dash(pe, dst, qT, h, t))
                if 1 <= t <= NT:
                    u = t - 1
                    pe.wait_ge(s.eqp, u + 1)
                    for ci, (c0, cw) in enumerate(MC):
                        for h0 in (0, 4):
                            dst = tq.take()
                            for h in range(4):
                                last = nc.tensor.transpose(dst[:cw, h * P:(h + 1) * P], ef[u % 2][:, h0 + h, c0:c0 + cw], ident)
                            tq.done(last)
                if t >= 2:
                    u = t - 2
                    pe.wait_ge(s.qpt, u + 1)
                    for h0 in (0, 4):
                        dst = oq.take()
                        for h in range(h0, h0 + 4):
                            last = product(nc, dst[:, (h - h0) * VW:(h - h0 + 1) * VW],
                                           [qpT[u % 2][:cw, ci, h, :] for ci, (_, cw) in enumerate(MC)],
                                           [cx[:cw, ci, h, :] for ci, (_, cw) in enumerate(MC)])
                        oq.done(last)
            for t0, nt in GRP:
                pe.wait_ge(s.orow, t0 + nt)
                for c in range(KC):
                    transposes(nc, tq, orow, ident, t0, nt, c)
            pe.wait_ge(s.o_in, 1)
            pe.wait_ge(w_s[1], 32)
            for t in range(NT):
                dst = oq.take()
                oq.done(product(nc, dst[:, :], tile(sqT, t), chunks(wgt[1])))

        @block.scalar
        def _(act):
            full = Emptier(act, bank[:4], s.fa, s.fa_free)
            for i, out in enumerate((qT, kT)):
                for m in range(KC):
                    for c0, cw in CH:
                        src = full.take()
                        full.done(nc.scalar.activation(out[:, m, c0:c0 + cw], src[:, 0:cw], ACT.Copy, scale=NORM))
                full.all_done()
                if i:
                    act.wait_ge(s.diag_in, 1)
                nc.scalar.activation(sqT[:, :, :], out, ACT.Square).then_inc(s.sq, 1)
            for t in range(NT):
                src = full.take()
                full.done(nc.scalar.activation(v1[:, t, :, 0:HD], src[:, :].rearrange("p (h d) -> p h d", h=H), ACT.Copy))
            full.all_done()
            act.sem_inc(s.v_in, 1)
            act.wait_ge(s.kbias, 1)
            for t in range(NT):
                if t >= 2:
                    act.wait_ge(s.ekf, t - 1)
                for h in range(H):
                    src = full.take()
                    full.done(nc.scalar.activation(ef[t % 2][:valid(t), h, :], src[:valid(t), 0:M], ACT.Exp,
                                                   bias=kb[:valid(t), t, h:h + 1]))
                full.all_done()
                act.sem_inc(s.ek, 1)
            act.wait_ge(s.ekf, NT)
            for n in range(3 * H):
                h, ci = n // 3, n % 3
                cw = MC[ci][1]
                nc.scalar.activation(cx[:cw, ci, h, :], bank[4 + n // PER][:cw, (n % PER) * VW:(n % PER + 1) * VW],
                                     ACT.Copy).then_inc(s.ctx_in, 1)
            tq = Emptier(act, bank[0:3], s.tq, s.tq_free)
            for t in range(NT + 1):
                if t < NT:
                    if t >= 2:
                        act.wait_ge(s.tq, 6 * (t - 1))
                    for h in range(H):
                        n = t * H + h
                        act.wait_ge(s.qbias, n + 1)
                        nc.scalar.activation(ef[t % 2][:, h, :], bank[4 + n % 3][:, 0:M], ACT.Exp,
                                             bias=qb[:, t, h:h + 1]).then_inc(s.dq_free, 1)
                if t:
                    u = t - 1
                    if u >= 2:
                        act.wait_ge(s.oq, 2 * (u - 1))
                    for ci, (c0, cw) in enumerate(MC):
                        for h0 in (0, 4):
                            src = tq.take()
                            tq.done(nc.scalar.activation(qpT[u % 2][:cw, ci, h0:h0 + 4, :],
                                                         src[:cw, :].rearrange("p (h n) -> p h n", h=4), ACT.Copy))
                    tq.all_done()
                    act.sem_inc(s.qpt, 1)
            for t0, nt in GRP:
                for c in range(KC):
                    src = tq.take()
                    tq.done(nc.scalar.activation(sqT[:, c, t0 * P:(t0 + nt) * P], src[:, 0:nt * P], ACT.Copy))
            tq.all_done()
            act.sem_inc(s.o_in, 1)

        @block.vector
        def _(dve):
            v = nc.vector
            link = chain(dve, s.cv)
            v.memset(ones[:, :], 1.0)
            v.memset(zeros[:, :], 0.0)
            v.memset(v1[:, :, :, HD:VW], 1.0).then_inc(s.ones_in, 1)
            link(v.memset(kmax[:, :, :], -BIG))
            full = Emptier(dve, bank[4:], s.fd, s.fd_free)
            for i in range(2):
                src = full.take()
                full.done(v.tensor_scalar(diag[:, i, :, :], src[:, 0:NT * H].rearrange("p (t h) -> p t h", t=NT), 0.5, None, ALU.mult))
                full.all_done()
                dve.sem_inc(s.diag_in, 1)
            for t in range(NT):
                for h in range(H):
                    src = full.take()
                    full.done(v.tensor_reduce(kmax[:valid(t), t, h:h + 1], src[:valid(t), 0:M], AX.X, ALU.max))
            full.all_done()
            v.tensor_reduce(g1[:, 0:1], kmax[:, :, :], AX.XY, ALU.max).then_inc(s.gm, 1)
            src = full.take()
            full.done(v.tensor_reduce(gr[:, 0:1], src[0:1, 0:P], AX.X, ALU.max))
            full.all_done()
            dve.sem_inc(s.gm, 1)
            src = full.take()
            full.done(v.tensor_copy(g1[:, 1:2], src[:, 0:1]))
            full.all_done()
            v.tensor_scalar(kb[:, :, :], diag[:, 1, :, :], -1.0, g1[:, 1:2], ALU.mult, ALU.subtract).then_inc(s.kbias, 1)
            for t in range(NT):
                dve.wait_ge(s.ek, t + 1)
                v.tensor_scalar_add(ef[t % 2][:valid(t), :, :], ef[t % 2][:valid(t), :, :], EPS).then_inc(s.ekp, 1)

            def bias_of(n):
                t, h = n // H, n % H
                dve.wait_ge(s.kmx, n + 1)
                v.tensor_tensor(qb[:, t, h:h + 1], qmax[:, t, h:h + 1], diag[:, 0, t, h:h + 1], ALU.subtract).then_inc(s.qbias, 1)

            oq = Emptier(dve, [bank[3], bank[7]], s.oq, s.oq_free)
            for t in range(NT + 2):
                if 1 <= t <= NT:
                    dve.wait_ge(s.dq_free, t * H)
                    v.tensor_scalar_add(ef[(t - 1) % 2][:, :, :], ef[(t - 1) % 2][:, :, :], EPS).then_inc(s.eqp, 1)
                if t < NT:
                    for h in range(H):
                        n = t * H + h
                        dve.wait_ge(s.dq, n + 1)
                        v.tensor_reduce(qmax[:, t, h:h + 1], bank[4 + n % 3][:, 0:M], AX.X, ALU.max, negate=True).then_inc(s.kmx, 1)
                        bias_of(n)
                if t >= 2:
                    u = t - 2
                    for h0 in (0, 4):
                        src = oq.take()
                        blocks = src[:, 0:4 * VW].rearrange("p (h w) -> p h w", h=4)
                        link(v.reciprocal(rd[:, u, h0:h0 + 4], blocks[:, :, HD]))
                        oq.done(v.tensor_tensor(orow[:, u, h0 * HD:(h0 + 4) * HD].rearrange("p (h d) -> p h d", h=4), blocks[:, :, 0:HD],
                                                rd[:, u, h0:h0 + 4].unsqueeze(2).broadcast_to([P, 4, HD]), ALU.mult))
                    oq.all_done()
                    dve.sem_inc(s.orow, 1)
            for t in range(NT):
                dve.wait_ge(s.biased, t + 1)
                src = oq.take()
                oq.done(v.tensor_tensor(R0[:, t, :], R0[:, t, :], src[:, :], ALU.add))
            oq.all_done()

        @block.gpsimd
        def _(pool):
            pool.wait_ge(s.bo, 16)
            for t in range(NT):
                nc.gpsimd.tensor_tensor(R0[:, t, :], R0[:, t, :], bo[:, :], ALU.add).then_inc(s.biased, 1)


def expert1(b, top):
    nc, a, cst = b.nc, b.a, b.cst
    ident = cst[:, 0:128]
    with ExitStack() as ctx:
        sb, ps, s = b.tools(ctx, "fa fa_free fd fd_free g_in stats sd scaled xf xfT_in mean sc ex idx we_in be_in gate "
                                "y cv out_s")
        wg, bg = sb("wg", [P, KC, EXP1]), sb("bg", [1, EXP1])
        we, be = sb("we", [P, KC, D]), sb("be", [P, D])
        mean = sb("mean", [P, KC])
        sc = sb("sc", [1, 4, EXP1])
        mx8, ix8 = sb("mx8", [1, 8]), sb("ix8", [1, 8], U32)
        gate = sb("gate", [P, 1])
        ones = sb("ones", [1, P])
        y = sb("y", [P, NT, D])
        norm = Norm(nc, sb, "n")
        bank = [ps(f"bank{i}", [P, D]) for i in range(8)]
        R0, xfT, xf = b.R0, b.xnT, b.vals
        block = ctx.enter_context(nc.Block())

        @block.sync
        def _(sp):
            sp.dma_start(wg[:, :, :], row_chunks(a["L1_ffn_Wg"])).then_inc(s.g_in, 16)
            sp.dma_start(bg[:, :], bcast(a["L1_ffn_bg"], 1)).then_inc(s.g_in, 16)
            sp.wait_ge(s.idx, 1)
            e = sp.value_load(ix8[0:1, 0:1], min_val=0, max_val=EXP1 - 1)
            w = a["L1_ffn_We"].rearrange("e (c p) n -> p e c n", p=P)
            for c in range(KC):
                sp.dma_start(we[:, c, :], w[:, bass.ds(e, 1), c, :]).then_inc(s.we_in, 16)
            sp.dma_start(be[:, :], a["L1_ffn_be"][bass.ds(e, 1), :].broadcast_to([P, D])).then_inc(s.be_in, 16)
            for t in range(NT):
                sp.wait_ge(s.y, t + 1)
                rows = P if t < NT - 1 else LAST
                sp.dma_start(b.out[t * P:t * P + rows, :], y[:rows, t, :]).then_inc(s.out_s, 16)
            sp.wait_ge(s.out_s, 16 * NT)

        @block.tensor
        def _(pe):
            fa = Filler(pe, bank[:4], s.fa, s.fa_free)
            fd = Filler(pe, bank[4:], s.fd, s.fd_free)
            for t0, nt in GRP:
                pe.wait_ge(s.xf, t0 + nt)
                for c in range(KC):
                    transposes(nc, fa, xf, ident, t0, nt, c)
            pe.wait_ge(s.mean, 1)
            pe.wait_ge(s.g_in, 32)
            dst = fd.take()
            fd.done(product(nc, dst[0:1, 0:EXP1], [mean[:, c:c + 1] for c in range(KC)], chunks(wg, 0, EXP1)))
            pe.wait_ge(s.gate, 1)
            dst = fd.take()
            fd.done(nc.tensor.matmul(dst[:, 0:1], ones[:, :], mx8[0:1, 0:1], start=True, stop=True))
            pe.wait_ge(s.we_in, 16 * KC)
            for t in range(NT):
                dst = fd.take()
                fd.done(product(nc, dst[:, :], tile(xfT, t), chunks(we)))

        @block.scalar
        def _(act):
            full = Emptier(act, bank[:4], s.fa, s.fa_free)
            norm.root(act, s.stats, 1, s.sd)
            act.wait_ge(s.scaled, 1)
            for t in range(NT):
                norm.apply(xf, R0, t).then_inc(s.xf, 1)
            for t0, nt in GRP:
                for c in range(KC):
                    src = full.take()
                    full.done(nc.scalar.activation(xfT[:, c, t0 * P:(t0 + nt) * P], src[:, 0:nt * P], ACT.Copy))
            full.all_done()
            act.sem_inc(s.xfT_in, 1)
            act.wait_ge(s.sc, 1)
            nc.scalar.activation(sc[:, 1, :], sc[:, 0, :], ACT.Exp).then_inc(s.ex, 1)

        @block.vector
        def _(dve):
            v = nc.vector
            link = chain(dve, s.cv)
            full = Emptier(dve, bank[4:], s.fd, s.fd_free)
            v.memset(ones[:, :], 1.0)
            norm.stats(link, R0, s.stats)
            norm.scales(dve, link, s.sd, 1, s.scaled)
            dve.wait_ge(s.xfT_in, 1)
            link(v.tensor_reduce(mean[:, :], xfT[:, :, 0:N], AX.X, ALU.add))
            v.tensor_scalar(mean[:, :], mean[:, :], 1.0 / N, None, ALU.mult).then_inc(s.mean, 1)
            src = full.take()
            full.done(v.tensor_tensor(sc[:, 0, :], src[0:1, 0:EXP1], bg[:, :], ALU.add))
            full.all_done()
            link(v.tensor_reduce(sc[:, 2, 0:1], sc[:, 0, :], AX.X, ALU.max, negate=True))
            v.tensor_scalar(sc[:, 0, :], sc[:, 0, :], sc[:, 2, 0:1], None, ALU.add).then_inc(s.sc, 1)
            dve.wait_ge(s.ex, 1)
            link(v.tensor_reduce(sc[:, 2, 1:2], sc[:, 1, :], AX.X, ALU.add))
            link(v.reciprocal(sc[:, 2, 2:3], sc[:, 2, 1:2]))
            link(v.tensor_scalar(sc[:, 3, :], sc[:, 1, :], sc[:, 2, 2:3], None, ALU.mult))
            link(v.max(mx8[:, :], sc[:, 3, :]))
            v.max_index(ix8[:, :], mx8[:, :], sc[:, 3, :]).then_inc(s.idx, 1)
            dve.sem_inc(s.gate, 1)
            src = full.take()
            full.done(v.tensor_copy(gate[:, :], src[:, 0:1]))
            full.all_done()
            dve.wait_ge(s.be_in, 16)
            for t in range(NT):
                src = full.take()
                full.done(v.tensor_tensor(y[:, t, :], src[:, :], be[:, :], ALU.add))
                full.all_done()
                v.scalar_tensor_tensor(out=y[:, t, :], in0=y[:, t, :], scalar=gate[:, 0:1], in1=R0[:, t, :],
                                       op0=ALU.mult, op1=ALU.add).then_inc(s.y, 1)


_INS = ["x", "src", "dst", "edge_attr_8"] + ["L0_gnn_" + n for n in ("ln_g", "ln_b", "Wq", "bq", "Wk", "bk", "Wv", "bv", "W1", "b1", "W2", "b2")] \
    + ["L0_mix_WqkvT", "L0_mix_WoutT", "L0_mix_bout"] + ["L0_ffn_" + n for n in ("Wg", "bg", "W1", "b1", "W2", "b2")] \
    + ["L1_gnn_" + n for n in ("W1lT", "b1l", "W1rT", "W2lT", "b2l", "W2rT", "ln1_w", "ln1_b", "ln2_w", "ln2_b")] \
    + ["L1_mix_" + n for n in ("Wq", "Wk", "Wv", "Wo", "bo", "projT")] + ["L1_ffn_" + n for n in ("Wg", "bg", "We", "be")]


def lay_out(inputs):
    arrays = {}
    for name in _INS:
        if name.endswith("T") and name not in inputs:
            arrays[name] = np.ascontiguousarray(np.asarray(inputs[name[:-1]]).T)
        else:
            arrays[name] = np.ascontiguousarray(inputs[name])
    arrays["c_cols"] = np.ascontiguousarray(np.concatenate(
        [np.asarray(inputs[n]).reshape(-1, P) for n in ("L0_gnn_ln_g", "L0_gnn_ln_b", "L0_gnn_b1", "L0_ffn_b1")]).T)
    arrays["c_cst"], arrays["c_iota"] = constants()
    return arrays


def build_program(nc, a, out, stages=99):
    with ExitStack() as top:
        b = Build(nc, a, out)
        for stage in STAGES[:stages]:
            stage(b, top)
    return b


STAGES = [prepare, linear_attention, edge_scores, edge_softmax, edge_sums, attention_out, experts0, sage, performer, expert1]


def kernel(**inputs):
    import concourse.bacc as bacc
    from concourse.bass_utils import run_bass_kernel_spmd

    nc = bacc.Bacc("TRN2", target_bir_lowering=False, num_devices=1)
    arrays = lay_out(inputs)
    a = {n: nc.dram_tensor("in_" + n, v.shape, mybir.dt.from_np(v.dtype), kind="ExternalInput").ap() for n, v in arrays.items()}
    out = nc.dram_tensor("out_rows", (N, D), F32, kind="ExternalOutput").ap()
    build_program(nc, a, out)
    r = run_bass_kernel_spmd(nc, [{"in_" + n: v for n, v in arrays.items()}], core_ids=[0])
    return r.results[0]["out_rows"]
```

```python
from collections import namedtuple
from contextlib import ExitStack

import concourse.bass as bass
from concourse import mybir
import numpy as np

P = 128
N = 1250
D = 512
E = 20000
H = 8
HD = D // H
NT = 10
NP = NT * P
LAST = N - (NT - 1) * P
KC = D // P
GRP = [(0, 4), (4, 4), (8, 2)]
CH = [(0, 512), (512, 512), (1024, 256)]
EP = 125
ET = E // EP
ST = 176
RW = 12
HI, LO = 40, 32
M = 266
MC = [(0, 128), (128, 128), (256, 10)]
EXP0, HID0 = 8, 256
EXP1 = 16
SCALE = float(HD) ** -0.5
BIG = 1.0e30
LN_EPS = 1e-5

F32 = mybir.dt.float32
F32R = mybir.dt.float32r
BF16 = mybir.dt.bfloat16
F16 = mybir.dt.float16
I32 = mybir.dt.int32
U32 = mybir.dt.uint32
ALU = mybir.AluOpType
ACT = mybir.ActivationFunctionType
AX = mybir.AxisListType


def constants():
    i = np.arange(P)
    c = np.zeros((P, 1056), np.float32)
    c[:, 0:128] = np.eye(P)
    c[:, 128:256] = i[None, :]
    c[:, 256:256 + HI] = np.arange(HI)
    c[:, 256 + HI:256 + HI + LO] = np.arange(LO)
    h = np.arange(HI)
    c[:HI, 384:424] = (h[:, None] // 4 == h[None, :] // 4) & (h[:, None] < h[None, :])
    c[:HI, 424:464] = h[:, None] // 4 == h[None, :] // 4
    c[:HI, 464:504] = (h[:, None] % 4 == 0) & (h[:, None] // 4 < h[None, :] // 4)
    b = np.arange(11)
    c[:HI, 504:515] = (h[:, None] % 4 == 0) & (h[:, None] // 4 < b[None, :])
    c[:, 520:648] = i[None, :] < i[:, None]
    c[:, 648:650] = (i[:, None] // HD) == np.arange(2)[None, :]
    c[:, 656:784] = (i[:, None] // HD) == (i[None, :] // HD)
    c[:, 784:792] = np.arange(8)
    c[:8, 792 + 128:792 + 136] = np.eye(8)
    return c, np.broadcast_to(np.arange(NP, dtype=np.float16), (P, NP)).copy()


class Build:

    def __init__(self, nc, a, out):
        self.nc, self.a, self.out, self.stage = nc, a, out, 0
        self.where = {}

    def over(self, name, new, shape, dt=F32, words=0):
        return self.nc.alloc_sbuf_tensor_at(f"s{self.stage}_{new}", shape, dt, offset=self.where[name] + 4 * words)

    def tools(self, ctx, sems):
        nc = self.nc
        self.stage = n = self.stage + 1

        def sb(name, shape, dt=F32):
            self.where[name] = -(-nc.sbuf_base // 32) * 32
            return ctx.enter_context(nc.sbuf_tensor(f"s{n}_{name}", shape, dt))

        ps = lambda name, shape, dt=F32: ctx.enter_context(nc.psum_tensor(f"s{n}_{name}", shape, dt))
        self.held = held = []
        ctx.callback(self.clear, held)
        s = namedtuple("Semaphores", sems)(*[self.semaphore(f"{n}_{self.stage}") for n in sems.split()])
        return sb, ps, s

    def clear(self, held):
        if held:
            self.nc.clear_and_free_semaphores(held)
            self.nc.all_engine_barrier()

    def semaphore(self, name):
        self.held.append(self.nc.alloc_semaphore(name))
        return self.held[-1]


def chain(eng, sem):
    n = [0]

    def link(ins):
        n[0] += 1
        ins.then_inc(sem, 1)
        eng.wait_ge(sem, n[0])
    return link


class Filler:

    def __init__(self, pe, banks, full, free):
        self.pe, self.banks, self.full, self.free, self.n = pe, banks, full, free, 0

    def take(self):
        n, k = self.n, len(self.banks)
        self.n += 1
        if n >= k:
            self.pe.wait_ge(self.free, n - k + 1)
        return self.banks[n % k]

    def done(self, ins):
        ins.then_inc(self.full, 1)


class Emptier:

    def __init__(self, eng, banks, full, free):
        self.eng, self.banks, self.full, self.free, self.n = eng, banks, full, free, 0

    def take(self):
        self.n += 1
        self.eng.wait_ge(self.full, self.n)
        return self.banks[(self.n - 1) % len(self.banks)]

    def done(self, ins):
        ins.then_inc(self.free, 1)

    def all_done(self):
        self.eng.wait_ge(self.free, self.n)


def product(nc, dst, lhs, rhs, first=True, last=True):
    for i, (x, y) in enumerate(zip(lhs, rhs)):
        ins = nc.tensor.matmul(dst, x, y, start=first and i == 0, stop=last and i == len(lhs) - 1)
    return ins


def product3(nc, dst, lh, ll, rh, rl):
    return product(nc, dst, lh + ll + lh, rh + rh + rl)


def tile(x, t):
    return [x[:, c, t * P:(t + 1) * P] for c in range(x.shape[1])]


def chunks(w, c0=0, cw=D):
    return [w[:, c, c0:c0 + cw] for c in range(w.shape[1])]


def transposes(nc, fill, rows, ident, t0, nt, c):
    dst = fill.take()
    for t in range(nt):
        last = nc.tensor.transpose(dst[:, t * P:(t + 1) * P], rows[:, t0 + t, c * P:(c + 1) * P], ident)
    fill.done(last)


class Norm:

    def __init__(self, nc, sb, name):
        self.nc = nc
        self.st, self.mv, self.ln = sb(name + "_st", [P, NT, 6]), sb(name + "_mv", [P, NT, 2]), sb(name + "_ln", [P, 3, NT])

    def stats(self, link, rows, stats_sem):
        v = self.nc.vector
        for t in range(NT):
            last = v.bn_stats(self.st[:, t, :], rows[:, t, :])
        link(last)
        for t in range(NT):
            last = v.bn_aggr(self.mv[:, t, :], self.st[:, t, :])
        link(last)
        v.tensor_scalar_add(self.ln[:, 0, :], self.mv[:, :, 1], LN_EPS).then_inc(stats_sem, 1)

    def root(self, act, stats_sem, n, sd_sem):
        act.wait_ge(stats_sem, n)
        self.nc.scalar.activation(self.ln[:, 0, :], self.ln[:, 0, :], ACT.Sqrt).then_inc(sd_sem, 1)

    def scales(self, dve, link, sd_sem, n, ready_sem):
        v, ln = self.nc.vector, self.ln
        dve.wait_ge(sd_sem, n)
        link(v.reciprocal(ln[:, 1, :], ln[:, 0, :]))
        v.scalar_tensor_tensor(out=ln[:, 2, :], in0=self.mv[:, :, 0], scalar=-1.0, in1=ln[:, 1, :],
                               op0=ALU.mult, op1=ALU.mult).then_inc(ready_sem, 1)

    def apply(self, out, rows, t):
        return self.nc.scalar.activation(out[:, t, :], rows[:, t, :], ACT.Identity, scale=self.ln[:, 1, t:t + 1],
                                         bias=self.ln[:, 2, t:t + 1])


class RowNorm:

    def __init__(self, nc, sb, name, stats_sem, sd_sem, ready_sem):
        self.nc, self.stats_sem, self.sd_sem, self.ready_sem = nc, stats_sem, sd_sem, ready_sem
        self.st, self.mv, self.ln = sb(name + "_st", [P, 4, 6]), sb(name + "_mv", [P, 4, 2]), sb(name + "_ln", [P, 4, 4])

    def stats(self, dve, link, rows, n):
        v, k = self.nc.vector, n % 4
        link(v.bn_stats(self.st[:, k, :], rows))
        link(v.bn_aggr(self.mv[:, k, :], self.st[:, k, :]))
        v.tensor_scalar_add(self.ln[:, k, 0:1], self.mv[:, k, 1:2], LN_EPS).then_inc(self.stats_sem, 1)

    def root(self, act, n):
        act.wait_ge(self.stats_sem, n + 1)
        self.nc.scalar.activation(self.ln[:, n % 4, 1:2], self.ln[:, n % 4, 0:1], ACT.Sqrt).then_inc(self.sd_sem, 1)

    def scales(self, dve, link, n):
        v, k, ln = self.nc.vector, n % 4, self.ln
        dve.wait_ge(self.sd_sem, n + 1)
        link(v.reciprocal(ln[:, k, 2:3], ln[:, k, 1:2]))
        v.scalar_tensor_tensor(out=ln[:, k, 3:4], in0=self.mv[:, k, 0:1], scalar=-1.0, in1=ln[:, k, 2:3],
                               op0=ALU.mult, op1=ALU.mult).then_inc(self.ready_sem, 1)

    def apply(self, act, out, rows, n):
        act.wait_ge(self.ready_sem, n + 1)
        return self.nc.scalar.activation(out, rows, ACT.Identity, scale=self.ln[:, n % 4, 2:3], bias=self.ln[:, n % 4, 3:4])


def row_chunks(w):
    return w.rearrange("(c p) n -> p c n", p=P)


def bcast(v, parts=P):
    return v.rearrange("(a n) -> a n", a=1).broadcast_to([parts, v.shape[0]])


def prepare(b, top):
    nc, a = b.nc, b.a
    psb, _, _ = b.tools(top, "")
    b.cst = psb("cst", [P, 1056])
    b.iota_h = psb("iota_h", [P, NP], F16)
    b.starts = psb("starts", [1, 16], I32)
    b.cols = psb("cols", [P, 28])
    b.R0 = psb("R0", [P, NT, D])
    b.xnT = psb("xnT", [P, KC, NP])
    b.q_dram = nc.dram_tensor("q_dram", (NP, D), F32).ap()
    b.k_dram = nc.dram_tensor("k_dram", (NP, D), F32).ap()
    b.v_dram = nc.dram_tensor("v_dram", (NP, D), F32).ap()
    b.rec_dram = nc.dram_tensor("rec_dram", (P * ST, RW), F32).ap()
    cst = b.cst
    ident = cst[:, 0:128]

    with ExitStack() as ctx:
        sb, ps, s = b.tools(ctx, "cst_in x_in ids_in ew_in gb_in zeroed stats sd rs xn added xn2 tp tp_free onehot "
                                "chain_v chain_p counted offs_ps based pairs mm mm_free ids rec_ready pad_ready "
                                "pad_out scattered kv_sb identb_in")
        w_in = [b.semaphore(f"w_in{i}") for i in range(3)]
        kv_out = [b.semaphore(f"kv_out{i}") for i in range(4)]
        oh_reg = sb("xn_rows", [P, ET * (HI + LO) // 2])
        xn = oh_reg[:, 0:NT * D].rearrange("p (t d) -> p t d", t=NT)
        oh = oh_reg[:, :].bitcast(BF16).rearrange("p (t j) -> p t j", t=ET)
        xn2_reg = sb("xn2_rows", [P, NT * D])
        xn2 = xn2_reg[:, :].rearrange("p (t d) -> p t d", t=NT)
        cum = xn2_reg[:HI, 0:LO * ET].rearrange("p (l t) -> p l t", l=LO)
        xnormT = sb("xnormT", [P, KC, NP])
        ohT = sb("ohT", [HI + LO, ET, EP], BF16)
        hist = sb("hist", [HI, LO, ET], BF16)
        base_hi = sb("base_hi", [HI, LO, ET], BF16)
        w = [sb(f"w{i}", [P, KC, D]) for i in range(2)]
        rec = sb("rec", [EP, ET, RW])
        bias = sb("bias", [P, 2, D])
        st = sb("st", [P, NT, 6])
        mv = sb("mv", [P, NT, 2])
        ln = sb("ln", [P, 3, NT])
        identb = sb("identb", [P, P], BF16)
        ids_i = sb("ids_i", [EP, 2, ET], I32)
        hilo = sb("hilo", [EP, 2, ET], I32)
        lof = sb("lof", [EP, ET])
        tmp_i = sb("tmp_i", [EP, ET], I32)
        off = sb("off", [HI, 4])
        off_i = sb("off_i", [HI, 2], I32)
        rank = sb("rank", [EP, ET])
        basev = sb("basev", [EP, ET])
        rowid = sb("rowid", [EP, ET], I32)
        pos = sb("pos", [EP, 3, 16], I32)
        pad = sb("pad", [P, ST // 4, RW])
        kvs = oh_reg[:, 0:4 * D].rearrange("p (j d) -> p j d", j=4)
        bank = [ps(f"bank{i}", [P, D]) for i in range(8)]
        FULL = (NT - 1) * P
        PROJ = [("L0_gnn_Wk", "L0_gnn_bk", b.k_dram), ("L0_gnn_Wv", "L0_gnn_bv", b.v_dram),
                ("L0_gnn_Wq", "L0_gnn_bq", b.q_dram)]
        MAGIC = 1.5 * 2.0 ** 23 * 256

        block = ctx.enter_context(nc.Block())

        def store(sp, i, j):
            n = i * NT + j
            sp.wait_ge(s.kv_sb, n + 1)
            sp.dma_start(PROJ[i][2][j * P:(j + 1) * P, :], kvs[:, n % 4, :]).then_inc(kv_out[n % 4], 16)

        @block.sync
        def _(sp):
            sp.dma_start(cst[:, :], a["c_cst"]).then_inc(s.cst_in, 16)
            sp.dma_start(b.iota_h[:, :], a["c_iota"]).then_inc(s.cst_in, 16)
            sp.dma_start(b.R0[:, 0:NT - 1, :], a["x"][0:FULL].rearrange("(t p) d -> p t d", p=P)).then_inc(s.x_in, 16)
            sp.wait_ge(s.zeroed, 1)
            sp.dma_start(b.R0[0:LAST, NT - 1, :], a["x"][FULL:N]).then_inc(s.x_in, 16)
            sp.dma_start(ids_i[:, 0, :], a["src"].rearrange("(p t) -> p t", p=EP)).then_inc(s.ids_in, 16)
            sp.dma_start(ids_i[:, 1, :], a["dst"].rearrange("(p t) -> p t", p=EP)).then_inc(s.ids_in, 16)
            sp.dma_start(b.cols[:, :], a["c_cols"]).then_inc(s.gb_in, 16)
            for i, (wn, bn, _) in enumerate(PROJ):
                if i == 2:
                    sp.wait_ge(s.kv_sb, NT)
                sp.dma_start(w[i % 2][:, :, :], row_chunks(a[wn])).then_inc(w_in[i], 16)
                sp.dma_start(bias[:, i % 2, :], bcast(a[bn])).then_inc(w_in[i], 16)
                if i == 0:
                    sp.dma_start(rec[:, :, 4:RW], a["edge_attr_8"].rearrange("(p t) h -> p t h", p=EP)).then_inc(s.ew_in, 16)
                if i == 1:
                    sp.wait_ge(s.pad_ready, 1)
                    for j in range(4):
                        sp.dma_start(b.rec_dram.rearrange("(p t) w -> p t w", p=P)[:, j * ST // 4:(j + 1) * ST // 4, :],
                                     pad[:, :, :]).then_inc(s.pad_out, 16)
                    for j in range(NT):
                        store(sp, 0, j)
            for i in (1, 2):
                for j in range(NT):
                    store(sp, i, j)
            for i in range(4):
                sp.wait_ge(kv_out[i], 16 * len(range(i, 3 * NT, 4)))

        @block.gpsimd
        def _(pool):
            link = chain(pool, s.chain_p)
            link(nc.gpsimd.memset(pad[:, :, :], 0.0))
            for j in (0, 3):
                last = nc.gpsimd.memset(pad[:, :, j:j + 1], -1.0)
            last.then_inc(s.pad_ready, 1)
            for t in range(NT):
                pool.wait_ge(s.xn, t + 1)
                nc.gpsimd.tensor_tensor(b.R0[:, t, :], b.R0[:, t, :], xn[:, t, :], ALU.add).then_inc(s.added, 1)
            pool.wait_ge(s.rec_ready, 1)
            pool.wait_ge(s.ew_in, 16)
            pool.wait_ge(s.pad_out, 64)
            for t in range(ET):
                if t % 16 == 0:
                    pool.wait_ge(s.ids, t // 16 + 1)
                nc.gpsimd.indirect_dma_start(
                    out=b.rec_dram, out_offset=bass.IndirectOffsetOnAxis(ap=rowid[:, t:t + 1], axis=0),
                    in_=rec[:, t, :], in_offset=None).then_inc(s.scattered, 16)
            pool.wait_ge(s.scattered, 16 * ET)

        @block.scalar
        def _(act):
            def sqrt_var(n):
                act.wait_ge(s.stats, n)
                nc.scalar.activation(ln[:, 0, :], ln[:, 0, :], ACT.Sqrt).then_inc(s.sd, 1)

            sqrt_var(1)
            act.wait_ge(s.rs, 1)
            for t in range(NT):
                nc.scalar.activation(xn[:, t, :], b.R0[:, t, :], ACT.Identity, scale=ln[:, 1, t:t + 1],
                                     bias=ln[:, 2, t:t + 1]).then_inc(s.xn, 1)
            sqrt_var(2)
            n = 0
            act.wait_ge(s.gb_in, 16)
            for which in range(2):
                for t0, nt in GRP:
                    for c in range(KC):
                        act.wait_ge(s.tp, n + 1)
                        cols = slice(t0 * P, (t0 + nt) * P)
                        if which == 0:
                            ins = nc.scalar.activation(b.xnT[:, c, cols], bank[n % 4][:, 0:nt * P], ACT.Copy)
                        else:
                            ins = nc.scalar.activation(xnormT[:, c, cols], bank[n % 4][:, 0:nt * P], ACT.Identity,
                                                       scale=b.cols[:, c:c + 1], bias=b.cols[:, KC + c:KC + c + 1])
                        ins.then_inc(s.tp_free, 1)
                        n += 1
            for g in range(ET // 8):
                act.wait_ge(s.tp, n + 1)
                nc.scalar.activation(ohT[:, 8 * g:8 * g + 8, :],
                                     bank[n % 4][:, :].bitcast(BF16)[:HI + LO, :].rearrange("p (t e) -> p t e", t=8)[:, :, 0:EP],
                                     ACT.Copy).then_inc(s.tp_free, 1)
                n += 1
            for g in range(ET // 16):
                act.wait_ge(s.tp, n + 1)
                nc.scalar.activation(hist[:, :, 16 * g:16 * g + 16],
                                     bank[n % 4][:HI, :].rearrange("p (t l) -> p l t", t=16),
                                     ACT.Copy).then_inc(s.tp_free, 1)
                n += 1

        @block.vector
        def _(dve):
            link = chain(dve, s.chain_v)
            nc.vector.memset(b.R0[96:P, NT - 1, :], 0.0).then_inc(s.zeroed, 1)
            dve.wait_ge(s.cst_in, 32)
            nc.vector.tensor_copy(identb[:, :], ident).then_inc(s.identb_in, 1)

            def stats(rows, wait):
                for t in range(NT):
                    wait(t)
                    last = nc.vector.bn_stats(st[:, t, :], rows[:, t, :])
                link(last)
                for t in range(NT):
                    last = nc.vector.bn_aggr(mv[:, t, :], st[:, t, :])
                link(last)
                nc.vector.tensor_scalar_add(ln[:, 0, :], mv[:, :, 1], LN_EPS).then_inc(s.stats, 1)

            def scales(n):
                dve.wait_ge(s.sd, n)
                link(nc.vector.reciprocal(ln[:, 1, :], ln[:, 0, :]))
                link(nc.vector.scalar_tensor_tensor(out=ln[:, 2, :], in0=mv[:, :, 0], scalar=-1.0, in1=ln[:, 1, :],
                                                    op0=ALU.mult, op1=ALU.mult))

            stats(b.R0, lambda t: dve.wait_ge(s.x_in, 32) if t == 0 else None)
            scales(1)
            nc.vector.engine_nop().then_inc(s.rs, 1)
            stats(xn, lambda t: dve.wait_ge(s.xn, t + 1))
            scales(2)
            for t in range(NT):
                nc.vector.tensor_scalar(xn2[:, t, :], xn[:, t, :], ln[:, 1, t:t + 1], ln[:, 2, t:t + 1],
                                        ALU.mult, ALU.add).then_inc(s.xn2, 1)
            dve.wait_ge(s.ids_in, 32)
            nc.vector.tensor_scalar(hilo[:, 0, :], ids_i[:, 0, :], 5, None, ALU.logical_shift_right)
            nc.vector.tensor_scalar(tmp_i[:, :], ids_i[:, 0, :], P - 1, None, ALU.bitwise_and)
            link(nc.vector.tensor_scalar(hilo[:, 1, :], ids_i[:, 0, :], LO - 1, None, ALU.bitwise_and))
            nc.vector.tensor_copy(lof[:, :], hilo[:, 1, :])
            nc.vector.tensor_copy(rec[:, :, 0], tmp_i[:, :])
            nc.vector.tensor_copy(rec[:, :, 1], ids_i[:, 1, :])
            nc.vector.tensor_copy(rec[:, :, 2].bitcast(I32), ids_i[:, 1, :])
            nc.vector.tensor_copy(rec[:, :, 3], ids_i[:, 0, :]).then_inc(s.rec_ready, 1)
            dve.wait_ge(s.tp_free, 24)
            dve.wait_ge(s.added, NT)
            nc.vector.tensor_tensor(oh[:EP, :, 0:HI], hilo[:, 0, :].unsqueeze(2).broadcast_to([EP, ET, HI]),
                                    cst[:EP, 256:256 + HI].unsqueeze(1).broadcast_to([EP, ET, HI]), ALU.is_equal)
            nc.vector.tensor_tensor(oh[:EP, :, HI:], hilo[:, 1, :].unsqueeze(2).broadcast_to([EP, ET, LO]),
                                    cst[:EP, 256 + HI:256 + HI + LO].unsqueeze(1).broadcast_to([EP, ET, LO]),
                                    ALU.is_equal).then_inc(s.onehot, 1)
            dve.wait_ge(s.tp_free, 24 + ET // 8 + ET // 16)
            link(nc.vector.tensor_tensor_scan(cum.rearrange("p l t -> p (l t)"), hist[:, :, :].rearrange("p l t -> p (l t)"),
                                              hist[:, :, :].rearrange("p l t -> p (l t)"), 0.0, ALU.add, ALU.max))
            link(nc.vector.tensor_copy(off[:, 0:1], cum[:, LO - 1, ET - 1:ET]))
            nc.vector.engine_nop().then_inc(s.counted, 1)
            dve.wait_ge(s.offs_ps, 1)
            link(nc.vector.tensor_copy(off[:, 1:3], bank[4][:HI, 0:2]))
            link(nc.vector.tensor_scalar(off_i[:, 0:1], off[:, 2:3], 255.0, None, ALU.add))
            link(nc.vector.tensor_scalar(off_i[:, 1:2], off_i[:, 0:1], 8, None, ALU.logical_shift_right))
            nc.vector.tensor_scalar(off[:, 3:4], off_i[:, 1:2], 1.0, None, ALU.max).then_inc(s.pairs, 1)
            dve.wait_ge(s.offs_ps, 2)
            link(nc.vector.tensor_copy(b.starts[0:1, 0:11], bank[4][0:1, 16:27]))
            link(nc.vector.tensor_scalar(b.starts[0:1, 12:13], b.starts[0:1, 10:11], 1.0, None, ALU.add))
            link(nc.vector.tensor_scalar(b.starts[0:1, 11:12], b.starts[0:1, 12:13], 1, None, ALU.logical_shift_right))
            link(nc.vector.tensor_scalar(b.starts[0:1, 10:11], b.starts[0:1, 11:12], 2.0, None, ALU.mult))
            link(nc.vector.scalar_tensor_tensor(out=off[:, 2:3], in0=bank[4][:HI, 8:9], scalar=256.0, in1=off[:, 1:2],
                                                op0=ALU.mult, op1=ALU.add))
            link(nc.vector.scalar_tensor_tensor(out=cum, in0=cum, scalar=off[:, 2:3], in1=hist[:, :, :],
                                                op0=ALU.add, op1=ALU.subtract))
            link(nc.vector.tensor_scalar(base_hi[:, :, :], cum, MAGIC, -MAGIC, ALU.add, ALU.add))
            nc.vector.tensor_tensor(hist[:, :, :], cum, base_hi[:, :, :], ALU.subtract).then_inc(s.based, 1)

            n = 0
            for g in range(ET // 16):
                for q in range(4):
                    dve.wait_ge(s.mm, n + 1)
                    for i in range(4):
                        t = 16 * g + 4 * q + i
                        last = nc.vector.scalar_tensor_tensor(
                            out=bank[4 + n % 4][:EP, i * EP:(i + 1) * EP], in0=bank[4 + n % 4][:EP, i * EP:(i + 1) * EP], scalar=1.5,
                            in1=cst[:EP, 520:520 + EP], op0=ALU.is_ge, op1=ALU.mult, accum_out=rank[:, t:t + 1])
                    last.then_inc(s.mm_free, 1)
                    n += 1
                dve.wait_ge(s.mm, n + 1)
                for i in range(16):
                    t = 16 * g + i
                    last = nc.vector.scalar_tensor_tensor(
                        out=bank[4 + n % 4][:EP, i * LO:(i + 1) * LO], in0=cst[:EP, 256 + HI:256 + HI + LO], scalar=lof[:, t:t + 1],
                        in1=bank[4 + n % 4][:EP, i * LO:(i + 1) * LO], op0=ALU.is_equal, op1=ALU.mult,
                        accum_out=basev[:, t:t + 1])
                last.then_inc(s.mm_free, 1)
                n += 1
                dve.wait_ge(s.mm_free, n)
                sl = slice(16 * g, 16 * g + 16)
                link(nc.vector.tensor_tensor(pos[:, 0, :], basev[:, sl], rank[:, sl], ALU.add))
                nc.vector.tensor_scalar(pos[:, 1, :], pos[:, 0, :], 7, None, ALU.logical_shift_right)
                link(nc.vector.tensor_scalar(pos[:, 2, :], pos[:, 0, :], P - 1, None, ALU.bitwise_and))
                nc.vector.scalar_tensor_tensor(out=rowid[:, sl], in0=pos[:, 2, :], scalar=float(ST), in1=pos[:, 1, :],
                                               op0=ALU.mult, op1=ALU.add).then_inc(s.ids, 1)
                for j in range(3 * g, 3 * g + 3):
                    dve.wait_ge(s.mm, n + 1)
                    if j % NT == 0:
                        dve.wait_ge(w_in[j // NT], 32)
                    if j >= 4:
                        dve.wait_ge(kv_out[j % 4], 16 * (j // 4))
                    nc.vector.tensor_tensor(kvs[:, j % 4, :], bank[4 + n % 4][:, :], bias[:, (j // NT) % 2, :],
                                            ALU.add).then_inc(s.kv_sb, 1)
                    n += 1
                    dve.wait_ge(s.kv_sb, j + 1)
                    nc.vector.engine_nop().then_inc(s.mm_free, 1)

        @block.tensor
        def _(pe):
            pe.wait_ge(s.cst_in, 32)
            n = 0
            for which in range(2):
                for t0, nt in GRP:
                    pe.wait_ge((s.xn, s.xn2)[which], t0 + nt)
                    for c in range(KC):
                        if n >= 4:
                            pe.wait_ge(s.tp_free, n - 3)
                        for t in range(nt):
                            last = nc.tensor.transpose(bank[n % 4][:, t * P:(t + 1) * P],
                                                       (xn, xn2)[which][:, t0 + t, c * P:(c + 1) * P], ident)
                        last.then_inc(s.tp, 1)
                        n += 1
            pe.wait_ge(s.onehot, 1)
            pe.wait_ge(s.identb_in, 1)
            for g in range(ET // 8):
                pe.wait_ge(s.tp_free, n - 3)
                for i in range(8):
                    last = nc.tensor.transpose(bank[n % 4][:, :].bitcast(BF16)[:HI + LO, i * P:i * P + EP],
                                               oh[:EP, 8 * g + i, :], identb[:EP, :EP])
                last.then_inc(s.tp, 1)
                n += 1
            for g in range(ET // 16):
                pe.wait_ge(s.tp_free, n - 3)
                for i in range(16):
                    last = nc.tensor.matmul(bank[n % 4][:HI, i * LO:(i + 1) * LO], oh[:EP, 16 * g + i, 0:HI],
                                            oh[:EP, 16 * g + i, HI:], start=True, stop=True)
                last.then_inc(s.tp, 1)
                n += 1
            pe.wait_ge(s.counted, 1)
            nc.tensor.matmul(bank[4][:HI, 0:1], cst[:HI, 384:424], off[:, 0:1], start=True, stop=True)
            nc.tensor.matmul(bank[4][:HI, 1:2], cst[:HI, 424:464], off[:, 0:1], start=True, stop=True).then_inc(s.offs_ps, 1)
            pe.wait_ge(s.pairs, 1)
            nc.tensor.matmul(bank[4][:HI, 8:9], cst[:HI, 464:504], off[:, 3:4], start=True, stop=True)
            nc.tensor.matmul(bank[4][0:1, 16:27], off[:, 3:4], cst[:HI, 504:515], start=True, stop=True).then_inc(s.offs_ps, 1)
            pe.wait_ge(s.based, 1)

            n = 0

            def free(n):
                if n >= 4:
                    pe.wait_ge(s.mm_free, n - 3)

            for g in range(ET // 16):
                for q in range(4):
                    free(n)
                    for i in range(4):
                        t = 16 * g + 4 * q + i
                        last = nc.tensor.matmul(bank[4 + n % 4][:EP, i * EP:(i + 1) * EP], ohT[:, t, :], ohT[:, t, :],
                                                start=True, stop=True)
                    last.then_inc(s.mm, 1)
                    n += 1
                free(n)
                for i in range(16):
                    t = 16 * g + i
                    out = bank[4 + n % 4][:EP, i * LO:(i + 1) * LO]
                    nc.tensor.matmul(out, ohT[:HI, t, :], base_hi[:, :, t], start=True, stop=False)
                    last = nc.tensor.matmul(out, ohT[:HI, t, :], hist[:, :, t], start=False, stop=True)
                last.then_inc(s.mm, 1)
                n += 1
                for j in range(3 * g, 3 * g + 3):
                    free(n)
                    if j % NT == 0:
                        pe.wait_ge(w_in[j // NT], 32)
                    t = j % NT
                    for c in range(KC):
                        last = nc.tensor.matmul(bank[4 + n % 4][:, :], xnormT[:, c, t * P:(t + 1) * P],
                                                w[(j // NT) % 2][:, c, :], start=(c == 0), stop=(c == KC - 1))
                    last.then_inc(s.mm, 1)
                    n += 1



def linear_attention(b, top):
    nc, a, cst = b.nc, b.a, b.cst
    ident = cst[:, 0:128]
    with ExitStack() as ctx:
        sb, ps, s = b.tools(ctx, "fa fa_free fd fd_free kmax kexp qsub qexp qn v_in krow qT_in ctx_in cv ca")
        w_in = [b.semaphore(f"mw_in{i}") for i in range(3)]
        w = [sb(f"w{i}", [P, KC, D]) for i in range(3)]
        kT = sb("kT", [P, KC, NP])
        q = sb("q", [P, NT, D])
        v = sb("v", [P, NT, D])
        krow = sb("krow", [P, NT, D])
        qT = sb("qT", [P, KC, NP])
        nmax = sb("nmax", [P, KC])
        ksum = sb("ksum", [P, KC])
        rsum = sb("rsum", [P, KC])
        hm = sb("hm", [P, NT, 3, H])
        cx = sb("cx", [P, KC, P])
        bank = [ps(f"bank{i}", [P, D]) for i in range(8)]
        block = ctx.enter_context(nc.Block())

        @block.sync
        def _(sp):
            for i in (1, 0, 2):
                sp.dma_start(w[i][:, :, :], row_chunks(a["L0_mix_WqkvT"])[:, :, i * D:(i + 1) * D]).then_inc(w_in[i], 16)

        @block.tensor
        def _(pe):
            na, nd = [0], [0]

            def fill_a():
                n = na[0]
                na[0] += 1
                if n >= 4:
                    pe.wait_ge(s.fa_free, n - 3)
                return bank[n % 4]

            def fill_d():
                n = nd[0]
                nd[0] += 1
                if n >= 4:
                    pe.wait_ge(s.fd_free, n - 3)
                return bank[4 + n % 4]

            def rows(dst, wi, t, sem):
                for c in range(KC):
                    last = nc.tensor.matmul(dst[:, :], b.xnT[:, c, t * P:(t + 1) * P], w[wi][:, c, :], start=(c == 0), stop=(c == KC - 1))
                last.then_inc(sem, 1)

            pe.wait_ge(w_in[1], 16)
            for m in range(KC):
                for c0, cw in CH:
                    dst = fill_a()
                    for c in range(KC):
                        last = nc.tensor.matmul(dst[:, 0:cw], w[1][:, c, m * P:(m + 1) * P], b.xnT[:, c, c0:c0 + cw],
                                                start=(c == 0), stop=(c == KC - 1))
                    last.then_inc(s.fa, 1)
            pe.wait_ge(w_in[0], 16)
            pe.wait_ge(w_in[2], 16)
            for t in range(NT):
                rows(fill_d(), 0, t, s.fd)
                rows(fill_a(), 2, t, s.fa)
            for m in range(KC):
                pe.wait_ge(s.kexp, m + 1)
                for t0, nt in GRP:
                    dst = fill_a()
                    for t in range(nt):
                        last = nc.tensor.transpose(dst[:, t * P:(t + 1) * P], kT[:, m, (t0 + t) * P:(t0 + t + 1) * P], ident)
                    last.then_inc(s.fa, 1)
            for t0, nt in GRP:
                pe.wait_ge(s.qn, t0 + nt)
                for m in range(KC):
                    dst = fill_a()
                    for t in range(nt):
                        last = nc.tensor.transpose(dst[:, t * P:(t + 1) * P], q[:, t0 + t, m * P:(m + 1) * P], ident)
                    last.then_inc(s.fa, 1)
            pe.wait_ge(s.v_in, NT)
            pe.wait_ge(s.krow, 3 * KC)
            for m in range(KC):
                dst = fill_d()
                for t in range(NT):
                    last = nc.tensor.matmul(dst[:, 0:P], krow[:, t, m * P:(m + 1) * P], v[:, t, m * P:(m + 1) * P],
                                            start=(t == 0), stop=(t == NT - 1))
                last.then_inc(s.fd, 1)
            pe.wait_ge(s.qT_in, 3 * KC)
            for m in range(KC):
                pe.wait_ge(s.ctx_in, m + 1)
                for c0, cw in CH:
                    dst = fill_a()
                    nc.tensor.matmul(dst[:, 0:cw], cx[:, m, :], qT[:, m, c0:c0 + cw], start=True, stop=True).then_inc(s.fa, 1)

        @block.scalar
        def _(act):
            n = [0]

            def empty(out, shape, sem):
                act.wait_ge(s.fa, n[0] + 1)
                src = bank[n[0] % 4][:, 0:shape]
                if len(out.shape) == 3:
                    src = src.rearrange("p (t d) -> p t d", d=out.shape[2])
                n[0] += 1
                nc.scalar.activation(out, src, ACT.Copy).then_inc(s.fa_free, 1)

            link = chain(act, s.ca)
            for m in range(KC):
                for c0, cw in CH:
                    empty(kT[:, m, c0:c0 + cw], cw, None)
            for m in range(KC):
                act.wait_ge(s.kmax, m + 1)
                nc.scalar.activation(kT[:, m, 0:N], kT[:, m, 0:N], ACT.Exp, bias=nmax[:, m:m + 1],
                                     accum_out=ksum[:, m:m + 1]).then_inc(s.kexp, 1)
            for t in range(NT):
                act.wait_ge(s.qsub, t + 1)
                nc.scalar.activation(q[:, t, :], q[:, t, :], ACT.Exp).then_inc(s.qexp, 1)
                empty(v[:, t, :], D, None)
            act.wait_ge(s.fa_free, n[0])
            act.sem_inc(s.v_in, NT)
            for m in range(KC):
                for t0, nt in GRP:
                    empty(krow[:, t0:t0 + nt, m * P:(m + 1) * P], nt * P, None)
            act.wait_ge(s.fa_free, n[0])
            act.sem_inc(s.krow, 3 * KC)
            for t0, nt in GRP:
                for m in range(KC):
                    empty(qT[:, m, t0 * P:(t0 + nt) * P], nt * P, None)
            act.wait_ge(s.fa_free, n[0])
            act.sem_inc(s.qT_in, 3 * KC)
            for m in range(KC):
                for c0, cw in CH:
                    empty(b.xnT[:, m, c0:c0 + cw], cw, None)
            act.wait_ge(s.fa_free, n[0])

        @block.vector
        def _(dve):
            link = chain(dve, s.cv)
            for m in range(KC):
                dve.wait_ge(s.fa_free, 3 * (m + 1))
                nc.vector.memset(kT[:, m, N:NP], 0.0)
                nc.vector.tensor_reduce(nmax[:, m:m + 1], kT[:, m, 0:N], AX.X, ALU.max, negate=True).then_inc(s.kmax, 1)
            heads = lambda x: x.rearrange("p (h d) -> p h d", h=H)
            each = lambda x: x.unsqueeze(2).broadcast_to([P, H, HD])

            def normalise(t):
                dve.wait_ge(s.qexp, t + 1)
                link(nc.vector.tensor_reduce(hm[:, t, 1, :], heads(q[:, t, :]), AX.X, ALU.add))
                link(nc.vector.reciprocal(hm[:, t, 2, :], hm[:, t, 1, :]))
                nc.vector.tensor_tensor(heads(q[:, t, :]), heads(q[:, t, :]), each(hm[:, t, 2, :]), ALU.mult).then_inc(s.qn, 1)

            for t in range(NT):
                dve.wait_ge(s.fd, t + 1)
                link(nc.vector.tensor_reduce(hm[:, t, 0, :], heads(bank[4 + t % 4][:, :]), AX.X, ALU.max))
                nc.vector.tensor_tensor(heads(q[:, t, :]), heads(bank[4 + t % 4][:, :]), each(hm[:, t, 0, :]),
                                        ALU.subtract).then_inc(s.qsub, 1)
                dve.wait_ge(s.qsub, t + 1)
                dve.sem_inc(s.fd_free, 1)
                if t:
                    normalise(t - 1)
            normalise(NT - 1)
            dve.wait_ge(s.kexp, KC)
            link(nc.vector.reciprocal(rsum[:, :], ksum[:, :]))
            for m in range(KC):
                dve.wait_ge(s.fd, NT + m + 1)
                nc.vector.scalar_tensor_tensor(out=cx[:, m, :], in0=bank[4 + (NT + m) % 4][:, 0:P], scalar=rsum[:, m:m + 1],
                                               in1=cst[:, 656:784], op0=ALU.mult, op1=ALU.mult).then_inc(s.ctx_in, 1)


def bounds(b, eng, cols):
    return [eng.value_load(b.starts[0:1, j:j + 1], min_val=0 if j == 0 else 1, max_val=ST // (4 if j == 11 else 2))
            for j in cols]


def edge_scores(b, top):
    nc = b.nc
    psb, _, _ = b.tools(top, "")
    b.AT = psb("AT", [P, NT, NP], F32R)
    b.AT_dram = nc.dram_tensor("AT_dram", (P, NT, NP), F32).ap()
    b.deg = psb("deg", [P, NT])
    b.few = psb("few", [1, 1], I32)
    b.vals = psb("vals", [P, NT, D])
    b.den = psb("den", [P, NT, H])
    b.mid = top.enter_context(ExitStack())
    psb, _, _ = b.tools(b.mid, "")
    b.recs = psb("recs", [P, ST + 4, RW])
    b.W = psb("W", [P, ST, H])
    with ExitStack() as ctx:
        sb, ps, s = b.tools(ctx, "loaded zeroed oh0 oh1 tp0 tp1 ohT0 ohT1 qe0 qe1 prod0 prod1 red chain_p issued")
        arrived = [b.semaphore(f"k_in{i}") for i in range(4)]
        q_rows = sb("q_rows", [P, NT, D])
        ohf = [sb(f"ohf{i}", [P, P]) for i in range(2)]
        ohT = [sb(f"ohT_{i}", [P, P]) for i in range(2)]
        prod = [sb(f"prod{i}", [P, D]) for i in range(2)]
        kbuf = [sb(f"kbuf{i}", [P, D]) for i in range(4)]
        idx = [sb(f"idx{i}", [P, 1], I32) for i in range(4)]
        psT = [ps(f"psT{i}", [P, P]) for i in range(2)]
        psQ = [ps(f"psQ{i}", [P, D]) for i in range(2)]
        oh_s, tp, ohT_s, qe, prod_s = (s.oh0, s.oh1), (s.tp0, s.tp1), (s.ohT0, s.ohT1), (s.qe0, s.qe1), (s.prod0, s.prod1)
        recs, W = b.recs, b.W
        block = ctx.enter_context(nc.Block())

        @block.sync
        def _(sp):
            sp.dma_start(recs[:, 0:ST, :], b.rec_dram.rearrange("(p t) w -> p t w", p=P)).then_inc(s.loaded, 16)
            sp.dma_start(q_rows[:, :, :], b.q_dram.rearrange("(t p) d -> p t d", p=P)).then_inc(s.loaded, 16)


        @block.gpsimd
        def _(pool):
            pool.wait_ge(s.loaded, 32)
            pool.wait_ge(s.zeroed, 2)
            twos, = bounds(b, pool, (11,))
            with pool.Fori(0, twos) as v:
                for k in range(4):
                    pool.wait_ge(prod_s[k % 2], v * 2 + (k // 2 + 1))
                    nc.gpsimd.tensor_copy(idx[k][:, :], recs[:, bass.ds(v * 4 + k, 1), 2].bitcast(I32)).then_inc(s.chain_p, 1)
                    pool.wait_ge(s.chain_p, v * 4 + (k + 1))
                    pool.sem_inc(s.issued, 1)
                    nc.gpsimd.indirect_dma_start(out=kbuf[k][:, :], out_offset=None, in_=b.k_dram,
                                                 in_offset=bass.IndirectOffsetOnAxis(ap=idx[k][:, :], axis=0)
                                                 ).then_inc(arrived[k], 16)

        @block.scalar
        def _(act):
            twos, = bounds(b, act, (11,))
            with act.Fori(0, twos) as v:
                for k in range(4):
                    i = k % 2
                    act.wait_ge(tp[i], v * 2 + (k // 2 + 1))
                    act.wait_ge(qe[i], v * 2 + (k // 2 + 1))
                    nc.scalar.activation(ohT[i][:, :], psT[i][:, :], ACT.Copy).then_inc(ohT_s[i], 1)

        @block.vector
        def _(dve):
            nc.vector.memset(W[:, :, :], 0.0).then_inc(s.zeroed, 1)
            nc.vector.memset(recs[:, ST:ST + 4, :], 0.0).then_inc(s.zeroed, 1)
            dve.wait_ge(s.zeroed, 2)
            dve.wait_ge(s.loaded, 32)
            dve.sem_inc(s.prod0, 2)
            dve.sem_inc(s.prod1, 2)

            def one_hot(i, t):
                nc.vector.tensor_scalar(ohf[i][:, :], b.cst[:, 128:256], recs[:, t, 0], None,
                                        ALU.is_equal).then_inc(oh_s[i], 1)

            for i in range(2):
                one_hot(i, slice(i, i + 1))
            twos, = bounds(b, dve, (11,))
            with dve.Fori(0, twos) as v:
                for h in range(2):
                    for i in range(2):
                        dve.wait_ge(tp[i], v * 2 + (h + 1))
                        one_hot(i, bass.ds(v * 4 + (2 * h + 2 + i), 1))
                    for i in range(2):
                        dve.wait_ge(qe[i], v * 2 + (h + 2))
                        dve.wait_ge(arrived[2 * h + i], v * 16 + 16)
                        nc.vector.tensor_tensor(prod[i][:, :], psQ[i][:, :], kbuf[2 * h + i][:, :],
                                                ALU.mult).then_inc(prod_s[i], 1)
                    for i in range(2):
                        dve.wait_ge(prod_s[i], v * 2 + (h + 3))
                        nc.vector.tensor_reduce(W[:, bass.ds(v * 4 + (2 * h + i), 1), :],
                                                prod[i][:, :].rearrange("p (h d) -> p h d", h=H), AX.X,
                                                ALU.add).then_inc(s.red, 1)
                    dve.wait_ge(s.red, v * 4 + (2 * h + 2))

        @block.tensor
        def _(pe):
            pe.wait_ge(s.loaded, 32)
            pe.sem_inc(s.qe0, 1)
            pe.sem_inc(s.qe1, 1)
            at = bounds(b, pe, range(11))
            for j in range(NT):
                with pe.Fori(at[j], at[j + 1]) as u:
                    for i in range(2):
                        pe.wait_ge(oh_s[i], u + 1)
                        nc.tensor.transpose(psT[i][:, :], ohf[i][:, :], b.cst[:, 0:128]).then_inc(tp[i], 1)
                    for i in range(2):
                        pe.wait_ge(ohT_s[i], u + 1)
                        pe.wait_ge(prod_s[i], u + 2)
                        nc.tensor.matmul(psQ[i][:, :], ohT[i][:, :], q_rows[:, j, :], start=True,
                                         stop=True).then_inc(qe[i], 1)


def edge_softmax(b, top):
    nc, cst = b.nc, b.cst
    G = ST // 16
    with ExitStack() as ctx:
        sb, ps, s = b.tools(ctx, "c srep_s tpw tps evac sel selc back evc tb fin")
        srep = sb("srep", [P, ST, H])
        Wt = sb("Wt", [P, G * P])
        Ft = sb("Ft", [P, G, P])
        Fs = sb("Fs", [P, G * P + 4])
        B = sb("B", [P, G, P])
        T = sb("T", [P, G, P])
        X = sb("X", [P, 4, G])
        Y = sb("Y", [H, 4, G * 16 + 2])
        nf = sb("nf", [H, ST])
        cf = sb("cf", [H, ST + 2])
        mc = sb("mc", [H, ST])
        UV = sb("UV", [H, 2, ST + 2])
        LR = sb("LR", [H, 2, ST])
        LRb = sb("LRb", [P, 2, G])
        bank = [ps(f"sb{i}", [P, D]) for i in range(8)]
        W, recs = b.W, b.recs
        ident = cst[:, 0:128]
        flat = lambda x: x[:, :, :].rearrange("p g e -> p (g e)")
        block = ctx.enter_context(nc.Block())

        @block.vector
        def _(dve):
            link = chain(dve, s.c)
            v = nc.vector
            v.tensor_copy(srep[:, :, :], recs[:, 0:ST, 3].unsqueeze(2).broadcast_to([P, ST, H])).then_inc(s.srep_s, 1)
            v.scalar_tensor_tensor(out=W[:, :, :], in0=W[:, :, :], scalar=SCALE, in1=recs[:, 0:ST, 4:RW],
                                   op0=ALU.mult, op1=ALU.mult).then_inc(s.srep_s, 1)
            v.memset(Fs[:, :], -BIG)
            v.memset(Y[:, :, :], -1.0)
            v.memset(cf[:, :], -BIG)
            link(v.memset(UV[:, :, :], -BIG))
            dve.wait_ge(s.evac, 6)
            link(v.tensor_tensor(T[:, :, 1:P], Ft[:, :, 1:P], Ft[:, :, 0:P - 1], ALU.not_equal))
            link(v.tensor_scalar(Fs[:, 0:G * P].rearrange("p (g e) -> p g e", g=G)[:, :, 1:P], T[:, :, 1:P], -BIG, None, ALU.mult))
            link(v.tensor_tensor_scan(flat(T), Fs[:, 0:G * P], Wt[:, :], -BIG, ALU.add, ALU.max))
            link(v.tensor_tensor_scan(flat(B)[:, ::-1], Fs[:, 1:G * P + 1][:, ::-1], flat(T)[:, ::-1], -BIG, ALU.add, ALU.max))
            v.tensor_copy(X[:, 0, :], B[:, :, 0])
            v.tensor_copy(X[:, 1, :], B[:, :, P - 1])
            v.tensor_copy(X[:, 2, :], Ft[:, :, 0])
            v.tensor_copy(X[:, 3, :], Ft[:, :, P - 1]).then_inc(s.sel, 1)
            dve.wait_ge(s.selc, 1)
            link(v.tensor_copy(Y[:, 0:2, 0:ST].rearrange("h q (g t) -> h q g t", t=16),
                               bank[0][:H, 0:16 * 2 * G].rearrange("h (t q g) -> h q g t", t=16, q=2)))
            link(v.tensor_copy(Y[:, 2:4, 0:ST].rearrange("h q (g t) -> h q g t", t=16),
                               bank[1][:H, 0:16 * 2 * G].rearrange("h (t q g) -> h q g t", t=16, q=2)))
            link(v.tensor_tensor(nf[:, :], Y[:, 2, 0:ST], Y[:, 3, 0:ST], ALU.not_equal))
            link(v.tensor_tensor(mc[:, 1:ST], Y[:, 2, 1:ST], Y[:, 3, 0:ST - 1], ALU.not_equal))
            link(v.tensor_scalar(cf[:, 1:ST], mc[:, 1:ST], -BIG, None, ALU.mult))
            link(v.scalar_tensor_tensor(out=mc[:, :], in0=nf[:, :], scalar=-BIG, in1=cf[:, 0:ST], op0=ALU.mult, op1=ALU.add))
            link(v.tensor_tensor_scan(UV[:, 0, 1:ST + 1], mc[:, :], Y[:, 1, 0:ST], -BIG, ALU.add, ALU.max))
            link(v.scalar_tensor_tensor(out=mc[:, :], in0=nf[:, :], scalar=-BIG, in1=cf[:, 1:ST + 1], op0=ALU.mult, op1=ALU.add))
            link(v.tensor_tensor_scan(UV[:, 1, 0:ST][:, ::-1], mc[:, ::-1], Y[:, 0, 0:ST][:, ::-1], -BIG, ALU.add, ALU.max))
            v.tensor_tensor(LR[:, 0, :], UV[:, 0, 0:ST], cf[:, 0:ST], ALU.add)
            v.tensor_tensor(LR[:, 1, :], UV[:, 1, 1:ST + 1], cf[:, 1:ST + 1], ALU.add).then_inc(s.back, 1)
            dve.wait_ge(s.evc, 1)
            link(v.tensor_copy(LRb[:, :, :], bank[2][:, 0:2 * G].rearrange("p (q g) -> p q g", q=2)))
            for q, e in ((0, 0), (1, P - 1)):
                link(v.tensor_tensor(T[:, :, :], Ft[:, :, :], Ft[:, :, e:e + 1].broadcast_to([P, G, P]), ALU.not_equal))
                link(v.scalar_tensor_tensor(out=T[:, :, :], in0=T[:, :, :], scalar=-BIG,
                                            in1=LRb[:, q, :].unsqueeze(2).broadcast_to([P, G, P]), op0=ALU.mult, op1=ALU.add))
                link(v.tensor_tensor(B[:, :, :], B[:, :, :], T[:, :, :], ALU.max))
            v.engine_nop().then_inc(s.tb, 1)
            for n in range(3):
                g0, g1 = 4 * n, min(4 * n + 4, G)
                dve.wait_ge(s.fin, n + 1)
                last = v.tensor_tensor(W[:, 16 * g0:16 * g1, :], W[:, 16 * g0:16 * g1, :],
                                       bank[3 + n][:, 0:(g1 - g0) * P].rearrange("p (t h) -> p t h", h=H), ALU.subtract)
            link(last)
            v.engine_nop().then_inc(s.evac, 1)

        @block.tensor
        def _(pe):
            for which, src in ((0, srep), (1, W)):
                pe.wait_ge(s.srep_s, which + 1)
                for n in range(3):
                    for g in range(4 * n, min(4 * n + 4, G)):
                        last = nc.tensor.transpose(bank[3 * which + n][:, (g - 4 * n) * P:(g - 4 * n + 1) * P],
                                                   src[:, 16 * g:16 * g + 16, :].rearrange("p t h -> p (t h)"), ident)
                    last.then_inc(s.tps, 1)
            pe.wait_ge(s.sel, 1)
            for q in range(2):
                for t in range(16):
                    last = nc.tensor.matmul(bank[q][:H, t * 2 * G:(t + 1) * 2 * G], ident[:, 8 * t:8 * t + 8],
                                            X[:, 2 * q:2 * q + 2, :].rearrange("p q g -> p (q g)"), start=True, stop=True)
            last.then_inc(s.selc, 1)
            pe.wait_ge(s.back, 1)
            for q in range(2):
                for t in range(16):
                    last = nc.tensor.matmul(bank[2][:, q * G:(q + 1) * G], cst[:H, 792 + 128 - 8 * t:792 + 256 - 8 * t],
                                            LR[:, q, :].rearrange("h (g t) -> h t g", t=16)[:, t, :],
                                            start=(t == 0), stop=(t == 15))
            last.then_inc(s.evc, 1)
            pe.wait_ge(s.tb, 1)
            for n in range(3):
                for g in range(4 * n, min(4 * n + 4, G)):
                    last = nc.tensor.transpose(bank[3 + n][:, (g - 4 * n) * P:(g - 4 * n + 1) * P], B[:, g, :], ident)
                last.then_inc(s.fin, 1)

        @block.scalar
        def _(act):
            for which, dst in ((0, flat(Ft)), (1, Wt)):
                for n in range(3):
                    w = (min(4 * n + 4, G) - 4 * n) * P
                    act.wait_ge(s.tps, 3 * which + n + 1)
                    nc.scalar.activation(dst[:, 4 * n * P:4 * n * P + w], bank[3 * which + n][:, 0:w], ACT.Copy).then_inc(s.evac, 1)
            act.wait_ge(s.evac, 7)
            nc.scalar.activation(W[:, :, :], W[:, :, :], ACT.Exp).then_inc(s.tpw, 1)
            act.wait_ge(s.tpw, 1)


def edge_sums(b, top):
    nc = b.nc
    with ExitStack() as ctx:
        sb, ps, s = b.tools(ctx, "zeroed made0 made1 oh0 oh1 used0 used1 summed kept chain_p issued counts rounded stored degd deg_ps deg_in cv")
        arrived = [b.semaphore(f"v_in{i}") for i in range(4)]
        made, used, oh_s = (s.made0, s.made1), (s.used0, s.used1), (s.oh0, s.oh1)
        ohf = [sb(f"ohf{i}", [P, P]) for i in range(2)]
        ohb = [sb(f"ohb{i}", [P, P], BF16) for i in range(2)]
        ohd = [sb(f"ohd{i}", [P, NP], BF16) for i in range(2)]
        ew = [sb(f"ew{i}", [P, H]) for i in range(2)]
        vw = [sb(f"vw{i}", [P, D]) for i in range(2)]
        vbuf = [sb(f"vbuf{i}", [P, D]) for i in range(4)]
        idx = [sb(f"vidx{i}", [P, 1], I32) for i in range(4)]
        zeros = sb("zeros", [1, D], BF16)
        ones = sb("ones", [P, 1])
        A32 = [sb(f"A32_{i}", [P, NP]) for i in range(2)]
        deg_row = sb("deg_row", [1, NP])
        most = sb("most", [1, 1])
        pV = ps("pV", [P, D])
        pD = ps("pD", [P, H])
        pA = [ps(f"pA{i}", [P, D]) for i in range(3)]
        pG = [ps(f"pG{i}", [P, D]) for i in range(3)]
        recs, W = b.recs, b.W
        block = ctx.enter_context(nc.Block())


        @block.sync
        def _(sp):
            for j in range(NT):
                sp.wait_ge(s.counts, 3 * (j + 1))
                sp.dma_start(b.AT_dram[:, j, :], A32[j % 2][:, :]).then_inc(s.stored, 16)
                sp.wait_ge(s.stored, 16 * (j + 1))

        @block.gpsimd
        def _(pool):
            twos, = bounds(b, pool, (11,))
            with pool.Fori(0, twos) as v:
                for k in range(4):
                    pool.wait_ge(used[k % 2], v * 2 + (k // 2 + 1))
                    nc.gpsimd.tensor_copy(idx[k][:, :], recs[:, bass.ds(v * 4 + k, 1), 2].bitcast(I32)).then_inc(s.chain_p, 1)
                    pool.wait_ge(s.chain_p, v * 4 + (k + 1))
                    pool.sem_inc(s.issued, 1)
                    nc.gpsimd.indirect_dma_start(out=vbuf[k][:, :], out_offset=None, in_=b.v_dram,
                                                 in_offset=bass.IndirectOffsetOnAxis(ap=idx[k][:, :], axis=0)
                                                 ).then_inc(arrived[k], 16)

        @block.vector
        def _(dve):
            nc.vector.memset(ones[:, :], 1.0).then_inc(s.zeroed, 1)
            nc.vector.memset(zeros[:, :], 0.0).then_inc(s.zeroed, 1)
            dve.sem_inc(s.used0, 2)
            dve.sem_inc(s.used1, 2)
            twos, = bounds(b, dve, (11,))
            with dve.Fori(0, twos) as v:
                for k in range(4):
                    i, h = k % 2, k // 2
                    t = bass.ds(v * 4 + k, 1)
                    dve.wait_ge(used[i], v * 2 + (h + 2))
                    nc.vector.tensor_scalar(ohf[i][:, :], b.cst[:, 128:256], recs[:, t, 0], None, ALU.is_equal)
                    nc.vector.tensor_scalar(ohb[i][:, :], b.iota_h[:, 0:P], recs[:, t, 0], None, ALU.is_equal)
                    nc.vector.tensor_scalar(ohd[i][:, :], b.iota_h[:, :], recs[:, t, 1], None, ALU.is_equal)
                    nc.vector.tensor_copy(ew[i][:, :].unsqueeze(1), W[:, t, :]).then_inc(oh_s[i], 1)
                    dve.wait_ge(arrived[k], v * 16 + 16)
                    nc.vector.tensor_tensor(vw[i][:, :].rearrange("p (h d) -> p h d", h=H),
                                            vbuf[k][:, :].rearrange("p (h d) -> p h d", h=H),
                                            W[:, t, :].rearrange("p t h -> p (t h)").unsqueeze(2).broadcast_to([P, H, HD]),
                                            ALU.mult).then_inc(made[i], 1)
            link = chain(dve, s.cv)
            dve.wait_ge(s.deg_ps, 1)
            for (c0, cw), src in zip(CH, pG):
                last = nc.vector.tensor_copy(deg_row[:, c0:c0 + cw], src[0:1, 0:cw])
            last.then_inc(s.deg_in, 1)
            dve.wait_ge(s.deg_in, 1)
            link(nc.vector.tensor_reduce(most[:, :], deg_row[:, :], AX.X, ALU.max))
            link(nc.vector.tensor_scalar(b.few[:, :], most[:, :], 4096.0, None, ALU.is_le))
            dve.wait_ge(s.deg_ps, 2)
            link(nc.vector.tensor_copy(b.deg[:, :], pG[0][:, 0:NT]))

        @block.tensor
        def _(pe):
            pe.wait_ge(s.zeroed, 2)
            at = bounds(b, pe, range(11))

            def degrees(j):
                for (c0, cw), dst in zip(CH, pG):
                    last = nc.tensor.matmul(dst[0:1, 0:cw], ones[:, :], A32[j % 2][:, c0:c0 + cw], start=(j == 0), stop=(j == NT - 1),
                                            skip_group_check=True)
                last.then_inc(s.deg_ps if j == NT - 1 else s.degd, 1)

            for j in range(NT):
                if j:
                    pe.wait_ge(s.kept, 2 * j)
                    pe.wait_ge(s.counts, 3 * j)
                for dst, w in ((pV, D), (pD, H), (pA[0], 512), (pA[1], 512), (pA[2], 256)):
                    nc.tensor.matmul(dst[:, 0:w], zeros[:, 0:P], zeros[:, 0:w], start=True, stop=False, skip_group_check=True)
                with pe.Fori(at[j], at[j + 1]) as u:
                    for i in range(2):
                        pe.wait_ge(oh_s[i], u + 1)
                        nc.tensor.matmul(pD[:, :], ohf[i][:, :], ew[i][:, :], start=False, stop=False, skip_group_check=True)
                        for (c0, cw), dst in zip(CH, pA):
                            nc.tensor.matmul(dst[:, 0:cw], ohb[i][:, :], ohd[i][:, c0:c0 + cw], start=False, stop=False,
                                             skip_group_check=True)
                        pe.wait_ge(made[i], u + 1)
                        nc.tensor.matmul(pV[:, :], ohf[i][:, :], vw[i][:, :], start=False, stop=False,
                                         skip_group_check=True).then_inc(used[i], 1)
                for dst, w in ((pV, D), (pD, H), (pA[0], 512), (pA[1], 512), (pA[2], 256)):
                    last = nc.tensor.matmul(dst[:, 0:w], zeros[:, 0:P], zeros[:, 0:w], start=False, stop=True, skip_group_check=True)
                last.then_inc(s.summed, 1)
                if j:
                    degrees(j - 1)
            pe.wait_ge(s.counts, 3 * NT)
            degrees(NT - 1)
            pe.wait_ge(s.deg_in, 1)
            for t in range(NT):
                last = nc.tensor.matmul(pG[0][:, t:t + 1], deg_row[0:1, t * P:(t + 1) * P], ones[0:1, 0:1], start=True, stop=True)
            last.then_inc(s.deg_ps, 1)

        @block.scalar
        def _(act):
            for j in range(NT):
                act.wait_ge(s.summed, j + 1)
                if j >= 2:
                    act.wait_ge(s.stored, 16 * (j - 1))
                    act.wait_ge(s.degd, j - 1)
                for out, src in ((b.vals[:, j, :], pV[:, :]), (b.den[:, j, :], pD[:, :])):
                    nc.scalar.activation(out, src, ACT.Copy).then_inc(s.kept, 1)
                for (c0, cw), p in zip(CH, pA):
                    nc.scalar.activation(A32[j % 2][:, c0:c0 + cw], p[:, 0:cw], ACT.Copy).then_inc(s.counts, 1)
                act.wait_ge(s.counts, 3 * (j + 1))
                nc.scalar.activation(b.AT[:, j, :], A32[j % 2][:, :], ACT.Copy).then_inc(s.rounded, 1)
            act.wait_ge(s.kept, 2 * NT)
            act.wait_ge(s.rounded, NT)
    b.mid.close()


def attention_out(b, top):
    nc, a = b.nc, b.a
    ident = b.cst[:, 0:128]
    with ExitStack() as ctx:
        sb, ps, s = b.tools(ctx, "fa fa_free fd fd_free w_in b_in normed biased stats sd scaled xf cv cp vt_in h_in")
        w1, w2, wo = sb("w1", [P, KC, D]), sb("w2", [P, KC, D]), sb("wo", [P, KC, D])
        vT, hT = sb("vT", [P, KC, NP]), sb("hT", [P, KC, NP])
        bias = sb("bias", [P, 2, D])
        rden = sb("rden", [P, NT, H])
        norm = Norm(nc, sb, "x1")
        bank = [ps(f"bank{i}", [P, D]) for i in range(8)]
        vals, R0, mixT = b.vals, b.R0, b.xnT
        block = ctx.enter_context(nc.Block())

        @block.sync
        def _(sp):
            sp.dma_start(w1[:, :, :], row_chunks(a["L0_gnn_W1"])).then_inc(s.w_in, 16)
            sp.dma_start(w2[:, :, :], row_chunks(a["L0_gnn_W2"])).then_inc(s.w_in, 16)
            sp.dma_start(wo[:, :, :], row_chunks(a["L0_mix_WoutT"])).then_inc(s.w_in, 16)
            sp.dma_start(bias[:, 0, :], bcast(a["L0_gnn_b2"])).then_inc(s.b_in, 16)
            sp.dma_start(bias[:, 1, :], bcast(a["L0_mix_bout"])).then_inc(s.b_in, 16)

        @block.gpsimd
        def _(pool):
            link = chain(pool, s.cp)
            pool.wait_ge(s.b_in, 32)
            link(nc.gpsimd.tensor_tensor(bias[:, 0, :], bias[:, 0, :], bias[:, 1, :], ALU.add))
            for t in range(NT):
                nc.gpsimd.tensor_tensor(R0[:, t, :], R0[:, t, :], bias[:, 0, :], ALU.add).then_inc(s.biased, 1)

        @block.vector
        def _(dve):
            link = chain(dve, s.cv)
            v = nc.vector
            link(v.tensor_scalar_add(rden[:, :, :], b.den[:, :, :], 1e-16))
            link(v.reciprocal(rden[:, :, :], rden[:, :, :]))
            for t in range(NT):
                v.tensor_tensor(vals[:, t, :].rearrange("p (h d) -> p h d", h=H), vals[:, t, :].rearrange("p (h d) -> p h d", h=H),
                                rden[:, t, :].unsqueeze(2).broadcast_to([P, H, HD]), ALU.mult).then_inc(s.normed, 1)
            full = Emptier(dve, bank[4:], s.fd, s.fd_free)
            for t in range(NT):
                dve.wait_ge(s.biased, t + 1)
                src = full.take()
                full.done(v.tensor_tensor(R0[:, t, :], R0[:, t, :], src[:, :], ALU.add))
            full.all_done()
            norm.stats(link, R0, s.stats)
            norm.scales(dve, link, s.sd, 1, s.scaled)

        @block.scalar
        def _(act):
            full = Emptier(act, bank[:4], s.fa, s.fa_free)
            for t0, nt in GRP:
                for c in range(KC):
                    src = full.take()
                    full.done(nc.scalar.activation(vT[:, c, t0 * P:(t0 + nt) * P], src[:, 0:nt * P], ACT.Copy))
            full.all_done()
            act.sem_inc(s.vt_in, 1)
            for m in range(KC):
                for c0, cw in CH:
                    src = full.take()
                    full.done(nc.scalar.activation(hT[:, m, c0:c0 + cw], src[:, 0:cw], ACT.Identity,
                                                   bias=b.cols[:, 8 + m:9 + m]))
            full.all_done()
            act.sem_inc(s.h_in, 1)
            norm.root(act, s.stats, 1, s.sd)
            act.wait_ge(s.scaled, 1)
            for t in range(NT):
                norm.apply(vals, R0, t).then_inc(s.xf, 1)
            for t0, nt in GRP:
                for c in range(KC):
                    src = full.take()
                    full.done(nc.scalar.activation(mixT[:, c, t0 * P:(t0 + nt) * P], src[:, 0:nt * P], ACT.Copy))
            full.all_done()

        @block.tensor
        def _(pe):
            fa = Filler(pe, bank[:4], s.fa, s.fa_free)
            fd = Filler(pe, bank[4:], s.fd, s.fd_free)
            for t0, nt in GRP:
                pe.wait_ge(s.normed, t0 + nt)
                for c in range(KC):
                    transposes(nc, fa, vals, ident, t0, nt, c)
            pe.wait_ge(s.w_in, 48)
            pe.wait_ge(s.vt_in, 1)
            for m in range(KC):
                for c0, cw in CH:
                    dst = fa.take()
                    fa.done(product(nc, dst[:, 0:cw], chunks(w1, m * P, P), chunks(vT, c0, cw)))
            pe.wait_ge(s.h_in, 1)
            for t in range(NT):
                dst = fd.take()
                fd.done(product(nc, dst[:, :], tile(hT, t) + tile(mixT, t), chunks(w2) + chunks(wo)))
            for t0, nt in GRP:
                pe.wait_ge(s.xf, t0 + nt)
                for c in range(KC):
                    transposes(nc, fa, vals, ident, t0, nt, c)


def experts0(b, top):
    nc, a, cst = b.nc, b.a, b.cst
    ident = cst[:, 0:128]
    with ExitStack() as ctx:
        sb, ps, s = b.tools(ctx, "fa fa_free fd fd_free g_in w_in wh wl xh xl hh hl lg comb_in cv exp_s")
        w = sb("w", [P, 4 * D])
        wh, wl = ([sb(f"{n}{i}", [P, 4 * D], F32R) for i in range(2)] for n in ("wh", "wl"))
        wg = sb("wg", [P, KC, EXP0])
        bg = sb("bg", [P, EXP0])
        b2 = sb("b2", [EXP0, D])
        g = [sb(f"g{i}", [P, D]) for i in range(3)]
        hh, hl = ([sb(f"{n}{i}", [P, 2, D], F32R) for i in range(3)] for n in ("hh", "hl"))
        lg = sb("lg", [P, NT, EXP0])
        pr = sb("pr", [P, NT, EXP0])
        sm = sb("sm", [P, 3, NT])
        mx8 = sb("mx8", [P, NT, 8])
        ix8 = sb("ix8", [P, NT, 8], U32)
        ixf = sb("ixf", [P, NT, 8])
        m1, m2 = sb("m1", [P, NT, EXP0]), sb("m2", [P, NT, EXP0])
        comb = sb("comb", [P, NT, EXP0])
        combT = sb("combT", [EXP0, NP])
        bank = [ps(f"bank{i}", [P, D]) for i in range(8)]
        R0, xT = b.R0, b.xnT
        xh, xl = b.over("vals", "xh", [P, KC, NP], F32R), b.over("xnT", "xl", [P, KC, NP], F32R)
        W1 = lambda x: x[:, 0:2 * D].rearrange("p (c n) -> p c n", c=KC)
        W2 = lambda x: x[:, 2 * D:4 * D].rearrange("p (c n) -> p c n", c=2)
        ITEMS = [(e, i) for e in range(EXP0) for i in range(len(CH))]
        COMB_AT = 3
        tiles = lambda i: range(CH[i][0] // P, (CH[i][0] + CH[i][1]) // P)
        banks_to = lambda n: 1 + (3 if n >= COMB_AT else 0) + sum(len(tiles(i)) * (1 + (e == EXP0 - 1)) for e, i in ITEMS[:n + 1])
        block = ctx.enter_context(nc.Block())

        @block.sync
        def _(sp):
            sp.dma_start(wg[:, :, :], row_chunks(a["L0_ffn_Wg"])).then_inc(s.g_in, 16)
            sp.dma_start(bg[:, :], bcast(a["L0_ffn_bg"])).then_inc(s.g_in, 16)
            sp.dma_start(b2[:, :], a["L0_ffn_b2"]).then_inc(s.g_in, 16)
            for e in range(EXP0):
                if e:
                    sp.wait_ge(s.wl, e)
                sp.dma_start(W1(w), row_chunks(a["L0_ffn_W1"][e])).then_inc(s.w_in, 16)
                sp.dma_start(W2(w), row_chunks(a["L0_ffn_W2"][e])).then_inc(s.w_in, 16)

        @block.gpsimd
        def _(pool):
            for e in range(EXP0):
                pool.wait_ge(s.w_in, 32 * (e + 1))
                if e >= 2:
                    pool.wait_ge(s.fd, banks_to(3 * (e - 1) - 1))
                nc.gpsimd.tensor_copy(wh[e % 2][:, :], w[:, :]).then_inc(s.wh, 1)
                pool.wait_ge(s.wh, e + 1)
                nc.gpsimd.tensor_tensor(wl[e % 2][:, :], w[:, :], wh[e % 2][:, :], ALU.subtract).then_inc(s.wl, 1)

        @block.tensor
        def _(pe):
            fa = Filler(pe, bank[:3], s.fa, s.fa_free)
            fd = Filler(pe, bank[3:], s.fd, s.fd_free)

            def hidden(n):
                e, i = ITEMS[n]
                c0, cw = CH[i]
                pe.wait_ge(s.wl, e + 1)
                for m in range(2):
                    dst = fa.take()
                    fa.done(product3(nc, dst[:, 0:cw], *(chunks(W1(x[e % 2]), m * P, P) for x in (wh, wl)),
                                     *(chunks(x, c0, cw) for x in (xh, xl))))

            pe.wait_ge(s.g_in, 48)
            pe.wait_ge(s.xl, len(CH))
            dst = fd.take()
            for t in range(NT):
                last = product(nc, dst[:, t * EXP0:(t + 1) * EXP0], tile(xh[:, :, :].bitcast(F32), t) + tile(xl[:, :, :].bitcast(F32), t),
                               chunks(wg, 0, EXP0) * 2)
            fd.done(last)
            hidden(0)
            for n, (e, i) in enumerate(ITEMS):
                if n + 1 < len(ITEMS):
                    hidden(n + 1)
                if n == COMB_AT:
                    pe.wait_ge(s.comb_in, 1)
                    for t0, nt in GRP:
                        dst = fd.take()
                        for t in range(nt):
                            last = nc.tensor.transpose(dst[:EXP0, t * P:(t + 1) * P], comb[:, t0 + t, :], ident)
                        fd.done(last)
                pe.wait_ge(s.hl, 2 * n + 2)
                for t in tiles(i):
                    o = t * P - CH[i][0]
                    dst = fd.take()
                    fd.done(product3(nc, dst[:, :], *([x[n % 3][:, m, o:o + P] for m in range(2)] for x in (hh, hl)),
                                     *(chunks(W2(x[e % 2])) for x in (wh, wl))))
                    if e == EXP0 - 1:
                        dst = fd.take()
                        fd.done(nc.tensor.matmul(dst[:, :], combT[:, t * P:(t + 1) * P], b2[:, :], start=True, stop=True))

        @block.scalar
        def _(act):
            full = Emptier(act, bank[:3], s.fa, s.fa_free)
            for c0, cw in CH:
                nc.scalar.activation(xh[:, :, c0:c0 + cw], xT[:, :, c0:c0 + cw], ACT.Copy).then_inc(s.xh, 1)
            act.wait_ge(s.lg, 1)
            nc.scalar.activation(pr[:, :, :], lg[:, :, :], ACT.Exp).then_inc(s.exp_s, 1)

            def high(k):
                n, m = k // 2, k % 2
                cw = CH[ITEMS[n][1]][1]
                act.wait_ge(s.fa_free, k + 1)
                if n >= 3 and m == 0:
                    act.wait_ge(s.fd, banks_to(n - 3))
                nc.scalar.activation(hh[n % 3][:, m, 0:cw], g[k % 3][:, 0:cw], ACT.Copy).then_inc(s.hh, 1)

            for k in range(2 * len(ITEMS)):
                e, i = ITEMS[k // 2]
                cw = CH[i][1]
                if k >= 3:
                    act.wait_ge(s.hl, k - 2)
                src = full.take()
                full.done(nc.scalar.activation(g[k % 3][:, 0:cw], src[:, 0:cw], ACT.Gelu_apprx_tanh,
                                               bias=b.cols[:, 12 + 2 * e + k % 2:13 + 2 * e + k % 2]))
                if k % 2:
                    high(k - 1)
                    high(k)

        @block.vector
        def _(dve):
            v = nc.vector
            link = chain(dve, s.cv)
            full = Emptier(dve, bank[3:], s.fd, s.fd_free)
            each = lambda x: x.unsqueeze(2).broadcast_to([P, NT, EXP0])
            col = lambda x: x.broadcast_to([P, NT, EXP0])
            for i, (c0, cw) in enumerate(CH):
                dve.wait_ge(s.xh, i + 1)
                v.tensor_tensor(xl[:, :, c0:c0 + cw], xT[:, :, c0:c0 + cw], xh[:, :, c0:c0 + cw], ALU.subtract).then_inc(s.xl, 1)
            dve.wait_ge(s.g_in, 48)
            src = full.take()
            full.done(v.tensor_tensor(lg[:, :, :], src[:, 0:NT * EXP0].rearrange("p (t e) -> p t e", t=NT),
                                      bg[:, :].unsqueeze(1).broadcast_to([P, NT, EXP0]), ALU.add))
            full.all_done()
            link(v.tensor_reduce(sm[:, 0, :], lg[:, :, :], AX.X, ALU.max))
            v.tensor_tensor(lg[:, :, :], lg[:, :, :], each(sm[:, 0, :]), ALU.subtract).then_inc(s.lg, 1)
            dve.wait_ge(s.exp_s, 1)
            link(v.tensor_reduce(sm[:, 1, :], pr[:, :, :], AX.X, ALU.add))
            link(v.reciprocal(sm[:, 2, :], sm[:, 1, :]))
            link(v.tensor_tensor(pr[:, :, :], pr[:, :, :], each(sm[:, 2, :]), ALU.mult))
            for t in range(NT):
                last = v.max(mx8[:, t, :], pr[:, t, :])
            link(last)
            for t in range(NT):
                last = v.max_index(ix8[:, t, :], mx8[:, t, :], pr[:, t, :])
            link(last)
            link(v.tensor_copy(ixf[:, :, :], ix8[:, :, :]))
            iota = cst[:, 784:792].unsqueeze(1).broadcast_to([P, NT, EXP0])
            v.tensor_tensor(m1[:, :, :], iota, col(ixf[:, :, 0:1]), ALU.is_equal)
            link(v.tensor_tensor(m2[:, :, :], iota, col(ixf[:, :, 1:2]), ALU.is_equal))
            link(v.tensor_tensor(m1[:, :, :], m1[:, :, :], m2[:, :, :], ALU.add))
            link(v.tensor_tensor(comb[:, :, :], pr[:, :, :], m1[:, :, :], ALU.mult))
            dve.sem_inc(s.comb_in, 1)

            def low(n):
                cw = CH[ITEMS[n][1]][1]
                for m in range(2):
                    dve.wait_ge(s.hh, 2 * n + m + 1)
                    v.tensor_tensor(hl[n % 3][:, m, 0:cw], g[(2 * n + m) % 3][:, 0:cw], hh[n % 3][:, m, 0:cw],
                                    ALU.subtract).then_inc(s.hl, 1)

            low(0)
            added = [0] * NT
            for n, (e, i) in enumerate(ITEMS):
                if n + 1 < len(ITEMS):
                    low(n + 1)
                if n == COMB_AT:
                    for t0, nt in GRP:
                        src = full.take()
                        full.done(v.tensor_copy(combT[:, t0 * P:(t0 + nt) * P], src[:EXP0, 0:nt * P]))
                for t in tiles(i):
                    src = full.take()
                    if e:
                        dve.wait_ge(s.fd_free, added[t])
                    full.done(v.scalar_tensor_tensor(out=R0[:, t, :], in0=src[:, :], scalar=comb[:, t, e:e + 1],
                                                     in1=R0[:, t, :], op0=ALU.mult, op1=ALU.add))
                    added[t] = full.n
                    if e == EXP0 - 1:
                        src = full.take()
                        dve.wait_ge(s.fd_free, added[t])
                        full.done(v.tensor_tensor(R0[:, t, :], R0[:, t, :], src[:, :], ALU.add))


def sage(b, top):
    nc, a, cst = b.nc, b.a, b.cst
    ident = cst[:, 0:128]
    with ExitStack() as ctx:
        sb, ps, s = b.tools(ctx, "fa fa_free fy fy_half fy_free fd fd_free stats sd scaled xn z_in hn hw hb h1 cv  "
                                "mid at_in w_in b_in lnv_in x3a")
        wl, wr = sb("wl", [P, KC, D]), sb("wr", [P, KC, D])
        vec = sb("vec", [P, 3, D])
        h = sb("h", [P, NT, D])
        y_hi, y_lo = sb("y_hi", [P, NT, D], F32R), sb("y_lo", [P, NT, D], F32R)
        hT = [sb(f"hT{i}", [P, KC, P]) for i in range(2)]
        rdeg = sb("rdeg", [P, NT])
        norm = RowNorm(nc, sb, "n", s.stats, s.sd, s.scaled)
        bank = [ps(f"bank{i}", [P, D]) for i in range(8)]
        R0, xn, xnT, AT = b.R0, b.vals, b.xnT, b.AT
        A32 = b.over("AT", "A32", [P, NT, NP])
        VEC = (("L1_gnn_b1l", "L1_gnn_ln1_w", "L1_gnn_ln1_b"), ("L1_gnn_b2l", "L1_gnn_ln2_w", "L1_gnn_ln2_b"))
        block = ctx.enter_context(nc.Block())

        @block.sync
        def _(sp):
            few = sp.value_load(b.few[0:1, 0:1], min_val=0, max_val=1)
            with sp.If(few == 0):
                sp.dma_start(A32[:, :, :], b.AT_dram).then_inc(s.at_in, 16)
            for i in range(2):
                if i:
                    sp.wait_ge(s.z_in, NT)
                sp.dma_start(wl[:, :, :], row_chunks(a[f"L1_gnn_W{i + 1}lT"])).then_inc(s.w_in, 16)
                sp.dma_start(wr[:, :, :], row_chunks(a[f"L1_gnn_W{i + 1}rT"])).then_inc(s.w_in, 16)
                sp.dma_start(vec[:, 0, :], bcast(a[VEC[i][0]])).then_inc(s.b_in, 16)
                if i:
                    sp.wait_ge(s.h1, NT)
                for j in (1, 2):
                    sp.dma_start(vec[:, j, :], bcast(a[VEC[i][j]])).then_inc(s.lnv_in, 16)

        @block.tensor
        def _(pe):
            fa = Filler(pe, bank[:2], s.fa, s.fa_free)
            fy = Filler(pe, bank[2:5], s.fy, s.fy_free)
            fd = Filler(pe, bank[5:], s.fd, s.fd_free)
            few = pe.value_load(b.few[0:1, 0:1], min_val=0, max_val=1)
            for layer, rows in ((0, xn), (1, h)):
                pe.wait_ge(s.w_in, 32 * (layer + 1))
                for t in range(NT + 1):
                    if t < NT:
                        pe.wait_ge((s.xn, s.h1)[layer], t + 1)
                        dst = fa.take()
                        for c in range(KC):
                            last = nc.tensor.transpose(dst[:, c * P:(c + 1) * P], rows[:, t, c * P:(c + 1) * P], ident)
                        fa.done(last)
                    if t:
                        u = t - 1
                        pe.wait_ge(s.fa_free, layer * NT + u + 1)
                        x = tile(xnT, u) if layer == 0 else [hT[u % 2][:, c, :] for c in range(KC)]
                        dst = fy.take()
                        fy.done(product(nc, dst[:, :], x, chunks(wl)))
                        dst = fd.take()
                        fd.done(product(nc, dst[:, :], x, chunks(wr)))
                pe.wait_ge(s.fy_free, NT * (layer + 1))
                n = fd.n
                for yes, A, dt in ((1, AT, F32R), (0, A32, F32)):
                    fd.n = n
                    with pe.If(few == yes):
                        if not yes:
                            pe.wait_ge(s.at_in, 16)
                        for t in range(NT):
                            dst = fd.take()
                            fd.done(product(nc, dst[:, :], [A[:, k, t * P:(t + 1) * P] for k in range(NT) for _ in range(2)],
                                            [y[:, k, :].bitcast(dt) for k in range(NT) for y in (y_hi, y_lo)]))

        @block.scalar
        def _(act):
            fa = Emptier(act, bank[:2], s.fa, s.fa_free)
            fy = Emptier(act, bank[2:5], s.fy, s.fy_half)

            def rows_in(layer, t):
                src = fa.take()
                if layer:
                    if t >= 2:
                        act.wait_ge(s.fd, NT * 2 + t - 1)
                    out = hT[t % 2][:, :, :]
                else:
                    out = xnT[:, :, t * P:(t + 1) * P]
                fa.done(nc.scalar.activation(out, src[:, :].rearrange("p (c n) -> p c n", c=KC), ACT.Copy))

            def y_high(t):
                src = fy.take()
                fy.done(nc.scalar.activation(y_hi[:, t, :], src[:, :], ACT.Copy))

            for t in range(NT + 3):
                if t < NT:
                    norm.root(act, t)
                if 1 <= t <= NT:
                    norm.apply(act, xn[:, t - 1, :], R0[:, t - 1, :], t - 1).then_inc(s.xn, 1)
                if 2 <= t <= NT + 1:
                    rows_in(0, t - 2)
                if t >= 3:
                    y_high(t - 3)
            for layer, rows in ((0, h), (1, xn)):
                if layer:
                    for t in range(NT + 1):
                        if t < NT:
                            rows_in(1, t)
                        if t:
                            y_high(t - 1)
                for t in range(NT + 1):
                    if t < NT:
                        norm.root(act, NT * (layer + 1) + t)
                    if t:
                        norm.apply(act, rows[:, t - 1, :], rows[:, t - 1, :], NT * (layer + 1) + t - 1).then_inc(s.hn, 1)

        @block.vector
        def _(dve):
            v = nc.vector
            link = chain(dve, s.cv)
            fy = Emptier(dve, bank[2:5], s.fy_half, s.fy_free)
            fd = Emptier(dve, bank[5:], s.fd, s.fd_free)
            link(v.tensor_scalar(rdeg[:, :], b.deg[:, :], 1.0, None, ALU.max))
            link(v.reciprocal(rdeg[:, :], rdeg[:, :]))

            def y_low_and_z(layer, t):
                src = fy.take()
                fy.done(v.tensor_tensor(y_lo[:, t, :], src[:, :], y_hi[:, t, :], ALU.subtract))
                if t == 0:
                    dve.wait_ge(s.b_in, 16 * (layer + 1))
                src = fd.take()
                fd.done(v.tensor_tensor((h, xn)[layer][:, t, :], src[:, :], vec[:, 0, :], ALU.add))
                dve.wait_ge(s.fd_free, fd.n)
                dve.sem_inc(s.z_in, 1)

            for t in range(NT + 3):
                if t < NT:
                    norm.stats(dve, link, R0[:, t, :], t)
                if 1 <= t <= NT:
                    norm.scales(dve, link, t - 1)
                if t >= 3:
                    y_low_and_z(0, t - 3)
            for layer, out in ((0, h), (1, xn)):
                if layer:
                    for t in range(NT):
                        y_low_and_z(1, t)
                dve.wait_ge(s.lnv_in, 32 * (layer + 1))
                for t in range(NT + 3):
                    if t < NT:
                        src = fd.take()
                        fd.done(v.scalar_tensor_tensor(out=out[:, t, :], in0=src[:, :], scalar=rdeg[:, t:t + 1], in1=out[:, t, :],
                                                       op0=ALU.mult, op1=ALU.add))
                        fd.all_done()
                        norm.stats(dve, link, out[:, t, :], NT * (layer + 1) + t)
                    if 1 <= t <= NT:
                        norm.scales(dve, link, NT * (layer + 1) + t - 1)
                    if 2 <= t <= NT + 1:
                        dve.wait_ge(s.hn, layer * NT + t - 1)
                        v.tensor_tensor(out[:, t - 2, :], out[:, t - 2, :], vec[:, 1, :], ALU.mult).then_inc(s.hw, 1)
                    if t >= 3 and layer == 0:
                        dve.wait_ge(s.hb, t - 2)
                        v.scalar_tensor_tensor(out=h[:, t - 3, :], in0=h[:, t - 3, :], scalar=0.0, in1=xn[:, t - 3, :],
                                               op0=ALU.max, op1=ALU.add).then_inc(s.h1, 1)

        @block.gpsimd
        def _(pool):
            for layer, out in ((0, h), (1, xn)):
                pool.wait_ge(s.lnv_in, 32 * (layer + 1))
                for t in range(NT + 1):
                    if t < NT:
                        pool.wait_ge(s.hw, layer * NT + t + 1)
                        nc.gpsimd.tensor_tensor(out[:, t, :], out[:, t, :], vec[:, 2, :], ALU.add).then_inc(s.hb, 1)
                    if t:
                        u = t - 1
                        pool.wait_ge((s.h1, s.hb)[layer], layer * NT + u + 1)
                        if layer:
                            pool.wait_ge(s.mid, u + 1)
                        nc.gpsimd.tensor_tensor(R0[:, u, :], R0[:, u, :], out[:, u, :], ALU.add).then_inc((s.mid, s.x3a)[layer], 1)


def performer(b, top):
    nc, a, cst = b.nc, b.a, b.cst
    ident = cst[:, 0:128]
    EPS = 1e-4
    NORM = float(HD) ** -0.25
    VW = HD + 1
    with ExitStack() as ctx:
        sb, ps, s = b.tools(ctx, "xh xl w_in whs wls p_in p_zero ph pl v_in ones_in bo biased cv "
                                "fs fs_half fs_free fk fk_free sqs sq_used dg_free kin qin "
                                "km km_free gm gx gx_free kbias ek ek_free ekh ekl ctx_in ct ct_half ct_free kb_ps kb_in "
                                "dq dq_free kmx qbias rden scaled tq tq_half tq_free used oq_half oq_free fo fo_free o_in scr")
        T = [P, KC, NP]
        kh, kl = b.over("AT", "kh", T, F32R), b.over("AT", "kl", T, F32R, KC * NP)
        wst = b.over("AT", "wst", [P, KC, D], F32, 2 * KC * NP)
        xh, xl = b.over("vals", "xh", T, F32R), b.over("xnT", "xl", T, F32R)
        VN = NT * H * VW
        sb("v_reg", [P, max(2 * VN, 4 * 3 * D + 2 * 36 * HD)])
        vh, vl = (b.over("v_reg", n, [P, NT, H, VW], F32R, o) for n, o in (("vh", 0), ("vl", VN)))
        qp = [[b.over("v_reg", f"qp{i}{j}", [P, 3, D], F32R, (2 * i + j) * 3 * D) for j in range(2)]
              for i in range(2)]
        cx = [b.over("v_reg", f"cx{j}", [P, 36, HD], F32R, 12 * D + j * 36 * HD) for j in range(2)]
        heads_of = lambda x, cw, i: x[:cw, 12 * i:12 * i + 12, :].rearrange("p (q b) d -> p q b d", b=3)[:, :, 0:3:2, :]
        placed = lambda x, cw, i, h: x[:cw, 12 * i + 3 * (h // 2) + h % 2:12 * i + 3 * (h // 2) + h % 2 + 2, :].rearrange("p b d -> p (b d)")
        for n in ("E0", "E1"):
            sb(n, [P, H * M])
        cT, ks = sb("cT", [P, H, M]), sb("ks", [P, H, M])
        ef, eh, el = ([b.over(r, f"{n}{i}", [P, 4, M], dt, i * 4 * M) for i in range(2)]
                      for r, n, dt in (("E0", "ef", F32), ("E1", "eh", F32R), ("E0", "el", F32R)))
        WH, WL = ([b.over(r, f"{n}{i}", [P, KC, D], F32R) for i, r in enumerate(rs)]
                  for n, rs in (("WH", ("E0", "cT", "E0", "E1")), ("WL", ("E1", "ks", "E1", "cT"))))
        pj = sb("pj", [P, 2, M])
        ph, pl = sb("ph", [P, 2, M], F32R), sb("pl", [P, 2, M], F32R)
        sq = [sb(f"sq{i}", [P, D]) for i in range(2)]
        diag = sb("diag", [P, 2, NT, H])
        kmax, kb, qmax, qb, den, rd = (sb(n, [P, NT, H]) for n in ("kmax", "kb", "qmax", "qb", "den", "rd"))
        g1 = sb("g1", [P, 4])
        gr = sb("gr", [1, 4])
        ones = sb("ones", [P, P])
        scratch = sb("scratch", [P, M])
        bo = b.over("AT", "bo", [P, D], F32, 2 * KC * NP + KC * D)
        bank = [ps(f"bank{i}", [P, D]) for i in range(8)]
        R0 = b.R0
        valid = lambda t: P if t < NT - 1 else LAST
        GH = [(t0, nt, h) for t0, nt in GRP for h in range(H)]
        block = ctx.enter_context(nc.Block())

        @block.sync
        def _(sp):
            W = ("L1_mix_Wv", "L1_mix_Wk", "L1_mix_Wq", "L1_mix_Wo")
            sp.wait_ge(s.p_zero, 1)
            for i in range(2):
                sp.dma_start(pj[i * HD:(i + 1) * HD, i, :], a["L1_mix_projT"]).then_inc(s.p_in, 16)
            for i in range(4):
                if i:
                    sp.wait_ge(s.wls, i)
                sp.dma_start(wst[:, :, :], row_chunks(a[W[i]])).then_inc(s.w_in, 16)
                if i == 0:
                    sp.dma_start(bo[:, :], bcast(a["L1_mix_bo"])).then_inc(s.bo, 16)

        @block.gpsimd
        def _(pool):
            g = nc.gpsimd
            g.memset(pj[:, :, :], 0.0).then_inc(s.p_zero, 1)

            def split(i):
                pool.wait_ge(s.w_in, 16 * (i + 1))
                g.tensor_copy(WH[i][:, :, :], wst[:, :, :]).then_inc(s.whs, 1)
                pool.wait_ge(s.whs, i + 1)
                g.tensor_tensor(WL[i][:, :, :], wst[:, :, :], WH[i][:, :, :], ALU.subtract).then_inc(s.wls, 1)

            split(0)
            split(1)
            pool.wait_ge(s.p_in, 32)
            g.tensor_copy(ph[:, :, :], pj[:, :, :]).then_inc(s.ph, 1)
            pool.wait_ge(s.ph, 1)
            g.tensor_tensor(pl[:, :, :], pj[:, :, :], ph[:, :, :], ALU.subtract).then_inc(s.pl, 1)
            pool.wait_ge(s.bo, 16)
            for t in range(NT):
                g.tensor_tensor(R0[:, t, :], R0[:, t, :], bo[:, :], ALU.add).then_inc(s.biased, 1)
            pool.wait_ge(s.used, 2 * NT)
            split(2)
            for k, (t0, nt, h) in enumerate(GH):
                for t in range(nt):
                    if t == 0:
                        pool.wait_ge(s.rden, k + 1)
                    g.tensor_scalar(ef[k % 2][:, t, :], ef[k % 2][:, t, :], EPS, rd[:, t0 + t, h:h + 1], ALU.add,
                                    ALU.mult).then_inc(s.scaled, 1)
                if k == 2:
                    split(3)

        def dash3(nc, dst, t, h):
            c, cols = h // 2, slice(t * P, (t + 1) * P)
            return product3(nc, dst, [kh[:, c, cols]], [kl[:, c, cols]], [ph[:, h % 2, :]], [pl[:, h % 2, :]])

        @block.tensor
        def _(pe):
            fs = Filler(pe, bank[0:4], s.fs, s.fs_free)
            dg = Filler(pe, bank[7:8], s.sq_used, s.dg_free)

            def transposed(i, x, nsq):
                pe.wait_ge(s.wls, i + 1)
                dst2 = dg.take()

                def squares(k):
                    m, (c0, cw) = k // len(CH), CH[k % len(CH)]
                    pe.wait_ge(s.sqs, nsq + k + 1)
                    for t in range(cw // P):
                        last = nc.tensor.matmul(dst2[:, (c0 // P + t) * H + 2 * m:(c0 // P + t) * H + 2 * m + 2],
                                                sq[k % 2][:, t * P:(t + 1) * P], cst[:, 648:650], start=True, stop=True)
                    last.then_inc(s.sq_used, 1)
                    return last

                for k in range(KC * len(CH)):
                    m, (c0, cw) = k // len(CH), CH[k % len(CH)]
                    dst = fs.take()
                    fs.done(product3(nc, dst[:, 0:cw], chunks(WH[i], m * P, P), chunks(WL[i], m * P, P),
                                     chunks(xh, c0, cw), chunks(xl, c0, cw)))
                    if k:
                        squares(k - 1)
                squares(KC * len(CH) - 1)

            pe.wait_ge(s.wls, 1)
            pe.wait_ge(s.xl, len(CH))
            for t in range(NT):
                dst = fs.take()
                fs.done(product3(nc, dst[:, :], tile(xh, t), tile(xl, t), chunks(WH[0]), chunks(WL[0])))
            transposed(1, None, 0)
            pe.wait_ge(s.pl, 1)
            pe.wait_ge(s.kin, 1)
            pe.wait_ge(s.fs_free, fs.n)
            km = Filler(pe, bank[0:4], s.km, s.km_free)
            for t in range(NT):
                for h in range(H):
                    dst = km.take()
                    km.done(dash3(nc, dst[:, 0:M], t, h))
            pe.wait_ge(s.ones_in, 1)
            gx = Filler(pe, bank[7:8], s.gx, s.gx_free)
            pe.wait_ge(s.dg_free, 1)
            pe.wait_ge(s.gm, 1)
            dst = gx.take()
            gx.done(nc.tensor.transpose(dst[0:1, 0:P], g1[:, 0:1], ident))
            pe.wait_ge(s.gm, 2)
            dst = gx.take()
            gx.done(nc.tensor.matmul(dst[:, 0:1], ones[0:1, :], gr[:, 0:1], start=True, stop=True))
            pe.wait_ge(s.km_free, km.n)
            pe.wait_ge(s.gx_free, 2)
            ek = Filler(pe, bank[0:4], s.ek, s.ek_free)
            for r in range(2):
                if r:
                    pe.wait_ge(s.ctx_in, 4)
                for t in range(NT + 1):
                    if t < NT:
                        for h in range(4):
                            dst = ek.take()
                            ek.done(dash3(nc, dst[:, 0:M], t, 4 * r + h))
                    if t:
                        u, n = t - 1, r * NT + t - 1
                        pe.wait_ge(s.ekl, n + 1)
                        for h in range(4):
                            for i, (x, y) in enumerate(((vh, eh[n % 2]), (vl, eh[n % 2]), (vh, el[n % 2]))):
                                last = nc.tensor.matmul(bank[4 + h][:VW, 0:M], x[:valid(u), u, 4 * r + h, :], y[:valid(u), h, :],
                                                        start=(u == 0 and i == 0), stop=(u == NT - 1 and i == 2),
                                                        skip_group_check=True)
                        last.then_inc(s.used, 1)
            pe.wait_ge(s.ctx_in, 8)
            pe.wait_ge(s.ek_free, ek.n)
            ct = Filler(pe, bank[0:3], s.ct, s.ct_free)
            for c0, cw in MC:
                dst = ct.take()
                for h in range(H):
                    last = nc.tensor.transpose(dst[:cw, h * HD:(h + 1) * HD], cT[:HD, h, c0:c0 + cw], ident[:HD, :HD])
                ct.done(last)
            kbf = Filler(pe, bank[4:7], s.kb_ps, s.kb_in)
            for h in range(H):
                dst = kbf.take()
                kbf.done(nc.tensor.matmul(dst[:, 0:M], ones[HD:VW, :], cT[HD:VW, h, :], start=True, stop=True))
            pe.wait_ge(s.ct_free, 3)
            dg.n = 0
            transposed(2, None, KC * len(CH))
            pe.wait_ge(s.qin, 1)
            pe.wait_ge(s.fs_free, fs.n)
            pe.wait_ge(s.kb_in, H)
            pe.wait_ge(s.dg_free, 2)
            dq = Filler(pe, bank[0:3], s.dq, s.dq_free)
            tq = Filler(pe, bank[3:6], s.tq, s.tq_free)
            oq = Filler(pe, bank[6:8], s.used, s.oq_free)
            nq = 0
            for k in range(len(GH) + 2):
                if k < len(GH):
                    t0, nt, h = GH[k]
                    for t in range(nt):
                        dst = dq.take()
                        dq.done(dash3(nc, dst[:, 0:M], t0 + t, h))
                if 1 <= k <= len(GH):
                    t0, nt, h = GH[k - 1]
                    nq += nt
                    pe.wait_ge(s.scaled, nq)
                    for c0, cw in MC:
                        dst = tq.take()
                        for t in range(nt):
                            last = nc.tensor.transpose(dst[:cw, t * P:(t + 1) * P], ef[(k - 1) % 2][:, t, c0:c0 + cw], ident)
                        tq.done(last)
                if k >= 2:
                    t0, nt, h = GH[k - 2]
                    pe.wait_ge(s.tq_free, 3 * (k - 1))
                    if h % 2 == 0:
                        pair = oq.take()
                    xs = qp[k % 2]
                    ops = [(c, x, i, cw) for c, x in ((cx[0], xs[0]), (cx[1], xs[0]), (cx[0], xs[1])) for i, (_, cw) in enumerate(MC)]
                    for n, (c, x, i, cw) in enumerate(ops):
                        last = nc.tensor.matmul(pair[:, 0:nt * P], placed(c, cw, i, h), x[:cw, i, 0:nt * P], start=(h % 2 == 0 and n == 0),
                                                stop=(h % 2 == 1 and n == len(ops) - 1))
                    last.then_inc(s.used, 1)
            pe.wait_ge(s.oq_free, oq.n)
            pe.wait_ge(s.wls, 4)
            fo = Filler(pe, bank[0:6], s.fo, s.fo_free)
            for t in range(NT):
                dst = fo.take()
                fo.done(product3(nc, dst[:, :], tile(xh, t), tile(xl, t), chunks(WH[3]), chunks(WL[3])))

        @block.scalar
        def _(act):
            f = nc.scalar.activation
            for c0, cw in CH:
                f(xh[:, :, c0:c0 + cw], b.xnT[:, :, c0:c0 + cw], ACT.Copy).then_inc(s.xh, 1)
            fs = Emptier(act, bank[0:4], s.fs, s.fs_half)
            for t in range(NT):
                src = fs.take()
                fs.done(f(vh[:, t, :, 0:HD], src[:, :].rearrange("p (h d) -> p h d", h=H), ACT.Copy))

            def transposed(nsq):
                for k in range(KC * len(CH)):
                    m, (c0, cw) = k // len(CH), CH[k % len(CH)]
                    src = fs.take()
                    if nsq + k >= 2:
                        act.wait_ge(s.sq_used, nsq + k - 1)
                    f(sq[k % 2][:, 0:cw], src[:, 0:cw], ACT.Square, scale=NORM).then_inc(s.sqs, 1)
                    fs.done(f(kh[:, m, c0:c0 + cw], src[:, 0:cw], ACT.Copy, scale=NORM))

            transposed(0)
            act.wait_ge(s.kbias, 1)
            ek = Emptier(act, bank[0:4], s.ek, s.ek_free)
            for r in range(2):
                for t in range(NT):
                    n = r * NT + t
                    if n >= 2:
                        act.wait_ge(s.used, n - 1)
                    for h in range(4):
                        src = ek.take()
                        ek.done(f(ef[n % 2][:valid(t), h, :], src[:valid(t), 0:M], ACT.Exp, bias=kb[:valid(t), t, 4 * r + h:4 * r + h + 1]))
                act.wait_ge(s.used, (r + 1) * NT)
                for h in range(4):
                    f(cT[:VW, 4 * r + h, :], bank[4 + h][:VW, 0:M], ACT.Copy).then_inc(s.ctx_in, 1)
            ct = Emptier(act, bank[0:3], s.ct, s.ct_half)
            for i, (_, cw) in enumerate(MC):
                src = ct.take()
                ct.done(f(heads_of(cx[0], cw, i), src[:cw, :].rearrange("p (q b d) -> p q b d", q=4, b=2), ACT.Copy))
            kbe = Emptier(act, bank[4:7], s.kb_ps, s.kb_in)
            for h in range(H):
                src = kbe.take()
                kbe.done(f(ks[:, h, :], src[:, 0:M], ACT.Copy))
            transposed(KC * len(CH))
            dq = Emptier(act, bank[0:3], s.dq, s.dq_free)
            tq = Emptier(act, bank[3:6], s.tq, s.tq_half)
            for k in range(len(GH) + 2):
                if k < len(GH):
                    t0, nt, h = GH[k]
                    if k >= 2:
                        act.wait_ge(s.tq, 3 * (k - 1))
                    for t in range(nt):
                        act.wait_ge(s.qbias, dq.n + 1)
                        src = dq.take()
                        dq.done(f(ef[k % 2][:, t, :], src[:, 0:M], ACT.Exp, bias=qb[:, t0 + t, h:h + 1]))
                if 1 <= k <= len(GH):
                    t0, nt, h = GH[k - 1]
                    if k >= 3:
                        act.wait_ge(s.used, 2 * NT + k - 2)
                    for i, (_, cw) in enumerate(MC):
                        src = tq.take()
                        tq.done(f(qp[(k - 1) % 2][0][:cw, i, 0:nt * P], src[:cw, 0:nt * P], ACT.Copy))
                if k >= 2:
                    t0, nt, h = GH[k - 2]
                    if h % 2:
                        act.wait_ge(s.used, 2 * NT + k - 1)
                        f(xh[:, h // 2, t0 * P:(t0 + nt) * P], bank[6 + (k // 2 + 1) % 2][:, 0:nt * P], ACT.Copy).then_inc(s.oq_half, 1)

        @block.vector
        def _(dve):
            v = nc.vector
            link = chain(dve, s.cv)
            v.memset(ones[:, :], 1.0)
            link(v.memset(kmax[:, :, :], -BIG))
            one = ones[:, 0:NT * H].rearrange("p (t h w) -> p t h w", t=NT, h=H)
            link(v.tensor_copy(vh[:, :, :, HD:VW], one))
            link(v.tensor_scalar(vl[:, :, :, HD:VW], one, 0.0, None, ALU.mult))
            dve.sem_inc(s.ones_in, 1)
            for i, (c0, cw) in enumerate(CH):
                dve.wait_ge(s.xh, i + 1)
                v.tensor_tensor(xl[:, :, c0:c0 + cw], b.xnT[:, :, c0:c0 + cw], xh[:, :, c0:c0 + cw], ALU.subtract).then_inc(s.xl, 1)
            fs = Emptier(dve, bank[0:4], s.fs_half, s.fs_free)
            for t in range(NT):
                src = fs.take()
                fs.done(v.tensor_tensor(vl[:, t, :, 0:HD], src[:, :].rearrange("p (h d) -> p h d", h=H), vh[:, t, :, 0:HD], ALU.subtract))

            def transposed(i, done):
                for k in range(KC * len(CH)):
                    m, (c0, cw) = k // len(CH), CH[k % len(CH)]
                    src = fs.take()
                    fs.done(v.scalar_tensor_tensor(out=kl[:, m, c0:c0 + cw], in0=src[:, 0:cw], scalar=NORM,
                                                   in1=kh[:, m, c0:c0 + cw], op0=ALU.mult, op1=ALU.subtract))
                dve.wait_ge(s.fs_free, fs.n)
                dve.sem_inc(done, 1)
                dve.wait_ge(s.sq_used, i * KC * len(CH))
                v.tensor_scalar(diag[:, i - 1, :, :], bank[7][:, 0:NT * H].rearrange("p (t h) -> p t h", t=NT), 0.5, None,
                                ALU.mult).then_inc(s.dg_free, 1)
                dve.wait_ge(s.dg_free, i)

            transposed(1, s.kin)
            km = Emptier(dve, bank[0:4], s.km, s.km_free)
            for t in range(NT):
                for h in range(H):
                    src = km.take()
                    km.done(v.tensor_reduce(kmax[:valid(t), t, h:h + 1], src[:valid(t), 0:M], AX.X, ALU.max))
            km.all_done()
            v.tensor_reduce(g1[:, 0:1], kmax[:, :, :], AX.XY, ALU.max).then_inc(s.gm, 1)
            gx = Emptier(dve, bank[7:8], s.gx, s.gx_free)
            src = gx.take()
            gx.done(v.tensor_reduce(gr[:, 0:1], src[0:1, 0:P], AX.X, ALU.max))
            gx.all_done()
            dve.sem_inc(s.gm, 1)
            src = gx.take()
            gx.done(v.tensor_copy(g1[:, 1:2], src[:, 0:1]))
            gx.all_done()
            v.tensor_scalar(kb[:, :, :], diag[:, 0, :, :], -1.0, g1[:, 1:2], ALU.mult, ALU.subtract).then_inc(s.kbias, 1)
            for n in range(2 * NT):
                w = valid(n % NT)
                dve.wait_ge(s.ek_free, 4 * n + 4)
                v.tensor_scalar_add(eh[n % 2][:w, :, :], ef[n % 2][:w, :, :], EPS).then_inc(s.ekh, 1)
                dve.wait_ge(s.ekh, n + 1)
                v.scalar_tensor_tensor(out=el[n % 2][:w, :, :], in0=ef[n % 2][:w, :, :], scalar=EPS,
                                       in1=eh[n % 2][:w, :, :], op0=ALU.add, op1=ALU.subtract).then_inc(s.ekl, 1)
            ct = Emptier(dve, bank[0:3], s.ct_half, s.ct_free)
            for i, (_, cw) in enumerate(MC):
                src = ct.take()
                ct.done(v.tensor_tensor(heads_of(cx[1], cw, i), src[:cw, :].rearrange("p (q b d) -> p q b d", q=4, b=2),
                                        heads_of(cx[0], cw, i), ALU.subtract))
            for x in cx:
                link(v.tensor_scalar(x[:, 1:36:3, :], ones[:, 0:HD].unsqueeze(1).broadcast_to([P, 12, HD]), 0.0, None, ALU.mult))
            transposed(2, s.qin)
            dve.wait_ge(s.kb_in, H)
            tq = Emptier(dve, bank[3:6], s.tq_half, s.tq_free)
            oq = Emptier(dve, bank[6:8], s.oq_half, s.oq_free)
            n, before = 0, 0
            for k in range(len(GH) + 2):
                if 1 <= k <= len(GH):
                    t0, nt, h = GH[k - 1]
                    before += nt
                    dve.wait_ge(s.dq_free, before)
                    for t in range(nt):
                        if before - nt + t:
                            dve.wait_ge(s.scr, before - nt + t)
                        v.scalar_tensor_tensor(out=scratch[:, :], in0=ef[(k - 1) % 2][:, t, :], scalar=EPS, in1=ks[:, h, :],
                                               op0=ALU.add, op1=ALU.mult, accum_out=den[:, t0 + t, h:h + 1]).then_inc(s.scr, 1)
                    dve.wait_ge(s.scr, before)
                    v.reciprocal(rd[:, t0:t0 + nt, h:h + 1], den[:, t0:t0 + nt, h:h + 1]).then_inc(s.rden, 1)
                if k < len(GH):
                    t0, nt, h = GH[k]
                    for t in range(t0, t0 + nt):
                        n += 1
                        dve.wait_ge(s.dq, n)
                        v.tensor_reduce(qmax[:, t, h:h + 1], bank[(n - 1) % 3][:, 0:M], AX.X, ALU.max, negate=True).then_inc(s.kmx, 1)
                        dve.wait_ge(s.kmx, n)
                        v.tensor_tensor(qb[:, t, h:h + 1], qmax[:, t, h:h + 1], diag[:, 1, t, h:h + 1], ALU.subtract).then_inc(s.qbias, 1)
                if 1 <= k <= len(GH):
                    t0, nt, h = GH[k - 1]
                    for i, (_, cw) in enumerate(MC):
                        src = tq.take()
                        tq.done(v.tensor_tensor(qp[(k - 1) % 2][1][:cw, i, 0:nt * P], src[:cw, 0:nt * P],
                                                qp[(k - 1) % 2][0][:cw, i, 0:nt * P], ALU.subtract))
                if k >= 2:
                    t0, nt, h = GH[k - 2]
                    if h % 2:
                        src = oq.take()
                        cols = slice(t0 * P, (t0 + nt) * P)
                        oq.done(v.tensor_tensor(xl[:, h // 2, cols], src[:, 0:nt * P], xh[:, h // 2, cols], ALU.subtract))
            fo = Emptier(dve, bank[0:6], s.fo, s.fo_free)
            for t in range(NT):
                dve.wait_ge(s.biased, t + 1)
                src = fo.take()
                fo.done(v.tensor_tensor(R0[:, t, :], R0[:, t, :], src[:, :], ALU.add))
            fo.all_done()


def expert1(b, top):
    nc, a, cst = b.nc, b.a, b.cst
    ident = cst[:, 0:128]
    with ExitStack() as ctx:
        sb, ps, s = b.tools(ctx, "fa fa_free fd fd_free g_in stats sd scaled xf xfT_in mean sc ex idx we_in be_in gate "
                                "y cv out_s")
        wg, bg = sb("wg", [P, KC, EXP1]), sb("bg", [1, EXP1])
        we, be = sb("we", [P, KC, D]), sb("be", [P, D])
        mean = sb("mean", [P, KC])
        sc = sb("sc", [1, 4, EXP1])
        mx8, ix8 = sb("mx8", [1, 8]), sb("ix8", [1, 8], U32)
        gate = sb("gate", [P, 1])
        ones = sb("ones", [1, P])
        y = sb("y", [P, NT, D])
        norm = Norm(nc, sb, "n")
        bank = [ps(f"bank{i}", [P, D]) for i in range(8)]
        R0, xfT, xf = b.R0, b.xnT, b.vals
        block = ctx.enter_context(nc.Block())

        @block.sync
        def _(sp):
            sp.dma_start(wg[:, :, :], row_chunks(a["L1_ffn_Wg"])).then_inc(s.g_in, 16)
            sp.dma_start(bg[:, :], bcast(a["L1_ffn_bg"], 1)).then_inc(s.g_in, 16)
            sp.wait_ge(s.idx, 1)
            e = sp.value_load(ix8[0:1, 0:1], min_val=0, max_val=EXP1 - 1)
            w = a["L1_ffn_We"].rearrange("e (c p) n -> p e c n", p=P)
            for c in range(KC):
                sp.dma_start(we[:, c, :], w[:, bass.ds(e, 1), c, :]).then_inc(s.we_in, 16)
            sp.dma_start(be[:, :], a["L1_ffn_be"][bass.ds(e, 1), :].broadcast_to([P, D])).then_inc(s.be_in, 16)
            for t in range(NT):
                sp.wait_ge(s.y, t + 1)
                rows = P if t < NT - 1 else LAST
                sp.dma_start(b.out[t * P:t * P + rows, :], y[:rows, t, :]).then_inc(s.out_s, 16)
            sp.wait_ge(s.out_s, 16 * NT)

        @block.tensor
        def _(pe):
            fa = Filler(pe, bank[:4], s.fa, s.fa_free)
            fd = Filler(pe, bank[4:], s.fd, s.fd_free)
            for t0, nt in GRP:
                pe.wait_ge(s.xf, t0 + nt)
                for c in range(KC):
                    transposes(nc, fa, xf, ident, t0, nt, c)
            pe.wait_ge(s.mean, 1)
            pe.wait_ge(s.g_in, 32)
            dst = fd.take()
            fd.done(product(nc, dst[0:1, 0:EXP1], [mean[:, c:c + 1] for c in range(KC)], chunks(wg, 0, EXP1)))
            pe.wait_ge(s.gate, 1)
            dst = fd.take()
            fd.done(nc.tensor.matmul(dst[:, 0:1], ones[:, :], mx8[0:1, 0:1], start=True, stop=True))
            pe.wait_ge(s.we_in, 16 * KC)
            for t in range(NT):
                dst = fd.take()
                fd.done(product(nc, dst[:, :], tile(xfT, t), chunks(we)))

        @block.scalar
        def _(act):
            full = Emptier(act, bank[:4], s.fa, s.fa_free)
            norm.root(act, s.stats, 1, s.sd)
            act.wait_ge(s.scaled, 1)
            for t in range(NT):
                norm.apply(xf, R0, t).then_inc(s.xf, 1)
            for t0, nt in GRP:
                for c in range(KC):
                    src = full.take()
                    full.done(nc.scalar.activation(xfT[:, c, t0 * P:(t0 + nt) * P], src[:, 0:nt * P], ACT.Copy))
            full.all_done()
            act.sem_inc(s.xfT_in, 1)
            act.wait_ge(s.sc, 1)
            nc.scalar.activation(sc[:, 1, :], sc[:, 0, :], ACT.Exp).then_inc(s.ex, 1)

        @block.vector
        def _(dve):
            v = nc.vector
            link = chain(dve, s.cv)
            full = Emptier(dve, bank[4:], s.fd, s.fd_free)
            v.memset(ones[:, :], 1.0)
            norm.stats(link, R0, s.stats)
            norm.scales(dve, link, s.sd, 1, s.scaled)
            dve.wait_ge(s.xfT_in, 1)
            link(v.tensor_reduce(mean[:, :], xfT[:, :, 0:N], AX.X, ALU.add))
            v.tensor_scalar(mean[:, :], mean[:, :], 1.0 / N, None, ALU.mult).then_inc(s.mean, 1)
            src = full.take()
            full.done(v.tensor_tensor(sc[:, 0, :], src[0:1, 0:EXP1], bg[:, :], ALU.add))
            full.all_done()
            link(v.tensor_reduce(sc[:, 2, 0:1], sc[:, 0, :], AX.X, ALU.max, negate=True))
            v.tensor_scalar(sc[:, 0, :], sc[:, 0, :], sc[:, 2, 0:1], None, ALU.add).then_inc(s.sc, 1)
            dve.wait_ge(s.ex, 1)
            link(v.tensor_reduce(sc[:, 2, 1:2], sc[:, 1, :], AX.X, ALU.add))
            link(v.reciprocal(sc[:, 2, 2:3], sc[:, 2, 1:2]))
            link(v.tensor_scalar(sc[:, 3, :], sc[:, 1, :], sc[:, 2, 2:3], None, ALU.mult))
            link(v.max(mx8[:, :], sc[:, 3, :]))
            v.max_index(ix8[:, :], mx8[:, :], sc[:, 3, :]).then_inc(s.idx, 1)
            dve.sem_inc(s.gate, 1)
            src = full.take()
            full.done(v.tensor_copy(gate[:, :], src[:, 0:1]))
            full.all_done()
            dve.wait_ge(s.be_in, 16)
            for t in range(NT):
                src = full.take()
                full.done(v.tensor_tensor(y[:, t, :], src[:, :], be[:, :], ALU.add))
                full.all_done()
                v.scalar_tensor_tensor(out=y[:, t, :], in0=y[:, t, :], scalar=gate[:, 0:1], in1=R0[:, t, :],
                                       op0=ALU.mult, op1=ALU.add).then_inc(s.y, 1)


_INS = ["x", "src", "dst", "edge_attr_8"] + ["L0_gnn_" + n for n in ("ln_g", "ln_b", "Wq", "bq", "Wk", "bk", "Wv", "bv", "W1", "b1", "W2", "b2")] \
    + ["L0_mix_WqkvT", "L0_mix_WoutT", "L0_mix_bout"] + ["L0_ffn_" + n for n in ("Wg", "bg", "W1", "b1", "W2", "b2")] \
    + ["L1_gnn_" + n for n in ("W1lT", "b1l", "W1rT", "W2lT", "b2l", "W2rT", "ln1_w", "ln1_b", "ln2_w", "ln2_b")] \
    + ["L1_mix_" + n for n in ("Wq", "Wk", "Wv", "Wo", "bo", "projT")] + ["L1_ffn_" + n for n in ("Wg", "bg", "We", "be")]


def lay_out(inputs):
    arrays = {}
    for name in _INS:
        if name.endswith("T") and name not in inputs:
            arrays[name] = np.ascontiguousarray(np.asarray(inputs[name[:-1]]).T)
        else:
            arrays[name] = np.ascontiguousarray(inputs[name])
    arrays["c_cols"] = np.ascontiguousarray(np.concatenate(
        [np.asarray(inputs[n]).reshape(-1, P) for n in ("L0_gnn_ln_g", "L0_gnn_ln_b", "L0_gnn_b1", "L0_ffn_b1")]).T)
    arrays["c_cst"], arrays["c_iota"] = constants()
    return arrays


def build_program(nc, a, out, stages=99):
    with ExitStack() as top:
        b = Build(nc, a, out)
        for stage in STAGES[:stages]:
            stage(b, top)
    return b


STAGES = [prepare, linear_attention, edge_scores, edge_softmax, edge_sums, attention_out, experts0, sage, performer, expert1]


def kernel(**inputs):
    import concourse.bacc as bacc
    from concourse.bass_utils import run_bass_kernel_spmd

    nc = bacc.Bacc("TRN2", target_bir_lowering=False, num_devices=1)
    arrays = lay_out(inputs)
    a = {n: nc.dram_tensor("in_" + n, v.shape, mybir.dt.from_np(v.dtype), kind="ExternalInput").ap() for n, v in arrays.items()}
    out = nc.dram_tensor("out_rows", (N, D), F32, kind="ExternalOutput").ap()
    build_program(nc, a, out)
    r = run_bass_kernel_spmd(nc, [{"in_" + n: v for n, v in arrays.items()}], core_ids=[0])
    return r.results[0]["out_rows"]
```
